# Optimizing a Trainium2 kernel written in Bass

```python
import numpy as np
import jax
import jax.numpy as jnp

def _softmax(x, axis=-1):
    return jax.nn.softmax(x, axis=axis)

def _gelu(x):
    return jax.nn.gelu(x, approximate=True)

def _silu(x):
    return jax.nn.silu(x)

def _sigmoid(x):
    return jax.nn.sigmoid(x)

def _layernorm(x, axis=-1, eps=1e-05):
    m = jnp.mean(x, axis=axis, keepdims=True)
    v = jnp.var(x, axis=axis, keepdims=True)
    return (x - m) / jnp.sqrt(v + eps)

def _scatter_add(tgt, idx, src, axis=0):
    return tgt.at[idx].add(src)

def _segment_sum(src, seg, n):
    return jax.ops.segment_sum(src, seg, n)
kernel_name = 'mk_perceiver_d2_seqx_r2_9aad09'

def setup_inputs(seed: int=0):
    np.random.seed(seed)
    _w = jnp.asarray

    def _rec_inputs():
        import jax
        import jax.numpy as jnp
        _rk = jax.random.key(seed)
        x = -0.0003929 + 0.9999 * jax.random.normal(jax.random.fold_in(_rk, 1), (16, 64, 512), jnp.float32)
        _lenS = 64 - jax.random.randint(jax.random.fold_in(_rk, 7), (16,), 0, max(1, 64 // 4) + 1, jnp.int32)
        _lenS2 = 1601 - jax.random.randint(jax.random.fold_in(_rk, 8), (16,), 0, max(1, 1601 // 4) + 1, jnp.int32)
        _ctx_512P = jax.random.normal(jax.random.fold_in(_rk, 11), (16, 16, 256), jnp.float32)
        _ctx_512c = jax.random.dirichlet(jax.random.fold_in(_rk, 511), 0.3 * jnp.ones((16,), jnp.float32), (16, 1601))
        _ctx_512t = jnp.einsum('bsk,bkd->bsd', _ctx_512c, _ctx_512P)
        _ctx_512t = _ctx_512t * jax.lax.rsqrt(jnp.mean(jnp.square(_ctx_512t)) + 1e-12) * 0.953939
        ctx_512 = -1.39393e-06 + 0.999914 * (_ctx_512t + 0.3 * jax.random.normal(jax.random.fold_in(_rk, 611), (16, 1601, 256), jnp.float32))
        return (x, ctx_512)
    x, ctx_512 = _rec_inputs()

    def _L0_xattn_setup():
        import jax, jax.numpy as jnp
        import numpy as np
        HEADS = 16
        D_MODEL = 512
        IMG_MODEL = 256
        D_K = D_MODEL // HEADS
        key = jax.random.key(seed)
        ks = jax.random.split(key, 12)
        B, LQ, LKV = (8, 1024, 512)
        s_dm = 1.0 / np.sqrt(D_MODEL)
        s_im = 1.0 / np.sqrt(IMG_MODEL)
        return {'q': jax.random.normal(ks[0], (B, LQ, D_MODEL), jnp.float32), 'k': jax.random.normal(ks[1], (B, LKV, IMG_MODEL), jnp.float32), 'v': jax.random.normal(ks[2], (B, LKV, IMG_MODEL), jnp.float32), 'Wq': jax.random.normal(ks[3], (D_MODEL, D_MODEL), jnp.float32) * s_dm, 'bq': jnp.zeros((D_MODEL,), jnp.float32), 'Wk': jax.random.normal(ks[4], (IMG_MODEL, D_MODEL), jnp.float32) * s_im, 'bk': jnp.zeros((D_MODEL,), jnp.float32), 'Wv': jax.random.normal(ks[5], (IMG_MODEL, D_MODEL), jnp.float32) * s_im, 'bv': jnp.zeros((D_MODEL,), jnp.float32), 'Wo': jax.random.normal(ks[6], (D_MODEL, D_MODEL), jnp.float32) * s_dm, 'bo': jnp.zeros((D_MODEL,), jnp.float32)}
    _L0_xattn_all = _L0_xattn_setup()
    _L0_xattn_in = {k: v for k, v in _L0_xattn_all.items() if k in ('Wq', 'bq', 'Wk', 'bk', 'Wv', 'bv', 'Wo', 'bo')}
    del _L0_xattn_all

    def _L0_attn_setup():
        import jax, jax.numpy as jnp
        import numpy as np
        H_HEADS = 16
        STATE_N = 64

        def _mamba2_forward(inp, W_logA, b_logA, W_XBC, b_XBC, W_gate, b_gate, W_out, b_out):
            B, T, D = inp.shape
            H, N = (H_HEADS, STATE_N)
            ch = D // H
            x = inp.reshape(B, T, H, ch)
            logA = jnp.einsum('hoc,bthc->btho', W_logA, x)[..., 0] + b_logA[:, 0]
            XBC = jax.nn.silu(jnp.einsum('hoc,bthc->btho', W_XBC, x) + b_XBC)
            X = XBC[..., :ch]
            Bm = XBC[..., ch:ch + N]
            Cm = XBC[..., ch + N:]
            cum = jnp.cumsum(jnp.swapaxes(logA, 1, 2), axis=-1)
            diff = cum[..., :, None] - cum[..., None, :]
            causal = jnp.tril(jnp.ones((T, T), dtype=bool))
            A_ss = jnp.where(causal, jnp.exp(jnp.where(causal, diff, 0.0)), 0.0)
            G = jnp.einsum('bihn,bjhn->bhij', Cm, Bm)
            Y = jnp.einsum('bhij,bjhc->bihc', A_ss * G, X)
            gate = jnp.einsum('hoc,bthc->btho', W_gate, x) + b_gate
            Yg = (gate * Y).reshape(B, T, D)
            return Yg @ W_out.T + b_out
        key = jax.random.key(seed)
        ks = jax.random.split(key, 9)
        B, T, D = (2, 512, 512)
        H, ch, N = (H_HEADS, D // H_HEADS, STATE_N)
        inp = jax.random.normal(ks[0], (B, T, D), dtype=jnp.float32)
        W_logA = jax.random.normal(ks[1], (H, 1, ch), dtype=jnp.float32) * 0.01
        b_logA = jnp.full((H, 1), -0.05, dtype=jnp.float32)
        W_XBC = jax.random.normal(ks[3], (H, ch + 2 * N, ch), dtype=jnp.float32) * (1.0 / np.sqrt(ch))
        b_XBC = jax.random.normal(ks[4], (H, ch + 2 * N), dtype=jnp.float32) * 0.02
        W_gate = jax.random.normal(ks[5], (H, ch, ch), dtype=jnp.float32) * (1.0 / np.sqrt(ch))
        b_gate = jax.random.normal(ks[6], (H, ch), dtype=jnp.float32) * 0.02
        W_out = jax.random.normal(ks[7], (D, D), dtype=jnp.float32) * (1.0 / np.sqrt(D))
        b_out = jax.random.normal(ks[8], (D,), dtype=jnp.float32) * 0.02
        return {'inp': inp, 'W_logA': W_logA, 'b_logA': b_logA, 'W_XBC': W_XBC, 'b_XBC': b_XBC, 'W_gate': W_gate, 'b_gate': b_gate, 'W_out': W_out, 'b_out': b_out}
    _L0_attn_all = _L0_attn_setup()
    _L0_attn_in = {k: v for k, v in _L0_attn_all.items() if k in ('W_logA', 'b_logA', 'W_XBC', 'b_XBC', 'W_gate', 'b_gate', 'W_out', 'b_out')}
    del _L0_attn_all

    def _L0_ffn_setup():
        import jax, jax.numpy as jnp
        import numpy as np
        IN_F, OUT_F, BLOCK, NBLK = (512, 2048, 128, 16)
        TOPK = NBLK // 4
        key = jax.random.key(seed)
        ks = jax.random.split(key, 7)
        s = 1.0 / np.sqrt(IN_F)
        s2 = 1.0 / np.sqrt(OUT_F)
        return {'x': jax.random.normal(ks[0], (4, 2048, IN_F), jnp.float32), 'router_w': jax.random.uniform(ks[1], (NBLK, IN_F), jnp.float32, -s, s), 'router_b': jax.random.uniform(ks[2], (NBLK,), jnp.float32, -s, s), 'w1': jax.random.uniform(ks[3], (OUT_F, IN_F), jnp.float32, -s, s), 'b1': jax.random.uniform(ks[4], (OUT_F,), jnp.float32, -s, s), 'w2': jax.random.uniform(ks[5], (IN_F, OUT_F), jnp.float32, -s2, s2), 'b2': jax.random.uniform(ks[6], (IN_F,), jnp.float32, -s2, s2)}
    _L0_ffn_all = _L0_ffn_setup()
    _L0_ffn_in = {k: v for k, v in _L0_ffn_all.items() if k in ('router_w', 'router_b', 'w1', 'b1', 'w2', 'b2')}
    del _L0_ffn_all

    def _L1_xattn_setup():
        import jax, jax.numpy as jnp
        import numpy as np
        B, LQ, LK = (8, 1024, 1024)
        QD, KD, VD = (512, 256, 256)
        key = jax.random.key(seed)
        ks = jax.random.split(key, 9)
        s = 0.02
        return {'query': jax.random.normal(ks[0], (B, LQ, QD), jnp.float32), 'key': jax.random.normal(ks[1], (B, LK, KD), jnp.float32), 'value': jax.random.normal(ks[2], (B, LK, VD), jnp.float32), 'Wq': jax.random.normal(ks[3], (QD, QD), jnp.float32) * s, 'bq': jnp.zeros((QD,), jnp.float32), 'Wk': jax.random.normal(ks[4], (KD, QD), jnp.float32) * s, 'bk': jnp.zeros((QD,), jnp.float32), 'Wv': jax.random.normal(ks[5], (VD, QD), jnp.float32) * s, 'bv': jnp.zeros((QD,), jnp.float32)}
    _L1_xattn_all = _L1_xattn_setup()
    _L1_xattn_in = {k: v for k, v in _L1_xattn_all.items() if k in ('Wq', 'bq', 'Wk', 'bk', 'Wv', 'bv')}
    del _L1_xattn_all

    def _L1_attn_setup():
        import jax, jax.numpy as jnp
        import numpy as np
        import math
        D_MODEL = 512
        D_QUERY = 64
        key = jax.random.key(seed)
        k1, k2, k3, k4 = jax.random.split(key, 4)
        X = jax.random.normal(k1, (4, 2048, D_MODEL), dtype=jnp.float32)
        Wq = jax.random.normal(k2, (D_MODEL, D_QUERY), dtype=jnp.float32) * (1.0 / math.sqrt(D_MODEL))
        Wk = jax.random.normal(k3, (D_MODEL, D_QUERY), dtype=jnp.float32) * (1.0 / math.sqrt(D_MODEL))
        Wv = jax.random.normal(k4, (D_MODEL, D_MODEL), dtype=jnp.float32) * (1.0 / math.sqrt(D_MODEL))
        return {'X': X, 'Wq': Wq, 'Wk': Wk, 'Wv': Wv}
    _L1_attn_all = _L1_attn_setup()
    _L1_attn_in = {k: v for k, v in _L1_attn_all.items() if k in ('Wq', 'Wk', 'Wv')}
    del _L1_attn_all

    def _L1_ffn_setup():
        import jax, jax.numpy as jnp
        import numpy as np
        BLOCK = 32
        W_BITS = 4
        ACT_BITS = 16

        def act_qdq(x):
            qmax = 2.0 ** (ACT_BITS - 1) - 1.0
            scale = jnp.maximum(jnp.max(jnp.abs(x)) / qmax, 1e-12)
            return jnp.clip(jnp.round(x / scale), -qmax - 1.0, qmax) * scale

        def fixed_qdq_u16(x):
            scale = 1.0 / 65536.0
            return jnp.clip(jnp.round(x / scale), 0.0, 65535.0) * scale

        def lpbq_dequant(w):
            O, I = w.shape
            qmax = 2.0 ** (W_BITS - 1) - 1.0
            wb = w.reshape(O, I // BLOCK, BLOCK)
            s = jnp.maximum(jnp.max(jnp.abs(wb), axis=-1, keepdims=True) / qmax, 1e-12)
            wq = jnp.clip(jnp.round(wb / s), -qmax - 1.0, qmax) * s
            return wq.reshape(O, I)
        key = jax.random.key(seed)
        k1, k2, k3, k4 = jax.random.split(key, 4)
        B, S, H, I = (2, 2048, 512, 1536)
        x = jax.random.normal(k1, (B, S, H), jnp.float32)
        w_gate = jax.random.normal(k2, (I, H), jnp.float32) * 0.02
        w_up = jax.random.normal(k3, (I, H), jnp.float32) * 0.02
        w_down = jax.random.normal(k4, (H, I), jnp.float32) * 0.02
        return {'x': x, 'w_gate': w_gate, 'w_up': w_up, 'w_down': w_down}
    _L1_ffn_all = _L1_ffn_setup()
    _L1_ffn_in = {k: v for k, v in _L1_ffn_all.items() if k in ('w_gate', 'w_up', 'w_down')}
    del _L1_ffn_all
    return {'x': x, 'ctx_512': ctx_512, 'L0_xattn_Wq': _L0_xattn_in['Wq'], 'L0_xattn_bq': _L0_xattn_in['bq'], 'L0_xattn_Wk': _L0_xattn_in['Wk'], 'L0_xattn_bk': _L0_xattn_in['bk'], 'L0_xattn_Wv': _L0_xattn_in['Wv'], 'L0_xattn_bv': _L0_xattn_in['bv'], 'L0_xattn_Wo': _L0_xattn_in['Wo'], 'L0_xattn_bo': _L0_xattn_in['bo'], 'L0_attn_W_logA': _L0_attn_in['W_logA'], 'L0_attn_b_logA': _L0_attn_in['b_logA'], 'L0_attn_W_XBC': _L0_attn_in['W_XBC'], 'L0_attn_b_XBC': _L0_attn_in['b_XBC'], 'L0_attn_W_gate': _L0_attn_in['W_gate'], 'L0_attn_b_gate': _L0_attn_in['b_gate'], 'L0_attn_W_out': _L0_attn_in['W_out'], 'L0_attn_b_out': _L0_attn_in['b_out'], 'L0_ffn_router_w': _L0_ffn_in['router_w'], 'L0_ffn_router_b': _L0_ffn_in['router_b'], 'L0_ffn_w1': _L0_ffn_in['w1'], 'L0_ffn_b1': _L0_ffn_in['b1'], 'L0_ffn_w2': _L0_ffn_in['w2'], 'L0_ffn_b2': _L0_ffn_in['b2'], 'L1_xattn_Wq': _L1_xattn_in['Wq'], 'L1_xattn_bq': _L1_xattn_in['bq'], 'L1_xattn_Wk': _L1_xattn_in['Wk'], 'L1_xattn_bk': _L1_xattn_in['bk'], 'L1_xattn_Wv': _L1_xattn_in['Wv'], 'L1_xattn_bv': _L1_xattn_in['bv'], 'L1_attn_Wq': _L1_attn_in['Wq'], 'L1_attn_Wk': _L1_attn_in['Wk'], 'L1_attn_Wv': _L1_attn_in['Wv'], 'L1_ffn_w_gate': _L1_ffn_in['w_gate'], 'L1_ffn_w_up': _L1_ffn_in['w_up'], 'L1_ffn_w_down': _L1_ffn_in['w_down']}

def reference(x, ctx_512, L0_xattn_Wq, L0_xattn_bq, L0_xattn_Wk, L0_xattn_bk, L0_xattn_Wv, L0_xattn_bv, L0_xattn_Wo, L0_xattn_bo, L0_attn_W_logA, L0_attn_b_logA, L0_attn_W_XBC, L0_attn_b_XBC, L0_attn_W_gate, L0_attn_b_gate, L0_attn_W_out, L0_attn_b_out, L0_ffn_router_w, L0_ffn_router_b, L0_ffn_w1, L0_ffn_b1, L0_ffn_w2, L0_ffn_b2, L1_xattn_Wq, L1_xattn_bq, L1_xattn_Wk, L1_xattn_bk, L1_xattn_Wv, L1_xattn_bv, L1_attn_Wq, L1_attn_Wk, L1_attn_Wv, L1_ffn_w_gate, L1_ffn_w_up, L1_ffn_w_down):
    import jax
    import jax.numpy as jnp

    def _L0_xattn_ref(q, k, v, Wq, bq, Wk, bk, Wv, bv, Wo, bo):
        import jax, jax.numpy as jnp
        import numpy as np
        HEADS = 16
        D_MODEL = 512
        IMG_MODEL = 256
        D_K = D_MODEL // HEADS
        B, LQ, _ = q.shape
        LKV = k.shape[1]
        qh = (q @ Wq + bq).reshape(B, LQ, HEADS, D_K).transpose(0, 2, 1, 3)
        kh = (k @ Wk + bk).reshape(B, LKV, HEADS, D_K).transpose(0, 2, 1, 3)
        vh = (v @ Wv + bv).reshape(B, LKV, HEADS, D_K).transpose(0, 2, 1, 3)
        scale = 1.0 / np.sqrt(D_K)
        scores = jnp.einsum('bhqd,bhkd->bhqk', qh, kh) * scale
        attn = jax.nn.softmax(scores, axis=-1)
        out = jnp.einsum('bhqk,bhkd->bhqd', attn, vh)
        concat = out.transpose(0, 2, 1, 3).reshape(B, LQ, D_MODEL)
        return concat @ Wo + bo

    def _L0_attn_ref(inp, W_logA, b_logA, W_XBC, b_XBC, W_gate, b_gate, W_out, b_out):
        import jax, jax.numpy as jnp
        import numpy as np
        H_HEADS = 16
        STATE_N = 64

        def _mamba2_forward(inp, W_logA, b_logA, W_XBC, b_XBC, W_gate, b_gate, W_out, b_out):
            B, T, D = inp.shape
            H, N = (H_HEADS, STATE_N)
            ch = D // H
            x = inp.reshape(B, T, H, ch)
            logA = jnp.einsum('hoc,bthc->btho', W_logA, x)[..., 0] + b_logA[:, 0]
            XBC = jax.nn.silu(jnp.einsum('hoc,bthc->btho', W_XBC, x) + b_XBC)
            X = XBC[..., :ch]
            Bm = XBC[..., ch:ch + N]
            Cm = XBC[..., ch + N:]
            cum = jnp.cumsum(jnp.swapaxes(logA, 1, 2), axis=-1)
            diff = cum[..., :, None] - cum[..., None, :]
            causal = jnp.tril(jnp.ones((T, T), dtype=bool))
            A_ss = jnp.where(causal, jnp.exp(jnp.where(causal, diff, 0.0)), 0.0)
            G = jnp.einsum('bihn,bjhn->bhij', Cm, Bm)
            Y = jnp.einsum('bhij,bjhc->bihc', A_ss * G, X)
            gate = jnp.einsum('hoc,bthc->btho', W_gate, x) + b_gate
            Yg = (gate * Y).reshape(B, T, D)
            return Yg @ W_out.T + b_out
        return _mamba2_forward(inp, W_logA, b_logA, W_XBC, b_XBC, W_gate, b_gate, W_out, b_out)

    def _L0_ffn_ref(x, router_w, router_b, w1, b1, w2, b2):
        import jax, jax.numpy as jnp
        import numpy as np
        IN_F, OUT_F, BLOCK, NBLK = (512, 2048, 128, 16)
        TOPK = NBLK // 4
        x_shape = x.shape
        xf = x.reshape(-1, IN_F)
        n = xf.shape[0]
        prob = jax.nn.softmax(xf @ router_w.T + router_b, axis=-1)
        _, idx = jax.lax.top_k(prob, TOPK)
        mask = jnp.zeros((n, NBLK), bool).at[jnp.arange(n)[:, None], idx].set(True)
        w1b = w1.reshape(NBLK, BLOCK, IN_F)
        b1b = b1.reshape(NBLK, BLOCK)
        h = jnp.einsum('nd,ibd->nib', xf, w1b) + b1b
        h = jnp.where(mask[:, :, None], h, jnp.zeros((), h.dtype))
        h = jax.nn.relu(h)
        w2b = w2.reshape(IN_F, NBLK, BLOCK)
        y = jnp.einsum('nib,dib->nd', jnp.where(mask[:, :, None], h, 0.0), w2b) + b2
        return y.reshape(x_shape)

    def _L1_xattn_ref(query, key, value, Wq, bq, Wk, bk, Wv, bv):
        import jax, jax.numpy as jnp
        import numpy as np
        B, LQ, LK = (8, 1024, 1024)
        QD, KD, VD = (512, 256, 256)
        q = jnp.einsum('bld,de->ble', query, Wq) + bq
        k = jnp.einsum('bld,de->ble', key, Wk) + bk
        v = jnp.einsum('bld,de->ble', value, Wv) + bv
        scores = jnp.einsum('bqe,bke->bqk', q, k)
        attn = jax.nn.softmax(scores, axis=-1)
        out = jnp.einsum('bqk,bke->bqe', attn, v)
        return out

    def _L1_attn_ref(X, Wq, Wk, Wv):
        import jax, jax.numpy as jnp
        import numpy as np
        import math
        D_MODEL = 512
        D_QUERY = 64
        B, T, _ = X.shape
        Q = X @ Wq
        K = X @ Wk
        V = X @ Wv
        scores = jnp.einsum('btd,bsd->bts', Q, K)
        causal = jnp.tril(jnp.ones((T, T), dtype=bool))
        scores = jnp.where(causal[None, :, :], scores, -jnp.inf)
        attn = jax.nn.softmax(scores / math.sqrt(D_QUERY), axis=2)
        return attn @ V

    def _L1_ffn_ref(x, w_gate, w_up, w_down):
        import jax, jax.numpy as jnp
        import numpy as np
        BLOCK = 32
        W_BITS = 4
        ACT_BITS = 16

        def act_qdq(x):
            qmax = 2.0 ** (ACT_BITS - 1) - 1.0
            scale = jnp.maximum(jnp.max(jnp.abs(x)) / qmax, 1e-12)
            return jnp.clip(jnp.round(x / scale), -qmax - 1.0, qmax) * scale

        def fixed_qdq_u16(x):
            scale = 1.0 / 65536.0
            return jnp.clip(jnp.round(x / scale), 0.0, 65535.0) * scale

        def lpbq_dequant(w):
            O, I = w.shape
            qmax = 2.0 ** (W_BITS - 1) - 1.0
            wb = w.reshape(O, I // BLOCK, BLOCK)
            s = jnp.maximum(jnp.max(jnp.abs(wb), axis=-1, keepdims=True) / qmax, 1e-12)
            wq = jnp.clip(jnp.round(wb / s), -qmax - 1.0, qmax) * s
            return wq.reshape(O, I)
        x = act_qdq(x)
        up = act_qdq(x @ lpbq_dequant(w_up).T)
        gate = act_qdq(x @ lpbq_dequant(w_gate).T)
        sig = fixed_qdq_u16(jax.nn.sigmoid(gate))
        gate = act_qdq(gate * sig)
        o = act_qdq(gate * up)
        return o @ lpbq_dequant(w_down).T
    x = x + _L0_xattn_ref(_layernorm(x, axis=-1), ctx_512, ctx_512, L0_xattn_Wq, L0_xattn_bq, L0_xattn_Wk, L0_xattn_bk, L0_xattn_Wv, L0_xattn_bv, L0_xattn_Wo, L0_xattn_bo)
    x = x + _L0_attn_ref(_layernorm(x, axis=-1), L0_attn_W_logA, L0_attn_b_logA, L0_attn_W_XBC, L0_attn_b_XBC, L0_attn_W_gate, L0_attn_b_gate, L0_attn_W_out, L0_attn_b_out)
    x = x + _L0_ffn_ref(_layernorm(x, axis=-1), L0_ffn_router_w, L0_ffn_router_b, L0_ffn_w1, L0_ffn_b1, L0_ffn_w2, L0_ffn_b2)
    x = x + _L1_xattn_ref(_layernorm(x, axis=-1), ctx_512, ctx_512, L1_xattn_Wq, L1_xattn_bq, L1_xattn_Wk, L1_xattn_bk, L1_xattn_Wv, L1_xattn_bv)
    x = x + _L1_attn_ref(_layernorm(x, axis=-1), L1_attn_Wq, L1_attn_Wk, L1_attn_Wv)
    x = x + _L1_ffn_ref(_layernorm(x, axis=-1), L1_ffn_w_gate, L1_ffn_w_up, L1_ffn_w_down)
    return x

_drawn_inputs = setup_inputs


def setup_inputs(seed=0):
    import zlib

    import numpy as np

    out = dict(_drawn_inputs(seed))
    spreads = {'L0_xattn_bq': (0.0, 0.1),
     'L0_xattn_bk': (0.0, 2.0),
     'L0_xattn_bv': (0.0, 0.1),
     'L0_xattn_bo': (0.0, 0.1),
     'L0_attn_b_logA': (-0.05000000074505806, 0.2),
     'L1_xattn_bq': (0.0, 0.8),
     'L1_xattn_bk': (0.0, 2.0),
     'L1_xattn_bv': (0.0, 0.8)}
    factors = {'L0_attn_b_gate': 3.038,
     'L0_attn_b_out': 8.0,
     'L0_ffn_router_w': 8.0,
     'L0_ffn_router_b': 8.0,
     'L0_ffn_w1': 8.0,
     'L0_ffn_b1': 8.0,
     'L0_ffn_w2': 8.0,
     'L0_ffn_b2': 21.468,
     'L1_xattn_Wq': 5.869,
     'L1_xattn_Wk': 5.626,
     'L1_xattn_Wv': 4.791,
     'L1_attn_Wq': 6.951,
     'L1_attn_Wk': 7.041,
     'L1_attn_Wv': 2.946,
     'L1_ffn_w_gate': 8.0,
     'L1_ffn_w_up': 8.0,
     'L1_ffn_w_down': 8.0}
    for name, (base, spread) in spreads.items():
        noise = np.random.default_rng([zlib.crc32(name.encode()), seed]).standard_normal(out[name].shape)
        drawn = base * np.exp(spread * noise) if base else spread * noise
        out[name] = jnp.asarray(drawn.astype(out[name].dtype))
    for name, factor in factors.items():
        out[name] = (out[name] * factor).astype(out[name].dtype)
    return out
```

```python
from contextlib import ExitStack

import numpy as np
import concourse.bass as bass
from concourse import mybir

F32 = mybir.dt.float32
BF16 = mybir.dt.bfloat16
ALU = mybir.AluOpType
ACT = mybir.ActivationFunctionType
AX = mybir.AxisListType.X

P = 128
B, L, D = 16, 64, 512
TOK = B * L
NT = TOK // P
KD = D // P
NK, CD = 1601, 256
KC = CD // P
H, DH = 16, D // 16
NPAIR = H // 2
KTILES = [(n, min(P, NK - n)) for n in range(0, NK, P)]
CHUNKS = [(n, min(512, NK - n)) for n in range(0, NK, 512)]
NTG = 4
TGROUPS = [KTILES[4 * j:4 * j + 4] for j in range(NTG)]
EPS = 1e-5
ROUND = 12582912.0
FAR = -3.0e38
QMAX = 32767.0


class Kit:

    def __init__(self, nc, d, out):
        self.nc, self.d, self.out = nc, d, out
        self.used = []
        self.scratch = {n: nc.dram_tensor(f"parts_{n}", (P, 2, WCOLS), BF16, kind="Internal").ap()
                        for n in Dequant.MATRICES}

    def sb(self, ctx, name, shape, dt=F32):
        return ctx.enter_context(self.nc.sbuf_tensor(name, shape, dt))

    def ps(self, ctx, name, shape, dt=F32):
        return ctx.enter_context(self.nc.psum_tensor(name, shape, dt))

    def sem(self, ctx, name):
        self.used.append(self.nc.alloc_semaphore(name=name))
        return self.used[-1]

    def clear_semaphores(self):
        self.nc.clear_and_free_semaphores(self.used)
        self.used = []
        self.nc.all_engine_barrier()



class Norm:

    def __init__(self, k, ctx, name, x, ident, banks, xT, loaded=None, xhat=None, split=None):
        self.split = split
        self.x, self.ident, self.banks, self.xT = x, ident, banks, xT
        self.loaded = loaded
        self.stats = k.sb(ctx, name + "_stats", [P, NT, 6])
        self.meanvar = k.sb(ctx, name + "_meanvar", [P, NT, 2])
        self.rstd = k.sb(ctx, name + "_rstd", [P, NT, 1])
        self.xhat = k.sb(ctx, name + "_xhat", [P, NT, D]) if xhat is None else xhat
        self.s_stats = k.sem(ctx, name + "_stats_done")
        self.small = k.sb(ctx, name + "_small", [P, 4, NT])
        self.s_var = k.sem(ctx, name + "_var_done")
        self.s_root = k.sem(ctx, name + "_root_done")
        self.s_hat = k.sem(ctx, name + "_xhat_done")
        self.s_low = k.sem(ctx, name + "_low_done")
        self.s_turned = k.sem(ctx, name + "_turned")
        self.s_xT = k.sem(ctx, name + "_xT_done")

    def on_vector(self, dve):
        for t in range(NT):
            if self.loaded:
                dve.wait_ge(*self.loaded(t))
            dve.bn_stats(self.stats[:, t, :], self.x[:, t, :]).then_inc(self.s_stats, 1)
        dve.wait_ge(self.s_stats, NT)
        for t in range(NT):
            dve.bn_aggr(self.meanvar[:, t, :], self.stats[:, t, :]).then_inc(self.s_stats, 1)
        dve.wait_ge(self.s_stats, 2 * NT)
        ve, root, r, u = (self.small[:, n, :] for n in range(4))
        dve.tensor_scalar(ve, self.meanvar[:, :, 1], EPS, None, ALU.add).then_inc(self.s_var, 1)
        dve.wait_ge(self.s_root, 1)
        dve.reciprocal(r, root).then_inc(self.s_var, 1)
        dve.wait_ge(self.s_var, 2)
        dve.tensor_tensor(u, r, r, ALU.mult).then_inc(self.s_var, 1)
        dve.wait_ge(self.s_var, 3)
        dve.tensor_tensor(u, u, ve, ALU.mult).then_inc(self.s_var, 1)
        dve.wait_ge(self.s_var, 4)
        dve.tensor_scalar(u, u, -0.5, 1.5, ALU.mult, ALU.add).then_inc(self.s_var, 1)
        dve.wait_ge(self.s_var, 5)
        dve.tensor_tensor(self.rstd[:, :, 0], r, u, ALU.mult).then_inc(self.s_var, 1)
        dve.wait_ge(self.s_var, 6)
        for t in range(NT):
            dve.tensor_scalar(self.xhat[:, t, :], self.x[:, t, :], self.meanvar[:, t, 0:1],
                              self.rstd[:, t, :], ALU.subtract, ALU.mult).then_inc(self.s_hat, 1)

    def on_tensor(self, pe):
        for t in range(NT):
            pe.wait_ge(self.s_hat, t + 1)
            if t >= 2:
                pe.wait_ge(self.s_xT, t - 1)
            for j in range(KD):
                last = pe.transpose(self.banks[t % 2][:, j * P:(j + 1) * P],
                                    self.xhat[:, t, j * P:(j + 1) * P], self.ident[:])
            last.then_inc(self.s_turned, 1)

    def on_scalar(self, nc, act):
        act.wait_ge(self.s_var, 1)
        nc.scalar.activation(self.small[:, 1, :], self.small[:, 0, :], ACT.Sqrt).then_inc(self.s_root, 1)
        for t in range(NT):
            act.wait_ge(self.s_turned, t + 1)
            for dst in (self.xT,) if self.split is None else (self.xT, self.split[0]):
                last = nc.scalar.copy(dst[:, :, t * P:(t + 1) * P],
                                      self.banks[t % 2][:].rearrange("p (j n) -> p j n", j=KD))
            last.then_inc(self.s_xT, 1)

    def low_on_vector(self, dve):
        for t in range(NT):
            c = slice(t * P, (t + 1) * P)
            dve.wait_ge(self.s_xT, t + 1)
            dve.tensor_tensor(self.split[1][:, :, c], self.xT[:, :, c], self.split[0][:, :, c],
                              ALU.subtract).then_inc(self.s_low, 1)



def constants(k, ident, tri, low):
    nc = k.nc
    with ExitStack() as ctx:
        s_set = k.sem(ctx, "c_set")
        s_done = k.sem(ctx, "c_done")
        block = ctx.enter_context(nc.Block())

        @block.gpsimd
        def _(pool):
            pool.memset(ident[:], 0.0).then_inc(s_set, 1)
            pool.memset(tri[:], 1.0).then_inc(s_set, 1)
            pool.memset(low[:], 0.0).then_inc(s_set, 1)
            pool.wait_ge(s_set, 3)
            pool.affine_select(out=ident[:], in_=ident[:], compare_op=ALU.not_equal, fill=1.0, base=0,
                               pattern=[[-1, P]], channel_multiplier=1).then_inc(s_done, 1)
            pool.affine_select(out=tri[:], in_=tri[:], compare_op=ALU.is_ge, fill=0.0, base=0,
                               pattern=[[1, P]], channel_multiplier=-1).then_inc(s_done, 1)
            pool.wait_ge(s_done, 2)
            pool.affine_select(out=tri[:, L:P], in_=tri[:, L:P], compare_op=ALU.is_ge, fill=0.0, base=-L,
                               pattern=[[0, P - L]], channel_multiplier=1).then_inc(s_done, 1)
            pool.affine_select(out=low[:], in_=low[:], compare_op=ALU.is_ge, fill=FAR, base=0,
                               pattern=[[-1, P]], channel_multiplier=1).then_inc(s_done, 1)
            pool.wait_ge(s_done, 4)
            pool.affine_select(out=low[:, 0:L], in_=low[:, 0:L], compare_op=ALU.is_ge, fill=FAR, base=L - 1,
                               pattern=[[0, L]], channel_multiplier=-1).then_inc(s_done, 1)
            pool.wait_ge(s_done, 5)



def cross0_queries(k, ident, qT, wk, wv, bk):
    nc, d = k.nc, k.d
    with ExitStack() as ctx:
        x = k.sb(ctx, "q0_x", [P, NT, D])
        xT = k.sb(ctx, "q0_xT", [P, KD, TOK])
        wq = k.sb(ctx, "q0_wq", [P, KD, D])
        bq = k.sb(ctx, "q0_bq", [P, KD])
        qf = k.sb(ctx, "q0_qf", [P, 2, 512])
        wkf = k.sb(ctx, "q0_wkf", [P, 2, KC, D])
        banks = [k.ps(ctx, f"q0_bank{n}", [P, 512]) for n in range(4)]
        s_x = k.sem(ctx, "q0_x_in")
        s_x2 = k.sem(ctx, "q0_x_in2")
        s_w = k.sem(ctx, "q0_w_in")
        s_wkv = k.sem(ctx, "q0_wkv_in")
        s_split = k.sem(ctx, "q0_split")
        s_q = k.sem(ctx, "q0_q_done")
        s_qf = k.sem(ctx, "q0_qf_done")
        s_hi = k.sem(ctx, "q0_hi_done")
        s_lo = k.sem(ctx, "q0_lo_done")
        norm = Norm(k, ctx, "q0", x, ident, banks[0:2], xT,
                    lambda t: (s_x, 16) if t < NT // 2 else (s_x2, 16))
        block = ctx.enter_context(nc.Block())
        xv = d["x"].rearrange("(t p) n -> p t n", p=P)
        groups = [(m, c) for m in range(KD) for c in range(TOK // 512)]

        @block.sync
        def _(sp):
            sp.dma_start(x[:, 0:NT // 2, :], xv[:, 0:NT // 2, :]).then_inc(s_x, 16)
            sp.dma_start(x[:, NT // 2:NT, :], xv[:, NT // 2:NT, :]).then_inc(s_x2, 16)
            sp.dma_start(wq[:], d["L0_xattn_Wq"].rearrange("(j p) n -> p j n", p=P)).then_inc(s_w, 16)
            sp.dma_start(bq[:], d["L0_xattn_bq"]).then_inc(s_w, 16)
            sp.dma_start(wkf[:, 0], d["L0_xattn_Wk"].rearrange("(j p) n -> p j n", p=P)).then_inc(s_wkv, 16)
            sp.dma_start(wkf[:, 1], d["L0_xattn_Wv"].rearrange("(j p) n -> p j n", p=P)).then_inc(s_wkv, 16)
            sp.dma_start(bk[:], d["L0_xattn_bk"]).then_inc(s_wkv, 16)
            sp.wait_ge(s_wkv, 48)

        @block.vector
        def _(dve):
            norm.on_vector(dve)
            dve.wait_ge(s_wkv, 48)
            for n, w in enumerate((wk, wv)):
                dve.tensor_copy(w[:, 0], wkf[:, n]).then_inc(s_split, 1)
            dve.wait_ge(s_split, 2)
            for n, w in enumerate((wk, wv)):
                dve.tensor_tensor(w[:, 1], wkf[:, n], w[:, 0], ALU.subtract).then_inc(s_split, 1)
            for n, (m, c) in enumerate(groups):
                dve.wait_ge(s_q, n + 1)
                dve.tensor_scalar(qf[:, n % 2, :], banks[2 + n % 2][:], bq[:, m:m + 1], float(DH) ** -0.5,
                                  ALU.add, ALU.mult).then_inc(s_qf, 1)
                half = qT[:, 8 * c:8 * c + 8, :, m, :]
                src = qf[:, n % 2, :].rearrange("p (b q) -> p b q", q=L)
                dve.wait_ge(s_qf, n + 1)
                dve.tensor_copy(half[:, :, 0, :], src).then_inc(s_hi, 1)
                dve.wait_ge(s_hi, n + 1)
                dve.tensor_tensor(half[:, :, 1, :], src, half[:, :, 0, :], ALU.subtract).then_inc(s_lo, 1)

        @block.scalar
        def _(act):
            norm.on_scalar(nc, act)

        @block.tensor
        def _(pe):
            norm.on_tensor(pe)
            pe.wait_ge(s_w, 32)
            pe.wait_ge(norm.s_xT, NT)
            for n, (m, c) in enumerate(groups):
                if n >= 2:
                    pe.wait_ge(s_qf, n - 1)
                for j in range(KD):
                    last = pe.matmul(banks[2 + n % 2][:], wq[:, j, m * P:(m + 1) * P],
                                     xT[:, j, 512 * c:512 * c + 512], start=(j == 0), stop=(j == KD - 1))
                last.then_inc(s_q, 1)



PROJ = []
for _c in range(len(CHUNKS)):
    PROJ += [("K", _c, m) for m in range(KD)]
    PROJ += [("V", _c, t) for t in range(4 * _c, min(4 * _c + 4, len(KTILES)))]
NPROJ = len(PROJ)
SLICES = [(4 * p, min(4 * p + 4, NPROJ)) if p < 6 else ((24, 27) if p == 6 else (27, NPROJ)) for p in range(NPAIR)]
CHUNK_AT = {0: 0, 1: 1, 3: 2, 5: 3}
RING = 3


def batch_plan(project, first):
    slots = []
    for p in range(NPAIR):
        proj = list(range(*SLICES[p])) if project else []
        turn = [] if (p == 0 and first) else [0, 1, 2, 3]
        steps = []
        for j in (0, 1):
            steps += [("proj", proj[j])] if j < len(proj) else []
            steps += [("turn", j)] if turn else []
        steps += [("proj", proj[2])] if len(proj) > 2 else []
        steps += [("turn", 2), ("pv", 0), ("turn", 3), ("pv", 1)] if turn else []
        steps += [("proj", proj[3])] if len(proj) > 3 else []
        steps += [("pv", 2), ("pv", 3)] if turn else []
        if p == 1 and not first:
            steps += [("out", 0)]
        slots.append(steps)
    return slots


def last_plan():
    return [[("turn", 0), ("turn", 1), ("turn", 2), ("pv", 0), ("turn", 3), ("pv", 1), ("pv", 2),
             ("pv", 3), ("out", 0)]]


def ring_uses(plan):
    return sum(1 for s in plan for e in s if e[0] != "pv")


PLAN_FIRST = batch_plan(True, True)
PLAN_MID = batch_plan(True, False)
PLAN_END = batch_plan(False, False)
PLAN_LAST = last_plan()
N_FIRST, N_MID, N_END = ring_uses(PLAN_FIRST), ring_uses(PLAN_MID), ring_uses(PLAN_END)


def ring_base(b):
    return NPROJ + N_FIRST - N_MID + b * N_MID


def cross0_batches(k, ident, qT, wk, wv, bk, catT, bvT):
    nc, d = k.nc, k.d
    with ExitStack() as ctx:
        stage = k.sb(ctx, "x0_stage", [P, 2, KC, 512])
        chi = k.sb(ctx, "x0_ctx_hi", [P, 2, KC, 512], BF16)
        clo = k.sb(ctx, "x0_ctx_lo", [P, 2, KC, 512], BF16)
        qp = k.sb(ctx, "x0_q_padded", [P, 2, 2, KD, 2, 2, L], BF16)
        kT = k.sb(ctx, "x0_kT", [P, 2, 2, KD, NK], BF16)
        v = k.sb(ctx, "x0_v", [P, 2, 2, len(KTILES), D], BF16)
        prob = k.sb(ctx, "x0_prob", [P, 2, NK])
        pT = k.sb(ctx, "x0_pT", [P, 2, NTG, 512], BF16)
        nmax = k.sb(ctx, "x0_negmax", [P, 2])
        rsum = k.sb(ctx, "x0_rowsum", [P, 2])
        rinv = k.sb(ctx, "x0_rowinv", [P, 2])
        o = k.sb(ctx, "x0_o", [P, 2, NPAIR, DH])
        ot = k.sb(ctx, "x0_ot", [P, 2 * P])
        score = k.ps(ctx, "x0_score", [P, 2048])
        ring = [k.ps(ctx, f"x0_ring{n}", [P, 512]) for n in range(RING)]
        pv = k.ps(ctx, "x0_pv", [P, 512])
        ctx_in = [k.sem(ctx, f"x0_ctx_in{n}") for n in range(2)]
        qp_in = [k.sem(ctx, f"x0_qp_in{n}") for n in range(2)]
        qp_zero = k.sem(ctx, "x0_qp_zero")
        chi_done = k.sem(ctx, "x0_chi_done")
        clo_done = k.sem(ctx, "x0_clo_done")
        ring_full = k.sem(ctx, "x0_ring_full")
        hi_done = k.sem(ctx, "x0_hi_done")
        ring_free = k.sem(ctx, "x0_ring_free")
        s_done = k.sem(ctx, "x0_scores_done")
        max_done = k.sem(ctx, "x0_max_done")
        exp_done = k.sem(ctx, "x0_exp_done")
        pv_done = k.sem(ctx, "x0_pv_done")
        inv_done = k.sem(ctx, "x0_inv_done")
        o_done = k.sem(ctx, "x0_o_done")
        block = ctx.enter_context(nc.Block())
        ctxT = d["ctxT"].rearrange("b (j p) n -> p b j n", p=P)

        def each_batch(eng, do, last=None):
            do(0, 0, PLAN_FIRST, NPROJ)
            with eng.Fori(0, (B - 2) // 2) as i:
                for u in range(2):
                    do(2 * i + 1 + u, (1 + u) % 2, PLAN_MID, ring_base(2 * i + 1 + u))
            do(B - 1, (B - 1) % 2, PLAN_END, ring_base(B - 1))
            do(B, B % 2, PLAN_LAST, ring_base(B - 1) + N_END)

        def pair_of(b, p):
            return 8 * b + p - 1

        @block.sync
        def _(sp):
            def load_chunk(b, c, ready):
                if ready is not None:
                    sp.wait_ge(clo_done, ready)
                n0, n = CHUNKS[c]
                src = ctxT[:, b, :, n0:n0 + n] if isinstance(b, int) else \
                    ctxT[:, bass.ds(b, 1), :, n0:n0 + n].rearrange("p a j n -> p (a j) n")
                sp.dma_start(stage[:, c % 2, :, 0:n], src).then_inc(ctx_in[c % 2], 16)

            def load_queries(b, par, free):
                if free is not None:
                    sp.wait_ge(s_done, free)
                for a in range(4):
                    src = qT[32 * a:32 * a + 32, b] if isinstance(b, int) else \
                        qT[32 * a:32 * a + 32, bass.ds(b, 1)].rearrange("p a h m q -> p (a h) m q")
                    for hl in range(2):
                        sp.dma_start(qp[32 * a:32 * a + 32, par, hl, :, a // 2, a % 2, :],
                                     src[:, hl]).then_inc(qp_in[par], 16)

            load_chunk(0, 0, None)
            load_chunk(0, 1, None)
            sp.wait_ge(qp_zero, 1)
            load_queries(0, 0, None)
            load_chunk(0, 2, 1)
            load_chunk(0, 3, 2)
            load_chunk(1, 0, 3)
            load_chunk(1, 1, 4)
            load_queries(1, 1, None)
            load_chunk(1, 2, 5)
            load_chunk(1, 3, 6)
            load_chunk(2, 0, 7)
            load_chunk(2, 1, 8)
            with sp.Fori(0, (B - 4) // 2) as i:
                for u in range(2):
                    b = 2 * i + 1 + u
                    load_queries(b + 1, u % 2, 8 * b)
                    load_chunk(b + 1, 2, 4 * b + 5)
                    load_chunk(b + 1, 3, 4 * b + 6)
                    load_chunk(b + 2, 0, 4 * b + 7)
                    load_chunk(b + 2, 1, 4 * b + 8)
            for b in (B - 3, B - 2):
                load_queries(b + 1, (b + 1) % 2, 8 * b)
                load_chunk(b + 1, 2, 4 * b + 5)
                load_chunk(b + 1, 3, 4 * b + 6)
                if b + 2 < B:
                    load_chunk(b + 2, 0, 4 * b + 7)
                    load_chunk(b + 2, 1, 4 * b + 8)

        @block.gpsimd
        def _(pool):
            pool.memset(qp[:], 0.0).then_inc(qp_zero, 1)
            with pool.Fori(0, B) as b:
                for c, (n0, n) in enumerate(CHUNKS):
                    pool.wait_ge(chi_done, 4 * b + c + 1)
                    pool.tensor_tensor(clo[:, c % 2, :, 0:n], stage[:, c % 2, :, 0:n],
                                       chi[:, c % 2, :, 0:n], ALU.subtract).then_inc(clo_done, 1)

        def ring_events(plan):
            r = 0
            for p, steps in enumerate(plan):
                for e in steps:
                    yield p, e, (None if e[0] == "pv" else r)
                    r += e[0] != "pv"

        def turn_place(plan, at, j):
            return next(r for p, e, r in ring_events(plan) if p == at and e == ("turn", j))

        def proj_end(plan, c):
            return 1 + max(r for p, e, r in ring_events(plan)
                           if e[0] == "proj" and PROJ[e[1]][1] == c)

        @block.tensor
        def _(pe):
            def wait_bank(r, base):
                if r >= RING:
                    pe.wait_ge(ring_free, base + (r - RING + 1))
                elif not (isinstance(base, int) and base == 0):
                    pe.wait_ge(ring_free, base - 1 if r == 0 else base)

            def project(n, b_next, par, r, base):
                kind, c, m = PROJ[n]
                n0, w = CHUNKS[c]
                if n == 0 or PROJ[n - 1][1] != c:
                    pe.wait_ge(clo_done, 4 * b_next + c + 1)
                wait_bank(r, base)
                bank, i = ring[r % RING], 0
                for hl_w, src in ((0, chi), (1, chi), (0, clo)):
                    for j in range(KC):
                        if kind == "K":
                            out_, lhs, rhs = bank[:, 0:w], wk[:, hl_w, j, m * P:(m + 1) * P], src[:, c % 2, j, 0:w]
                        else:
                            k0, kw = KTILES[m]
                            out_, lhs, rhs = bank[0:kw, :], src[:, c % 2, j, k0 - n0:k0 - n0 + kw], wv[:, hl_w, j, :]
                        last = pe.matmul(out_, lhs, rhs, start=(i == 0), stop=(i == 3 * KC - 1))
                        i += 1
                last.then_inc(ring_full, 1)

            def batch(b, par, plan, base):
                if plan is not PLAN_LAST:
                    pe.wait_ge(qp_in[par], 128 * (b // 2 + 1) if isinstance(b, int) else
                               64 * (b + (1 if par else 2)))
                for p, steps in enumerate(plan):
                    if plan is not PLAN_LAST:
                        if p == 0:
                            pe.wait_ge(ring_free, base)
                        if p or plan is not PLAN_FIRST:
                            pe.wait_ge(exp_done, 8 * b + p)
                        for c, (n0, w) in enumerate(CHUNKS):
                            for i, (hq, hk) in enumerate(((0, 0), (1, 0), (0, 1))):
                                last = pe.matmul(score[:, 512 * c:512 * c + w],
                                                 qp[:, par, hq, p // 2, p % 2, :, :].rearrange("p a q -> p (a q)"),
                                                 kT[:, par, hk, p // 2, n0:n0 + w], start=(i == 0), stop=(i == 2))
                        last.then_inc(s_done, 1)
                    pp, vpar = ((p - 1) % NPAIR, par if p else 1 - par)
                    for p_, e, r in ring_events(plan):
                        if p_ != p:
                            continue
                        if e[0] == "proj":
                            project(e[1], b + 1, 1 - par, r, base)
                        elif e[0] == "turn":
                            if e[1] == 0:
                                pe.wait_ge(exp_done, 8 * b + p)
                            wait_bank(r, base)
                            for i, (k0, kw) in enumerate(TGROUPS[e[1]]):
                                last = pe.transpose(ring[r % RING][0:kw, P * i:P * i + P],
                                                    prob[:, pp % 2, k0:k0 + kw], ident[:])
                            last.then_inc(ring_full, 1)
                        elif e[0] == "pv":
                            j = e[1]
                            if j == 0 and not (plan is PLAN_FIRST and p == 1):
                                pe.wait_ge(o_done, 8 * b + p - 1)
                            pe.wait_ge(ring_free, base + (turn_place(plan, p, j) + 1))
                            for i, (k0, kw) in enumerate(TGROUPS[j]):
                                for n, (hp, hv) in enumerate(((0, 0), (0, 1), (1, 0))):
                                    last = pe.matmul(pv[:, 0:2 * DH], pT[0:kw, hp, j, P * i:P * i + P],
                                                     v[0:kw, vpar, hv, 4 * j + i, 2 * DH * pp:2 * DH * (pp + 1)],
                                                     start=(j == 0 and i == 0 and n == 0),
                                                     stop=(j == NTG - 1 and n == 2))
                            if j == NTG - 1:
                                last.then_inc(pv_done, 1)
                        else:
                            pe.wait_ge(o_done, 8 * b)
                            wait_bank(r, base)
                            for h in range(2):
                                last = pe.transpose(ring[r % RING][:, P * h:P * h + P],
                                                    o[:, 1 - par, 4 * h:4 * h + 4, :].rearrange("p a d -> p (a d)"),
                                                    ident[:])
                            last.then_inc(ring_full, 1)

            for n in range(NPROJ):
                project(n, 0, 0, n, 0)
            each_batch(pe, batch)

        @block.scalar
        def _(act):
            def project_hi(n, par, r, number):
                kind, c, m = PROJ[n]
                n0, w = CHUNKS[c]
                act.wait_ge(ring_full, number)
                if kind == "K":
                    nc.scalar.activation(kT[:, par, 0, m, n0:n0 + w], ring[r % RING][:, 0:w], ACT.Identity,
                                         bias=bk[:, m:m + 1]).then_inc(hi_done, 1)
                else:
                    kw = KTILES[m][1]
                    nc.scalar.copy(v[0:kw, par, 0, m, :], ring[r % RING][0:kw, :]).then_inc(hi_done, 1)

            def batch(b, par, plan, base):
                for p, steps in enumerate(plan):
                    def exps():
                        act.wait_ge(max_done, 8 * b + p + 1)
                        nc.scalar.activation(prob[:, p % 2, :], score[:, 0:NK], ACT.Exp, bias=nmax[:, p % 2:p % 2 + 1],
                                             accum_out=rsum[:, p % 2:p % 2 + 1]).then_inc(exp_done, 1)
                    done = plan is PLAN_LAST
                    if not done and (not steps or steps[0][0] != "proj"):
                        exps()
                        done = True
                    for p_, e, r in ring_events(plan):
                        if p_ != p or r is None:
                            continue
                        if e[0] == "proj":
                            project_hi(e[1], 1 - par, r, base + (r + 1))
                        else:
                            act.wait_ge(ring_full, base + (r + 1))
                            if e[0] == "turn":
                                n = P * len(TGROUPS[e[1]])
                                kw = TGROUPS[e[1]][0][1]
                                nc.scalar.copy(pT[0:kw, 0, e[1], 0:n], ring[r % RING][0:kw, 0:n]).then_inc(hi_done, 1)
                            else:
                                nc.scalar.copy(ot[:], ring[r % RING][:, 0:2 * P]).then_inc(hi_done, 1)
                        if not done:
                            exps()
                            done = True

            for n in range(NPROJ):
                project_hi(n, 0, n, n + 1)
            each_batch(act, batch)

        @block.vector
        def _(dve):
            def split_chunk(b, c, ready):
                n0, n = CHUNKS[c]
                dve.wait_ge(ctx_in[c % 2], 16 * (2 * b + (c // 2 + 1)))
                if ready is not None:
                    dve.wait_ge(ring_full, ready)
                dve.tensor_copy(chi[:, c % 2, :, 0:n], stage[:, c % 2, :, 0:n]).then_inc(chi_done, 1)

            def project_lo(n, par, r, number):
                kind, c, m = PROJ[n]
                n0, w = CHUNKS[c]
                dve.wait_ge(hi_done, number)
                if kind == "K":
                    dve.scalar_tensor_tensor(kT[:, par, 1, m, n0:n0 + w], ring[r % RING][:, 0:w], bk[:, m:m + 1],
                                             kT[:, par, 0, m, n0:n0 + w], ALU.add, ALU.subtract).then_inc(ring_free, 1)
                else:
                    kw = KTILES[m][1]
                    dve.tensor_tensor(v[0:kw, par, 1, m, :], ring[r % RING][0:kw, :], v[0:kw, par, 0, m, :],
                                      ALU.subtract).then_inc(ring_free, 1)

            def batch(b, par, plan, base):
                for p, steps in enumerate(plan):
                    if plan in (PLAN_FIRST, PLAN_MID) and p in CHUNK_AT:
                        c = CHUNK_AT[p]
                        split_chunk(b + 1, c, base if c < 2 else base + proj_end(plan, c - 2))
                    if plan is not PLAN_LAST:
                        dve.wait_ge(s_done, 8 * b + p + 1)
                        dve.tensor_reduce(nmax[:, p % 2:p % 2 + 1], score[:, 0:NK], AX, ALU.max,
                                          negate=True).then_inc(max_done, 1)
                    pp, opar = ((p - 1) % NPAIR, par if p else 1 - par)
                    for p_, e, r in ring_events(plan):
                        if p_ != p:
                            continue
                        if e[0] == "proj":
                            project_lo(e[1], 1 - par, r, base + (r + 1))
                        elif e[0] == "turn":
                            n = P * len(TGROUPS[e[1]])
                            kw = TGROUPS[e[1]][0][1]
                            dve.wait_ge(hi_done, base + (r + 1))
                            dve.tensor_tensor(pT[0:kw, 1, e[1], 0:n], ring[r % RING][0:kw, 0:n], pT[0:kw, 0, e[1], 0:n],
                                              ALU.subtract).then_inc(ring_free, 1)
                        elif e[0] == "out":
                            dve.wait_ge(hi_done, base + (r + 1))
                            tok = bass.ds(L * (b - 1), L) if not isinstance(b, int) else slice(L * (b - 1), L * b)
                            dve.tensor_tensor(catT[:, :, :, tok], ot[:].rearrange("p (a h q) -> p a h q", a=2, h=2),
                                              bvT[:].rearrange("p (a h) -> p a h", a=2).unsqueeze(3).broadcast_to([P, 2, 2, L]),
                                              ALU.add).then_inc(ring_free, 1)
                        elif e == ("pv", 3):
                            dve.reciprocal(rinv[:, pp % 2:pp % 2 + 1], rsum[:, pp % 2:pp % 2 + 1]).then_inc(inv_done, 1)
                            dve.wait_ge(inv_done, 8 * b + p)
                            dve.wait_ge(pv_done, 8 * b + p)
                            dve.tensor_scalar(o[0:L, opar, pp, :], pv[0:L, 0:DH], rinv[0:L, pp % 2:pp % 2 + 1], None,
                                              ALU.mult)
                            dve.tensor_scalar(o[L:P, opar, pp, :], pv[L:P, DH:2 * DH], rinv[L:P, pp % 2:pp % 2 + 1], None,
                                              ALU.mult).then_inc(o_done, 1)

            for c in range(4):
                split_chunk(0, c, None if c < 2 else proj_end([[("proj", n) for n in range(NPROJ)]], c - 2))
                for n in range(NPROJ):
                    if PROJ[n][1] == c - 1:
                        project_lo(n, 0, n, n + 1)
            for n in range(NPROJ):
                if PROJ[n][1] == 3:
                    project_lo(n, 0, n, n + 1)
            each_batch(dve, batch)



def load_x_again(k, sp, x, s_in):
    sp.dma_start(x[:], k.d["x"].rearrange("(t p) n -> p t n", p=P)).then_inc(s_in, 16)


def cross0_output(k, x, catT):
    nc, d = k.nc, k.d
    with ExitStack() as ctx:
        wo = k.sb(ctx, "o0_wo", [P, 4, D])
        bo = k.sb(ctx, "o0_bo", [P, D])
        banks = [k.ps(ctx, f"o0_bank{n}", [P, 512]) for n in range(2)]
        s_in = k.sem(ctx, "o0_in")
        s_x = k.sem(ctx, "o0_x")
        s_sum = k.sem(ctx, "o0_sum")
        s_out = k.sem(ctx, "o0_out")
        block = ctx.enter_context(nc.Block())

        @block.sync
        def _(sp):
            load_x_again(k, sp, x, s_in)
            sp.dma_start(wo[:], d["L0_xattn_Wo"].rearrange("t p n -> p t n")).then_inc(s_in, 16)
            sp.dma_start(bo[:], d["L0_xattn_bo"].partition_broadcast(P)).then_inc(s_in, 16)
            sp.wait_ge(s_in, 48)

        @block.tensor
        def _(pe):
            pe.wait_ge(s_in, 48)
            for t in range(NT):
                if t >= 2:
                    pe.wait_ge(s_out, t - 1)
                for i in range(4):
                    last = pe.matmul(banks[t % 2][:], catT[:, i // 2, i % 2, t * P:(t + 1) * P], wo[:, i, :],
                                     start=(i == 0), stop=(i == 3))
                last.then_inc(s_sum, 1)

        @block.vector
        def _(dve):
            dve.wait_ge(s_in, 48)
            for t in range(NT):
                dve.tensor_tensor(x[:, t, :], x[:, t, :], bo[:], ALU.add).then_inc(s_x, 1)
            for t in range(NT):
                dve.wait_ge(s_x, t + 1)
                dve.wait_ge(s_sum, t + 1)
                dve.tensor_tensor(x[:, t, :], x[:, t, :], banks[t % 2][:], ALU.add).then_inc(s_out, 1)




NS = 64


def state_space(k, ident, tri, x):
    nc, d = k.nc, k.d
    with ExitStack() as ctx:
        xT = k.sb(ctx, "m_xT", [P, KD, TOK])
        wB = k.sb(ctx, "m_wB", [P, NPAIR, 2 * NS])
        wC = k.sb(ctx, "m_wC", [P, NPAIR, 2 * NS])
        wX = k.sb(ctx, "m_wX", [P, KD, P])
        wG = k.sb(ctx, "m_wG", [P, KD, P])
        wA = k.sb(ctx, "m_wA", [P, KD * H])
        wO = k.sb(ctx, "m_wO", [P, KD, D])
        bB = k.sb(ctx, "m_bB", [P, NPAIR])
        bC = k.sb(ctx, "m_bC", [P, NPAIR])
        bG = k.sb(ctx, "m_bG", [P, KD])
        bX = k.sb(ctx, "m_bX", [P, D])
        bA = k.sb(ctx, "m_bA", [P, H])
        bO = k.sb(ctx, "m_bO", [P, D])
        sel = k.sb(ctx, "m_sel", [H, H, P])
        bT = k.sb(ctx, "m_bT", [P, NPAIR, TOK])
        cT = k.sb(ctx, "m_cT", [P, NPAIR, TOK])
        xn = k.sb(ctx, "m_xn", [P, NT, D])
        xb = k.sb(ctx, "m_xb", [P, 2, D])
        gT = k.sb(ctx, "m_gT", [P, KD, TOK])
        la = k.sb(ctx, "m_la", [P, NT, H])
        cum = k.sb(ctx, "m_cum", [P, NT, H])
        cumT = k.sb(ctx, "m_cumT", [H, TOK])
        diff = k.sb(ctx, "m_diff", [P, 2, 4, P])
        dec = k.sb(ctx, "m_dec", [P, 2, 4, P])
        mix = k.sb(ctx, "m_mix", [P, 2, 4, P])
        banks = [k.ps(ctx, f"m_bank{n}", [P, 512]) for n in range(8)]
        s_zero = k.sem(ctx, "m_zero")
        s_sel = k.sem(ctx, "m_sel_done")
        s_w = k.sem(ctx, "m_w_in")
        s_b = k.sem(ctx, "m_b_in")
        s_p = k.sem(ctx, "m_p_full")
        s_pf = k.sem(ctx, "m_p_free")
        s_x = k.sem(ctx, "m_x_full")
        s_xb = k.sem(ctx, "m_xb_done")
        s_xn = k.sem(ctx, "m_xn_done")
        s_g = k.sem(ctx, "m_g_full")
        s_gT = k.sem(ctx, "m_gT_done")
        s_a = k.sem(ctx, "m_a_full")
        s_la = k.sem(ctx, "m_la_done")
        s_c = k.sem(ctx, "m_cum_full")
        s_cum = k.sem(ctx, "m_cum_done")
        s_cumT = k.sem(ctx, "m_cumT_done")
        s_r = k.sem(ctx, "m_r_full")
        s_diff = k.sem(ctx, "m_diff_done")
        s_dec = k.sem(ctx, "m_dec_done")
        s_mask = k.sem(ctx, "m_mask_done")
        s_mix = k.sem(ctx, "m_mix_done")
        s_y = k.sem(ctx, "m_y_full")
        s_yg = k.sem(ctx, "m_yg_done")
        s_o = k.sem(ctx, "m_o_full")
        s_xo = k.sem(ctx, "m_xo")
        s_out = k.sem(ctx, "m_out")
        norm = Norm(k, ctx, "m", x, ident, banks[0:2], xT)
        yg = norm.xhat[:].rearrange("p t n -> p (t n)").rearrange("p (g n) -> p g n", g=KD)
        block = ctx.enter_context(nc.Block())
        projections = [(w, dst, pr, c) for w, dst in ((0, bT), (1, cT)) for pr in range(NPAIR) for c in range(2)]
        units = [(t, g) for t in range(NT) for g in range(KD)]

        @block.gpsimd
        def _(pool):
            for w in (wB, wC, wX, wG, wA):
                pool.memset(w[:], 0.0).then_inc(s_zero, 1)
            pool.memset(sel[:], 0.0).then_inc(s_zero, 1)
            pool.wait_ge(s_zero, 6)
            pool.affine_select(out=sel[:], in_=sel[:], compare_op=ALU.not_equal, fill=1.0, base=0,
                               pattern=[[-1, H], [0, P]], channel_multiplier=1).then_inc(s_sel, 1)
            for n in range(len(units)):
                pool.wait_ge(s_dec, n + 1)
                pool.tensor_tensor(diff[:, n % 2], dec[:, n % 2],
                                   tri[:].unsqueeze(1).broadcast_to([P, 4, P]), ALU.mult).then_inc(s_mask, 1)

        @block.sync
        def _(sp):
            for dst, n in ((bB, "L0_attn_bB"), (bC, "L0_attn_bC"), (bG, "L0_attn_bG")):
                sp.dma_start(dst[:], d[n]).then_inc(s_b, 16)
            for dst, n in ((bX, "L0_attn_bX"), (bA, "L0_attn_bA"), (bO, "L0_attn_bO")):
                sp.dma_start(dst[:], d[n].partition_broadcast(P)).then_inc(s_b, 16)
            sp.dma_start(wO[:], d["L0_attn_W_out"].rearrange("(g p) n -> p g n", p=P)).then_inc(s_b, 16)
            sp.wait_ge(s_zero, 5)
            for a in range(4):
                r = slice(32 * a, 32 * a + 32)
                c = slice(NS * (a % 2), NS * (a % 2) + NS)
                sp.dma_start(wB[r, a // 2::2, c], d["L0_attn_WB"][:, a::4, :]).then_inc(s_w, 16)
                sp.dma_start(wC[r, a // 2::2, c], d["L0_attn_WC"][:, a::4, :]).then_inc(s_w, 16)
                sp.dma_start(wX[r, :, r], d["L0_attn_WX"][:, a::4, :]).then_inc(s_w, 16)
                sp.dma_start(wG[r, :, r], d["L0_attn_WG"][:, a::4, :]).then_inc(s_w, 16)
                sp.dma_start(wA[r, a::H + 4], d["L0_attn_WA"][:, a::4], allow_slow_non_contiguous=True).then_inc(s_w, 16)
            sp.wait_ge(s_w, 16 * 20)
            sp.wait_ge(s_b, 16 * 7)

        @block.tensor
        def _(pe):
            norm.on_tensor(pe)
            pe.wait_ge(norm.s_xT, NT)
            pe.wait_ge(s_w, 16 * 20)
            for t in range(NT):
                tile = slice(t * P, (t + 1) * P)
                for g in range(KD):
                    last = pe.matmul(banks[2][:, H * t:H * t + H], xT[:, g, tile], wA[:, H * g:H * g + H],
                                     start=(g == 0), stop=(g == KD - 1))
            last.then_inc(s_a, 1)
            for n, (w, dst, pr, c) in enumerate(projections):
                if n >= 2:
                    pe.wait_ge(s_pf, n - 1)
                pe.matmul(banks[n % 2][:], (wB, wC)[w][:, pr, :], xT[:, pr // 2, 512 * c:512 * c + 512],
                          start=True, stop=True).then_inc(s_p, 1)
                if n == 4:
                    pe.wait_ge(s_la, 1)
                    pe.matmul(banks[3][:, 0:NT * H], tri[:], la[:].rearrange("p t h -> p (t h)"),
                              start=True, stop=True).then_inc(s_c, 1)
                    for t in range(NT):
                        last = pe.matmul(banks[4 + t // 4][0:H, P * (t % 4):P * (t % 4) + P], la[:, t, :], tri[:],
                                         start=True, stop=True)
                    last.then_inc(s_c, 1)
            for t in range(NT):
                if t >= 2:
                    pe.wait_ge(s_xb, t - 1)
                for g in range(KD):
                    last = pe.matmul(banks[6 + t % 2][:, P * g:P * g + P], xT[:, g, t * P:(t + 1) * P], wX[:, g, :],
                                     start=True, stop=True)
                last.then_inc(s_x, 1)
            pe.wait_ge(s_pf, len(projections))
            for n in range(2 * KD):
                if n >= 2:
                    pe.wait_ge(s_gT, n - 1)
                pe.matmul(banks[n % 2][:], wG[:, n // 2, :], xT[:, n // 2, 512 * (n % 2):512 * (n % 2) + 512],
                          start=True, stop=True).then_inc(s_g, 1)
            pe.wait_ge(s_gT, 2 * KD)
            pe.wait_ge(s_xb, NT)
            pe.wait_ge(s_sel, 1)
            pe.wait_ge(s_cumT, 2)
            pe.wait_ge(s_cum, 1)

            def products(n):
                t, g = units[n]
                pe.wait_ge(s_mix, n + 1)
                if n == 0:
                    pe.wait_ge(s_xn, NT)
                if n >= 2:
                    pe.wait_ge(s_yg, n - 1)
                for a in range(4):
                    last = pe.matmul(banks[6 + n % 2][32 * a:32 * a + 32, 0:P],
                                     xn[:, t, P * g + 32 * a:P * g + 32 * a + 32], mix[:, n % 2, a, :],
                                     start=True, stop=True)
                last.then_inc(s_y, 1)

            for n, (t, g) in enumerate(units):
                tile = slice(t * P, (t + 1) * P)
                if n >= 2:
                    pe.wait_ge(s_diff, 4 * (n - 1))
                for a in range(4):
                    last = pe.matmul(banks[n % 2][:, P * a:P * a + P], sel[:, 4 * g + a, :], cumT[:, tile],
                                     start=True, stop=True)
                last.then_inc(s_r, 1)
                if n >= 2:
                    products(n - 2)
                for a in range(4):
                    r = slice(NS * (a % 2), NS * (a % 2) + NS)
                    last = pe.matmul(banks[2 + 2 * (n % 2) + a % 2][:, P * (a // 2):P * (a // 2) + P],
                                     bT[r, 2 * g + a // 2, tile],
                                     cT[r, 2 * g + a // 2, tile], start=True, stop=True)
                last.then_inc(s_r, 1)
            products(len(units) - 2)
            products(len(units) - 1)
            pe.wait_ge(s_yg, len(units))
            for t in range(NT):
                if t >= 2:
                    pe.wait_ge(s_out, t - 1)
                for g in range(KD):
                    last = pe.matmul(banks[6 + t % 2][:], yg[:, g, t * P:(t + 1) * P], wO[:, g, :],
                                     start=(g == 0), stop=(g == KD - 1))
                last.then_inc(s_o, 1)

        @block.scalar
        def _(act):
            norm.on_scalar(nc, act)
            act.wait_ge(s_b, 16 * 7)
            for n, (w, dst, pr, c) in enumerate(projections):
                act.wait_ge(s_p, n + 1)
                nc.scalar.activation(dst[:, pr, 512 * c:512 * c + 512], banks[n % 2][:], ACT.Silu,
                                     bias=(bB, bC)[w][:, pr:pr + 1]).then_inc(s_pf, 1)
            for t in range(NT):
                act.wait_ge(s_xb, t + 1)
                nc.scalar.activation(xn[:, t, :], xb[:, t % 2, :], ACT.Silu).then_inc(s_xn, 1)
            for n in range(len(units)):
                act.wait_ge(s_diff, 4 * (n + 1))
                if n >= 2:
                    act.wait_ge(s_mask, n - 1)
                nc.scalar.activation(dec[:, n % 2], diff[:, n % 2], ACT.Exp).then_inc(s_dec, 1)

        @block.vector
        def _(dve):
            norm.on_vector(dve)
            dve.wait_ge(s_b, 16 * 7)
            dve.wait_ge(s_a, 1)
            dve.tensor_tensor(la[:], banks[2][:, 0:NT * H].rearrange("p (t h) -> p t h", t=NT),
                              bA[:].unsqueeze(1).broadcast_to([P, NT, H]), ALU.add).then_inc(s_la, 1)
            dve.wait_ge(s_c, 2)
            dve.tensor_copy(cum[:], banks[3][:, 0:NT * H].rearrange("p (t h) -> p t h", t=NT)).then_inc(s_cum, 1)
            for n in range(2):
                dve.tensor_copy(cumT[:, 512 * n:512 * n + 512], banks[4 + n][0:H, :]).then_inc(s_cumT, 1)
            for t in range(NT):
                dve.wait_ge(s_x, t + 1)
                if t >= 2:
                    dve.wait_ge(s_xn, t - 1)
                dve.tensor_tensor(xb[:, t % 2, :], banks[6 + t % 2][:], bX[:], ALU.add).then_inc(s_xb, 1)
            for n in range(2 * KD):
                dve.wait_ge(s_g, n + 1)
                dve.tensor_scalar(gT[:, n // 2, 512 * (n % 2):512 * (n % 2) + 512], banks[n % 2][:],
                                  bG[:, n // 2:n // 2 + 1], None, ALU.add).then_inc(s_gT, 1)
            for t in range(NT):
                dve.tensor_tensor(x[:, t, :], x[:, t, :], bO[:], ALU.add).then_inc(s_xo, 1)

            def gated(n):
                t, g = units[n]
                dve.wait_ge(s_y, n + 1)
                dve.tensor_tensor(yg[:, g, t * P:(t + 1) * P], banks[6 + n % 2][:, 0:P],
                                  gT[:, g, t * P:(t + 1) * P], ALU.mult).then_inc(s_yg, 1)

            def mixed(n):
                dve.wait_ge(s_mask, n + 1)
                dve.wait_ge(s_r, 2 * (n + 1))
                if n >= 2:
                    dve.wait_ge(s_y, n - 1)
                for r in range(2):
                    last = dve.tensor_tensor(mix[:, n % 2, r::2, :], diff[:, n % 2, r::2, :],
                                             banks[2 + 2 * (n % 2) + r][:, 0:2 * P].rearrange("p (a i) -> p a i", a=2),
                                             ALU.mult)
                last.then_inc(s_mix, 1)

            for n, (t, g) in enumerate(units):
                dve.wait_ge(s_r, 2 * n + 1)
                if n >= 2:
                    dve.wait_ge(s_mix, n - 1)
                for a in range(4):
                    h = 4 * g + a
                    dve.scalar_tensor_tensor(diff[:, n % 2, a, :], banks[n % 2][:, P * a:P * a + P],
                                             cum[:, t, h:h + 1], tri[:], ALU.subtract, ALU.mult).then_inc(s_diff, 1)
                if n >= 1:
                    mixed(n - 1)
                if n >= 3:
                    gated(n - 3)
            mixed(len(units) - 1)
            for n in range(len(units) - 3, len(units)):
                gated(n)
            for t in range(NT):
                dve.wait_ge(s_xo, NT)
                dve.wait_ge(s_o, t + 1)
                dve.tensor_tensor(x[:, t, :], x[:, t, :], banks[6 + t % 2][:], ALU.add).then_inc(s_out, 1)



class Split:

    WIDTH = 2048

    def __init__(self, k, ctx, name, pieces):
        self.nc, self.pieces = k.nc, pieces
        self.stage = k.sb(ctx, name + "_stage", [P, 2, self.WIDTH])
        self.s_in = [k.sem(ctx, f"{name}_in{n}") for n in range(2)]
        self.s_hi = k.sem(ctx, name + "_hi_done")
        self.s_lo = k.sem(ctx, name + "_lo_done")

    def view(self, n):
        a, b = self.pieces[n][0].shape[1:]
        return self.stage[:, n % 2, 0:a * b].rearrange("p (a b) -> p a b", a=a)

    def on_sync(self, sp):
        for n, (src, _, _) in enumerate(self.pieces):
            if n >= 2:
                sp.wait_ge(self.s_lo, n - 1)
            sp.dma_start(self.view(n), src).then_inc(self.s_in[n % 2], 16)

    def high_on_scalar(self, act, which):
        for n in which:
            act.wait_ge(self.s_in[n % 2], 16 * (n // 2 + 1))
            self.nc.scalar.copy(self.pieces[n][1], self.view(n)).then_inc(self.s_hi, 1)

    def low_on_gpsimd(self, pool):
        for n, (_, hi, lo) in enumerate(self.pieces):
            pool.wait_ge(self.s_hi, n + 1)
            pool.tensor_tensor(lo, self.view(n), hi, ALU.subtract).then_inc(self.s_lo, 1)


TERMS = ((0, 0), (1, 0), (0, 1))



NB, BW = 16, 128
TOPK = NB // 4


def block_ffn(k, ident, x):
    nc, d = k.nc, k.d
    F = NB * BW
    with ExitStack() as ctx:
        h = k.sb(ctx, "f_h", [P, 2, NB, TOK], BF16)
        early = h[:, 0].rearrange("p a n -> p (a n)").bitcast(F32)
        xhat = early[:, 0:NT * D].rearrange("p (t n) -> p t n", t=NT)
        xT = early[:, NT * D:2 * NT * D].rearrange("p (j n) -> p j n", j=KD)
        xs = k.sb(ctx, "f_x_split", [P, 2, KD, TOK], BF16)
        w1 = k.sb(ctx, "f_w1", [P, 2, KD, F], BF16)
        w2 = k.sb(ctx, "f_w2", [P, 2, NB, D], BF16)
        rw = k.sb(ctx, "f_router", [P, KD, NB])
        rb = k.sb(ctx, "f_router_b", [P, NB])
        b1 = k.sb(ctx, "f_b1", [P, NB])
        b2 = k.sb(ctx, "f_b2", [P, D])
        logit = k.sb(ctx, "f_logit", [P, NT, NB])
        stat = k.sb(ctx, "f_stat", [P, 3, NT])
        prob = k.sb(ctx, "f_prob", [P, NT, NB])
        beats = k.sb(ctx, "f_beats", [P, 2, NB, NB])
        lower = k.sb(ctx, "f_lower", [P, NB, NB])
        rank = k.sb(ctx, "f_rank", [P, NT, NB])
        mask = k.sb(ctx, "f_mask", [P, NT, NB])
        maskT = k.sb(ctx, "f_maskT", [NB, TOK], BF16)
        sel = k.sb(ctx, "f_sel", [NB, NB, P], BF16)
        act_out = k.sb(ctx, "f_relu", [P, 2, 512])
        masked = k.sb(ctx, "f_masked", [P, 2, 512])
        banks = [k.ps(ctx, f"f_bank{n}", [P, 512]) for n in range(8)]
        pieces = [(d["L0_ffn_w1"].rearrange("(j p) n -> p j n", p=P)[:, j:j + 1, :], w1[:, 0, j:j + 1, :],
                   w1[:, 1, j:j + 1, :]) for j in range(KD)]
        pieces += [(d["L0_ffn_w2"].rearrange("(j p) n -> p j n", p=P)[:, j:j + 4, :], w2[:, 0, j:j + 4, :],
                    w2[:, 1, j:j + 4, :]) for j in range(0, NB, 4)]
        split = Split(k, ctx, "f_split", pieces)
        s_in = k.sem(ctx, "f_in")
        s_set = k.sem(ctx, "f_set")
        s_sel = k.sem(ctx, "f_sel_done")
        s_r = k.sem(ctx, "f_router_full")
        s_v = k.sem(ctx, "f_route_step")
        s_e = k.sem(ctx, "f_exp_done")
        s_mt = k.sem(ctx, "f_maskT_full")
        s_mtc = k.sem(ctx, "f_maskT_done")
        s_h = k.sem(ctx, "f_h_full")
        s_relu = k.sem(ctx, "f_relu_done")
        s_masked = k.sem(ctx, "f_masked_done")
        s_hhi = k.sem(ctx, "f_h_hi_done")
        s_hlo = k.sem(ctx, "f_h_lo_done")
        s_y = k.sem(ctx, "f_y_full")
        s_xo = k.sem(ctx, "f_x_bias")
        s_out = k.sem(ctx, "f_out")
        norm = Norm(k, ctx, "f", x, ident, banks[0:2], xT, xhat=xhat, split=(xs[:, 0], xs[:, 1]))
        block = ctx.enter_context(nc.Block())
        groups = [(blk, c) for blk in range(NB) for c in range(2)]

        @block.sync
        def _(sp):
            sp.dma_start(rw[:], d["L0_ffn_router_w"].rearrange("(j p) n -> p j n", p=P)).then_inc(s_in, 16)
            sp.dma_start(rb[:], d["L0_ffn_router_b"].partition_broadcast(P)).then_inc(s_in, 16)
            sp.dma_start(b1[:], d["L0_ffn_b1"]).then_inc(s_in, 16)
            sp.dma_start(b2[:], d["L0_ffn_b2"].partition_broadcast(P)).then_inc(s_in, 16)
            split.on_sync(sp)
            sp.wait_ge(s_in, 64)

        @block.gpsimd
        def _(pool):
            pool.memset(sel[:], 0.0).then_inc(s_set, 1)
            pool.memset(lower[:], 1.0).then_inc(s_set, 1)
            pool.wait_ge(s_set, 2)
            pool.affine_select(out=sel[:], in_=sel[:], compare_op=ALU.not_equal, fill=1.0, base=0,
                               pattern=[[-1, NB], [0, P]], channel_multiplier=1).then_inc(s_sel, 1)
            pool.affine_select(out=lower[:], in_=lower[:], compare_op=ALU.is_ge, fill=0.0, base=-1,
                               pattern=[[1, NB], [-1, NB]], channel_multiplier=0).then_inc(s_sel, 1)
            split.low_on_gpsimd(pool)
            for n, (blk, c) in enumerate(groups):
                pool.wait_ge(s_hhi, n + 1)
                pool.tensor_tensor(h[:, 1, blk, 512 * c:512 * c + 512], masked[:, n % 2, :],
                                   h[:, 0, blk, 512 * c:512 * c + 512], ALU.subtract).then_inc(s_hlo, 1)

        @block.tensor
        def _(pe):
            norm.on_tensor(pe)
            pe.wait_ge(s_in, 64)
            for t in range(NT):
                pe.wait_ge(norm.s_xT, t + 1)
                for j in range(KD):
                    last = pe.matmul(banks[2][:, NB * t:NB * t + NB], xT[:, j, t * P:(t + 1) * P], rw[:, j, :],
                                     start=(j == 0), stop=(j == KD - 1))
            last.then_inc(s_r, 1)

            def hidden(n):
                blk, c = groups[n]
                if n >= 3:
                    pe.wait_ge(s_relu, n - 2)
                for i, (hw, hx) in enumerate(TERMS):
                    for j in range(KD):
                        last = pe.matmul(banks[3 + n % 3][:], w1[:, hw, j, blk * BW:(blk + 1) * BW],
                                         xs[:, hx, j, 512 * c:512 * c + 512],
                                         start=(i == 0 and j == 0), stop=(i == 2 and j == KD - 1))
                last.then_inc(s_h, 1)

            def masks(n):
                blk, c = groups[n]
                if n >= 2:
                    pe.wait_ge(s_masked, n - 1)
                pe.matmul(banks[6 + n % 2][:], sel[:, blk, :], maskT[:, 512 * c:512 * c + 512],
                          start=True, stop=True).then_inc(s_mt, 1)

            pe.wait_ge(split.s_lo, KD)
            pe.wait_ge(norm.s_low, NT)
            for n in range(3):
                hidden(n)
            pe.wait_ge(s_v, 6 + 6 * NT)
            for t in range(NT):
                last = pe.transpose(banks[t // 4][0:NB, P * (t % 4):P * (t % 4) + P], mask[:, t, :], ident[:])
            last.then_inc(s_mt, 1)
            pe.wait_ge(s_sel, 2)
            pe.wait_ge(s_mtc, 2)
            for n in range(3):
                if n < 2:
                    masks(n)
            for n in range(3, len(groups)):
                masks(n - 1)
                hidden(n)
            masks(len(groups) - 1)
            pe.wait_ge(split.s_lo, KD + 4)
            pe.wait_ge(s_hlo, len(groups))
            for t in range(NT):
                if t >= 2:
                    pe.wait_ge(s_out, t - 1)
                for i, (hh, hw) in enumerate(TERMS):
                    for j in range(NB):
                        last = pe.matmul(banks[t % 2][:], h[:, hh, j, t * P:(t + 1) * P], w2[:, hw, j, :],
                                         start=(i == 0 and j == 0), stop=(i == 2 and j == NB - 1))
                last.then_inc(s_y, 1)

        @block.scalar
        def _(act):
            def high(n):
                blk, c = groups[n]
                act.wait_ge(s_masked, n + 1)
                nc.scalar.copy(h[:, 0, blk, 512 * c:512 * c + 512], masked[:, n % 2, :]).then_inc(s_hhi, 1)

            norm.on_scalar(nc, act)
            split.high_on_scalar(act, range(0, 2))
            act.wait_ge(s_v, 3)
            nc.scalar.activation(prob[:], logit[:], ACT.Exp).then_inc(s_e, 1)
            split.high_on_scalar(act, range(2, KD + 4))
            act.wait_ge(s_in, 64)
            for n, (blk, c) in enumerate(groups):
                act.wait_ge(s_h, n + 1)
                if n >= 2:
                    act.wait_ge(s_masked, n - 1)
                nc.scalar.activation(act_out[:, n % 2, :], banks[3 + n % 3][:], ACT.Relu,
                                     bias=b1[:, blk:blk + 1]).then_inc(s_relu, 1)
                if n >= 1:
                    high(n - 1)
            high(len(groups) - 1)

        @block.vector
        def _(dve):
            norm.on_vector(dve)
            norm.low_on_vector(dve)
            dve.wait_ge(s_in, 64)
            dve.wait_ge(s_r, 1)
            dve.tensor_tensor(logit[:], banks[2][:, 0:NT * NB].rearrange("p (t n) -> p t n", t=NT),
                              rb[:].unsqueeze(1).broadcast_to([P, NT, NB]), ALU.add).then_inc(s_v, 1)
            dve.wait_ge(s_v, 1)
            dve.tensor_reduce(stat[:, 0, :], logit[:], AX, ALU.max).then_inc(s_v, 1)
            dve.wait_ge(s_v, 2)
            dve.tensor_tensor(logit[:], logit[:], stat[:, 0, :].unsqueeze(2).broadcast_to([P, NT, NB]),
                              ALU.subtract).then_inc(s_v, 1)
            dve.wait_ge(s_e, 1)
            dve.tensor_reduce(stat[:, 1, :], prob[:], AX, ALU.add).then_inc(s_v, 1)
            dve.wait_ge(s_v, 4)
            dve.reciprocal(stat[:, 2, :], stat[:, 1, :]).then_inc(s_v, 1)
            dve.wait_ge(s_v, 5)
            dve.tensor_tensor(prob[:], prob[:], stat[:, 2, :].unsqueeze(2).broadcast_to([P, NT, NB]),
                              ALU.mult).then_inc(s_v, 1)
            dve.wait_ge(s_v, 6)
            dve.wait_ge(s_sel, 2)
            for t in range(NT):
                pj = prob[:, t, :].unsqueeze(1).broadcast_to([P, NB, NB])
                pi = prob[:, t, :].unsqueeze(2).broadcast_to([P, NB, NB])
                if t:
                    dve.wait_ge(s_v, 6 + 6 * t)
                dve.tensor_tensor(beats[:, 0], pj, pi, ALU.is_gt).then_inc(s_v, 1)
                dve.tensor_tensor(beats[:, 1], pj, pi, ALU.is_equal).then_inc(s_v, 1)
                dve.wait_ge(s_v, 6 + 6 * t + 2)
                dve.tensor_tensor(beats[:, 1], beats[:, 1], lower[:], ALU.mult).then_inc(s_v, 1)
                dve.wait_ge(s_v, 6 + 6 * t + 3)
                dve.tensor_tensor(beats[:, 0], beats[:, 0], beats[:, 1], ALU.add).then_inc(s_v, 1)
                dve.wait_ge(s_v, 6 + 6 * t + 4)
                dve.tensor_reduce(rank[:, t, :], beats[:, 0], AX, ALU.add).then_inc(s_v, 1)
                dve.wait_ge(s_v, 6 + 6 * t + 5)
                dve.tensor_scalar(mask[:, t, :], rank[:, t, :], float(TOPK), None, ALU.is_lt).then_inc(s_v, 1)
            dve.wait_ge(s_mt, 1)
            for n in range(2):
                dve.tensor_copy(maskT[:, 512 * n:512 * n + 512], banks[n][0:NB, :]).then_inc(s_mtc, 1)
            for t in range(NT):
                dve.tensor_tensor(x[:, t, :], x[:, t, :], b2[:], ALU.add).then_inc(s_xo, 1)
            for n, (blk, c) in enumerate(groups):
                dve.wait_ge(s_relu, n + 1)
                dve.wait_ge(s_mt, n + 2)
                if n >= 2:
                    dve.wait_ge(s_hlo, n - 1)
                dve.tensor_tensor(masked[:, n % 2, :], act_out[:, n % 2, :], banks[6 + n % 2][:],
                                  ALU.mult).then_inc(s_masked, 1)
            dve.wait_ge(s_xo, NT)
            for t in range(NT):
                dve.wait_ge(s_y, t + 1)
                dve.tensor_tensor(x[:, t, :], x[:, t, :], banks[t % 2][:], ALU.add).then_inc(s_out, 1)



def cross1(k, ident, x):
    nc, d = k.nc, k.d
    with ExitStack() as ctx:
        qk = k.sb(ctx, "y_qk", [P, NT, KC, P])
        cq = k.sb(ctx, "y_cq", [P, NT])
        cross1_queries(k, ident, x, qk, cq)
        cross1_batches(k, ident, x, qk, cq)


def cross1_queries(k, ident, x, qk, cq):
    nc, d = k.nc, k.d
    with ExitStack() as ctx:
        xT = k.sb(ctx, "yq_xT", [P, KD, TOK])
        qT = k.sb(ctx, "yq_qT", [P, KD, TOK])
        wq = k.sb(ctx, "yq_wq", [P, KD, D])
        wkT = k.sb(ctx, "yq_wkT", [P, KD, CD])
        bq = k.sb(ctx, "yq_bq", [P, KD])
        bk = k.sb(ctx, "yq_bk", [P, KD])
        bv = k.sb(ctx, "yq_bv", [P, D])
        banks = [k.ps(ctx, f"yq_bank{n}", [P, 512]) for n in range(5)]
        s_in = k.sem(ctx, "yq_in")
        s_q = k.sem(ctx, "yq_q_full")
        s_qT = k.sem(ctx, "yq_qT_done")
        s_k = k.sem(ctx, "yq_qk_full")
        s_qk = k.sem(ctx, "yq_qk_done")
        s_c = k.sem(ctx, "yq_cq_full")
        s_x = k.sem(ctx, "yq_x_done")
        norm = Norm(k, ctx, "yq", x, ident, banks[0:2], xT)
        block = ctx.enter_context(nc.Block())
        groups = [(m, c) for c in range(2) for m in range(KD)]
        kgroups = [(m, c) for c in range(2) for m in range(KC)]

        @block.sync
        def _(sp):
            sp.dma_start(wq[:], d["L1_xattn_Wq"].rearrange("(j p) n -> p j n", p=P)).then_inc(s_in, 16)
            sp.dma_start(wkT[:], d["L1_xattn_WkT"].rearrange("(j p) n -> p j n", p=P)).then_inc(s_in, 16)
            sp.dma_start(bq[:], d["L1_xattn_bq"]).then_inc(s_in, 16)
            sp.dma_start(bk[:], d["L1_xattn_bk"]).then_inc(s_in, 16)
            sp.dma_start(bv[:], d["L1_xattn_bv"].partition_broadcast(P)).then_inc(s_in, 16)
            sp.wait_ge(s_in, 80)

        @block.tensor
        def _(pe):
            norm.on_tensor(pe)
            pe.wait_ge(s_in, 80)
            pe.wait_ge(norm.s_xT, NT)
            for n, (m, c) in enumerate(groups):
                if n >= 2:
                    pe.wait_ge(s_qT, n - 1)
                for j in range(KD):
                    last = pe.matmul(banks[2 + n % 2][:], wq[:, j, m * P:(m + 1) * P],
                                     xT[:, j, 512 * c:512 * c + 512], start=(j == 0), stop=(j == KD - 1))
                last.then_inc(s_q, 1)
            pe.wait_ge(s_qT, 2 * KD)
            for n, (m, c) in enumerate(kgroups):
                if n >= 2:
                    pe.wait_ge(s_qk, n - 1)
                for j in range(KD):
                    last = pe.matmul(banks[n % 2][:], wkT[:, j, m * P:(m + 1) * P],
                                     qT[:, j, 512 * c:512 * c + 512], start=(j == 0), stop=(j == KD - 1))
                last.then_inc(s_k, 1)
            for t in range(NT):
                for j in range(KD):
                    last = pe.matmul(banks[4][:, t:t + 1], qT[:, j, t * P:(t + 1) * P], bk[:, j:j + 1],
                                     start=(j == 0), stop=(j == KD - 1))
            last.then_inc(s_c, 1)

        @block.scalar
        def _(act):
            norm.on_scalar(nc, act)

        @block.vector
        def _(dve):
            norm.on_vector(dve)
            dve.wait_ge(s_in, 80)
            for t in range(NT):
                dve.tensor_tensor(x[:, t, :], x[:, t, :], bv[:], ALU.add).then_inc(s_x, 1)
            for n, (m, c) in enumerate(groups):
                dve.wait_ge(s_q, n + 1)
                dve.tensor_scalar(qT[:, m, 512 * c:512 * c + 512], banks[2 + n % 2][:], bq[:, m:m + 1], None,
                                  ALU.add).then_inc(s_qT, 1)
            for n, (m, c) in enumerate(kgroups):
                dve.wait_ge(s_k, n + 1)
                dve.tensor_copy(qk[:, 4 * c:4 * c + 4, m, :],
                                banks[n % 2][:].rearrange("p (t q) -> p t q", q=P)).then_inc(s_qk, 1)
            dve.wait_ge(s_c, 1)
            dve.tensor_copy(cq[:], banks[4][:, 0:NT]).then_inc(s_x, 1)


def cross1_batches(k, ident, x, qk, cq):
    nc, d = k.nc, k.d
    NKT = len(KTILES)
    FULL = NK // P
    with ExitStack() as ctx:
        cT = k.sb(ctx, "y_ctxT", [P, 2, 2, KC, NK])
        cn = k.sb(ctx, "y_ctx", [P, 2, 2, NKT, CD])
        qs = k.sb(ctx, "y_qs", [P, 2, KC, P])
        cqs = k.sb(ctx, "y_cqs", [P, 2])
        prob = k.sb(ctx, "y_prob", [P, 2, NK])
        pT = k.sb(ctx, "y_pT", [P, NTG, 512])
        o = k.sb(ctx, "y_o", [P, CD])
        oT = k.sb(ctx, "y_oT", [P, KC * P])
        wv = k.sb(ctx, "y_wv", [P, KC, D])
        stat = k.sb(ctx, "y_stat", [P, 2, 4])
        rinv = k.sb(ctx, "y_rinv", [P, 1])
        score = k.ps(ctx, "y_score", [P, 2048])
        tb = [k.ps(ctx, f"y_turn{n}", [P, 512]) for n in range(2)]
        pv = k.ps(ctx, "y_pv", [P, 512])
        wb = k.ps(ctx, "y_wout", [P, 512])
        s_w = k.sem(ctx, "y_w_in")
        cT_in = [k.sem(ctx, f"y_ctxT_in{n}") for n in range(2)]
        cn_in = [k.sem(ctx, f"y_ctx_in{n}") for n in range(2)]
        qs_in = [k.sem(ctx, f"y_qs_in{n}") for n in range(2)]
        cqs_in = [k.sem(ctx, f"y_cqs_in{n}") for n in range(2)]
        s_s = k.sem(ctx, "y_scores_done")
        s_m = k.sem(ctx, "y_stat_step")
        s_e = k.sem(ctx, "y_exp_done")
        s_t = k.sem(ctx, "y_turn_full")
        s_tf = k.sem(ctx, "y_turn_free")
        s_pv = k.sem(ctx, "y_pv_full")
        s_inv = k.sem(ctx, "y_inv_done")
        s_o = k.sem(ctx, "y_o_done")
        s_wo = k.sem(ctx, "y_wout_full")
        s_x = k.sem(ctx, "y_x_done")
        block = ctx.enter_context(nc.Block())
        ctxT = d["ctxT"].rearrange("b (j p) n -> p b j n", p=P)
        ctxN = d["ctx"].rearrange("b n c -> n b c")

        @block.sync
        def _(sp):
            def load(u, par, ready):
                one = isinstance(u, int)
                if ready is not None:
                    sp.wait_ge(s_s, ready)
                if one:
                    sp.dma_start(qs[:, par], qk[:, u]).then_inc(qs_in[par], 16)
                else:
                    sp.dma_start(qs[:, par], qk[:, bass.ds(u, 1)].rearrange("p a j q -> p (a j) q")).then_inc(qs_in[par], 16)
                for s in range(2):
                    src = ctxT[:, 2 * u + s] if one else \
                        ctxT[:, bass.ds(2 * u + s, 1)].rearrange("p a j n -> p (a j) n")
                    sp.dma_start(cT[:, par, s], src).then_inc(cT_in[par], 16)
                if ready is not None:
                    sp.wait_ge(s_pv, ready)
                sp.dma_start(cqs[:, par:par + 1], cq[:, u:u + 1] if one else cq[:, bass.ds(u, 1)]).then_inc(cqs_in[par], 16)
                for s in range(2):
                    src = ctxN[:, 2 * u + s] if one else \
                        ctxN[:, bass.ds(2 * u + s, 1)].rearrange("n a c -> n (a c)")
                    sp.dma_start(cn[:, par, s, 0:FULL, :],
                                 src[0:FULL * P, :].rearrange("(t p) c -> p t c", p=P)).then_inc(cn_in[par], 16)
                    sp.dma_start(cn[0:NK - FULL * P, par, s, FULL, :], src[FULL * P:NK, :]).then_inc(cn_in[par], 16)

            sp.dma_start(wv[:], d["L1_xattn_Wv"].rearrange("(j p) n -> p j n", p=P)).then_inc(s_w, 16)
            load(0, 0, None)
            load(1, 1, None)
            with sp.Fori(0, (NT - 2) // 2) as i:
                for a in range(2):
                    load(2 * i + 2 + a, a, 2 * i + 1 + a)
            sp.wait_ge(s_w, 16)

        def each_tile(eng, do):
            do(0, 0, True, False)
            do(1, 1, True, True)
            with eng.Fori(0, (NT - 2) // 2) as i:
                for a in range(2):
                    do(2 * i + 2 + a, a, True, True)
            do(NT, NT % 2, False, True)

        @block.tensor
        def _(pe):
            def tile(u, par, scores, products):
                if scores:
                    n_in = 32 * (u // 2 + 1) if isinstance(u, int) else 16 * (u + (1 if par else 2))
                    n_q = 16 * (u // 2 + 1) if isinstance(u, int) else 8 * (u + (1 if par else 2))
                    pe.wait_ge(qs_in[par], n_q)
                    pe.wait_ge(cT_in[par], n_in)
                    if products:
                        pe.wait_ge(s_e, u)
                    for c, (n0, w) in enumerate(CHUNKS):
                        for s in range(2):
                            for j in range(KC):
                                last = pe.matmul(score[L * s:L * s + L, 512 * c:512 * c + w],
                                                 qs[:, par, j, L * s:L * s + L], cT[:, par, s, j, n0:n0 + w],
                                                 start=(j == 0), stop=(j == KC - 1))
                    last.then_inc(s_s, 1)
                if products:
                    other = 1 - par
                    n_in = 64 * ((u - 1) // 2 + 1) if isinstance(u, int) else 32 * (u + (1 if par else 0))
                    pe.wait_ge(s_e, u)
                    pe.wait_ge(cn_in[other], n_in)
                    pe.wait_ge(s_w, 16)

                    def turn(j):
                        t = (other + j) % 2
                        if j >= 2 or not (isinstance(u, int) and u == 1):
                            pe.wait_ge(s_tf, 5 * (u - 1) + j - 1)
                        for i, (k0, kw) in enumerate(TGROUPS[j]):
                            last = pe.transpose(tb[t][0:kw, P * i:P * i + P], prob[:, other, k0:k0 + kw], ident[:])
                        last.then_inc(s_t, 1)

                    def product(j):
                        pe.wait_ge(s_tf, 5 * (u - 1) + j + 1)
                        for i, (k0, kw) in enumerate(TGROUPS[j]):
                            for s in range(2):
                                last = pe.matmul(pv[L * s:L * s + L, 0:CD], pT[0:kw, j, P * i + L * s:P * i + L * s + L],
                                                 cn[0:kw, other, s, 4 * j + i, :],
                                                 start=(j == 0 and i == 0), stop=(j == NTG - 1))
                        return last

                    turn(0)
                    turn(1)
                    if not (isinstance(u, int) and u == 1):
                        pe.wait_ge(s_o, u - 1)
                    product(0)
                    turn(2)
                    product(1)
                    turn(3)
                    product(2)
                    product(3).then_inc(s_pv, 1)
                    pe.wait_ge(s_o, u)
                    pe.wait_ge(s_tf, 5 * (u - 1) + 3)
                    for j in range(KC):
                        last = pe.transpose(tb[other][:, P * j:P * j + P], o[:, P * j:P * j + P], ident[:])
                    last.then_inc(s_t, 1)
                    pe.wait_ge(s_tf, 5 * u)
                    if not (isinstance(u, int) and u == 1):
                        pe.wait_ge(s_x, u - 1)
                    for j in range(KC):
                        last = pe.matmul(wb[:], oT[:, P * j:P * j + P], wv[:, j, :], start=(j == 0), stop=(j == KC - 1))
                    last.then_inc(s_wo, 1)

            each_tile(pe, tile)

        @block.scalar
        def _(act):
            def tile(u, par, scores, products):
                if scores:
                    act.wait_ge(s_m, 3 * u + 3)
                    nc.scalar.activation(prob[:, par, :], score[:, 0:NK], ACT.Exp, bias=stat[:, par, 2:3],
                                         accum_out=stat[:, par, 3:4]).then_inc(s_e, 1)
                if products:
                    other = 1 - par
                    for j in range(NTG):
                        t = (other + j) % 2
                        n, kw = P * len(TGROUPS[j]), TGROUPS[j][0][1]
                        act.wait_ge(s_t, 5 * (u - 1) + j + 1)
                        nc.scalar.copy(pT[0:kw, j, 0:n], tb[t][0:kw, 0:n]).then_inc(s_tf, 1)
                    act.wait_ge(s_t, 5 * u)
                    nc.scalar.copy(oT[:], tb[other][:, 0:KC * P]).then_inc(s_tf, 1)

            each_tile(act, tile)

        @block.vector
        def _(dve):
            def tile(u, par, scores, products):
                if scores:
                    dve.wait_ge(s_s, u + 1)
                    dve.tensor_reduce(stat[:, par, 0:1], score[:, 0:NK], AX, ALU.max).then_inc(s_m, 1)
                    dve.wait_ge(s_m, 3 * u + 1)
                    n_q = 16 * (u // 2 + 1) if isinstance(u, int) else 8 * (u + (1 if par else 2))
                    dve.wait_ge(cqs_in[par], n_q)
                    dve.tensor_tensor(stat[:, par, 1:2], stat[:, par, 0:1], cqs[:, par:par + 1],
                                      ALU.add).then_inc(s_m, 1)
                    dve.wait_ge(s_m, 3 * u + 2)
                    dve.tensor_tensor(stat[:, par, 2:3], cqs[:, par:par + 1], stat[:, par, 1:2],
                                      ALU.subtract).then_inc(s_m, 1)
                if products:
                    other = 1 - par
                    dve.wait_ge(s_e, u)
                    dve.reciprocal(rinv[:], stat[:, other, 3:4]).then_inc(s_inv, 1)
                    dve.wait_ge(s_inv, u)
                    dve.wait_ge(s_pv, u)
                    dve.tensor_scalar(o[:], pv[:, 0:CD], rinv[:], None, ALU.mult).then_inc(s_o, 1)
                    dve.wait_ge(s_wo, u)
                    if isinstance(u, int):
                        xt = x[:, u - 1, :]
                    else:
                        xt = x[:, bass.ds(u - 1, 1), :].rearrange("p a n -> p (a n)")
                    dve.tensor_tensor(xt, xt, wb[:], ALU.add).then_inc(s_x, 1)

            each_tile(dve, tile)



DQ = 64


def self1(k, ident, low, x):
    nc, d = k.nc, k.d
    with ExitStack() as ctx:
        xT = k.sb(ctx, "s_xT", [P, KD, TOK])
        wq = k.sb(ctx, "s_wq", [P, 2, KD, DQ])
        wv = k.sb(ctx, "s_wv", [P, KD, D])
        qkT = k.sb(ctx, "s_qkT", [DQ, 2, TOK])
        v = k.sb(ctx, "s_v", [P, NT, D])
        sc = k.sb(ctx, "s_sc", [P, NT, P])
        prob = k.sb(ctx, "s_prob", [P, NT, P])
        pT = k.sb(ctx, "s_pT", [P, NT, P])
        stat = k.sb(ctx, "s_stat", [P, 4, NT])
        banks = [k.ps(ctx, f"s_bank{n}", [P, 512]) for n in range(8)]
        s_in = k.sem(ctx, "s_in")
        s_q = k.sem(ctx, "s_q_full")
        s_qc = k.sem(ctx, "s_q_done")
        s_v = k.sem(ctx, "s_v_full")
        s_vc = k.sem(ctx, "s_v_done")
        s_s = k.sem(ctx, "s_scores_full")
        s_sc = k.sem(ctx, "s_scores_done")
        s_m = k.sem(ctx, "s_max_done")
        s_b = k.sem(ctx, "s_shift_done")
        s_e = k.sem(ctx, "s_exp_done")
        s_t = k.sem(ctx, "s_turned")
        s_tc = k.sem(ctx, "s_turned_done")
        s_r = k.sem(ctx, "s_inv_done")
        s_o = k.sem(ctx, "s_o_full")
        s_x = k.sem(ctx, "s_x_done")
        norm = Norm(k, ctx, "sn", x, ident, banks[0:2], xT)
        block = ctx.enter_context(nc.Block())

        @block.sync
        def _(sp):
            for n, w in enumerate(("L1_attn_Wq", "L1_attn_Wk")):
                sp.dma_start(wq[:, n], d[w].rearrange("(j p) n -> p j n", p=P)).then_inc(s_in, 16)
            sp.dma_start(wv[:], d["L1_attn_Wv"].rearrange("(j p) n -> p j n", p=P)).then_inc(s_in, 16)
            sp.wait_ge(s_in, 48)

        @block.tensor
        def _(pe):
            norm.on_tensor(pe)
            pe.wait_ge(s_in, 48)
            pe.wait_ge(norm.s_xT, NT)
            for n in range(4):
                for j in range(KD):
                    last = pe.matmul(banks[2 + n][0:DQ, :], wq[:, n // 2, j, :],
                                     xT[:, j, 512 * (n % 2):512 * (n % 2) + 512], start=(j == 0), stop=(j == KD - 1))
                last.then_inc(s_q, 1)

            def values(t):
                if t >= 2:
                    pe.wait_ge(s_vc, t - 1)
                for j in range(KD):
                    last = pe.matmul(banks[t % 2][:], xT[:, j, t * P:(t + 1) * P], wv[:, j, :],
                                     start=(j == 0), stop=(j == KD - 1))
                last.then_inc(s_v, 1)

            for t in range(2):
                values(t)
            pe.wait_ge(s_qc, 4)
            for t in range(NT):
                tile = slice(t * P, (t + 1) * P)
                last = pe.matmul(banks[6 + t // 4][:, P * (t % 4):P * (t % 4) + P], qkT[:, 0, tile], qkT[:, 1, tile],
                                 start=True, stop=True)
            last.then_inc(s_s, 1)
            for t in range(2, NT):
                values(t)
            pe.wait_ge(s_sc, NT)
            for t in range(NT):
                pe.wait_ge(s_e, t + 1)
                last = pe.transpose(banks[6 + t // 4][:, P * (t % 4):P * (t % 4) + P], prob[:, t, :], ident[:])
                if t % 4 == 3:
                    last.then_inc(s_t, 1)
            pe.wait_ge(s_vc, NT)
            for t in range(NT):
                pe.wait_ge(s_tc, t // 4 + 1)
                if t >= 4:
                    pe.wait_ge(s_x, t - 3)
                pe.matmul(banks[2 + t % 4][:], pT[:, t, :], v[:, t, :], start=True, stop=True).then_inc(s_o, 1)

        @block.scalar
        def _(act):
            norm.on_scalar(nc, act)
            for t in range(NT):
                act.wait_ge(s_v, t + 1)
                nc.scalar.copy(v[:, t, :], banks[t % 2][:]).then_inc(s_vc, 1)
            act.wait_ge(s_b, 1)
            for t in range(NT):
                nc.scalar.activation(prob[:, t, :], sc[:, t, :], ACT.Exp, bias=stat[:, 1, t:t + 1],
                                     scale=float(DQ) ** -0.5, accum_out=stat[:, 2, t:t + 1]).then_inc(s_e, 1)

        @block.vector
        def _(dve):
            norm.on_vector(dve)
            for n in range(4):
                dve.wait_ge(s_q, n + 1)
                dve.tensor_copy(qkT[:, n // 2, 512 * (n % 2):512 * (n % 2) + 512], banks[2 + n][0:DQ, :]).then_inc(s_qc, 1)
            dve.wait_ge(s_s, 1)
            for t in range(NT):
                dve.tensor_tensor(sc[:, t, :], banks[6 + t // 4][:, P * (t % 4):P * (t % 4) + P], low[:],
                                  ALU.add).then_inc(s_sc, 1)
            dve.wait_ge(s_sc, NT)
            dve.tensor_reduce(stat[:, 0, :], sc[:], AX, ALU.max).then_inc(s_m, 1)
            dve.wait_ge(s_m, 1)
            dve.tensor_scalar(stat[:, 1, :], stat[:, 0, :], -float(DQ) ** -0.5, None, ALU.mult).then_inc(s_b, 1)
            for n in range(2):
                dve.wait_ge(s_t, n + 1)
                dve.tensor_copy(pT[:, 4 * n:4 * n + 4, :],
                                banks[6 + n][:].rearrange("p (t q) -> p t q", q=P)).then_inc(s_tc, 1)
            dve.wait_ge(s_e, NT)
            dve.reciprocal(stat[:, 3, :], stat[:, 2, :]).then_inc(s_r, 1)
            dve.wait_ge(s_r, 1)
            for t in range(NT):
                dve.wait_ge(s_o, t + 1)
                dve.scalar_tensor_tensor(x[:, t, :], banks[2 + t % 4][:], stat[:, 3, t:t + 1], x[:, t, :],
                                         ALU.mult, ALU.add).then_inc(s_x, 1)



NF = 1536
MF = NF // P
QB = 32
WCOLS = NF * D // P


class Dequant:

    def __init__(self, k, ctx, name, banks, ident):
        self.k, self.nc, self.banks, self.ident = k, k.nc, banks, ident
        self.w = k.sb(ctx, name + "_w", [P, 2, WCOLS])
        self.scale = k.sb(ctx, name + "_scale", [P, 3, WCOLS // QB])
        self.parts = k.sb(ctx, name + "_parts", [P, 2, 2, WCOLS], BF16)
        self.s_in = [k.sem(ctx, f"{name}_in{n}") for n in range(2)]
        self.s_max = k.sem(ctx, name + "_absmax")
        self.s_unit = k.sem(ctx, name + "_units")
        self.s_round = k.sem(ctx, name + "_rounded")
        self.s_back = k.sem(ctx, name + "_scaled")
        self.s_turn = k.sem(ctx, name + "_turned")
        self.s_hi = k.sem(ctx, name + "_high")
        self.s_lo = k.sem(ctx, name + "_low")
        self.s_out = [k.sem(ctx, f"{name}_out{n}") for n in range(2)]

    MATRICES = ("L1_ffn_w_up", "L1_ffn_w_gate", "L1_ffn_w_down")

    def turns(self, n):
        w = self.w[:, n % 2]
        if n < 2:
            w = w.rearrange("p (o j c) -> p o j c", o=MF, j=KD)
            return [([w[:, 4 * og + i, j, :] for i in range(4)], slice(j * NF + 512 * og, j * NF + 512 * og + 512))
                    for j in range(KD) for og in range(MF // 4)]
        w = w.rearrange("p (o j c) -> p o j c", o=KD, j=MF)
        return [([w[:, i, j, :] for i in range(4)], slice(512 * j, 512 * j + 512)) for j in range(MF)]

    def on_sync(self, sp):
        for n, name in enumerate(self.MATRICES):
            if n >= 2:
                sp.wait_ge(self.s_turn, MF * (n - 1))
            src = self.k.d[name].rearrange("(o p) c -> p o c", p=P)
            o = src.shape[1]
            sp.dma_start(self.w[:, n % 2].rearrange("p (o c) -> p o c", o=o), src).then_inc(self.s_in[n % 2], 16)
        for n, name in enumerate(self.MATRICES):
            sp.wait_ge(self.s_lo, MF * (n + 1))
            sp.dma_start(self.k.scratch[name], self.parts[:, n % 2]).then_inc(self.s_out[n % 2], 16)
        sp.wait_ge(self.s_out[0], 32)
        sp.wait_ge(self.s_out[1], 16)

    def on_vector(self, dve):
        for n in range(3):
            w = self.w[:, n % 2].rearrange("p (b i) -> p b i", i=QB)
            s, inv = self.scale[:, 0], self.scale[:, 1]
            wide = [P, WCOLS // QB, QB]
            dve.wait_ge(self.s_in[n % 2], 16 * (n // 2 + 1))
            if n:
                dve.wait_ge(self.s_back, n)
            dve.tensor_reduce(s, w, AX, ALU.max, apply_absolute_value=True).then_inc(self.s_max, 1)
            dve.wait_ge(self.s_max, n + 1)
            dve.tensor_scalar(s, s, 1.0 / 7.0, 1e-12, ALU.mult, ALU.max).then_inc(self.s_unit, 1)
            dve.wait_ge(self.s_unit, 4 * n + 1)
            dve.reciprocal(inv, s).then_inc(self.s_unit, 1)
            dve.wait_ge(self.s_unit, 4 * n + 2)
            dve.tensor_tensor(w, w, inv.unsqueeze(2).broadcast_to(wide), ALU.mult).then_inc(self.s_unit, 1)
            dve.wait_ge(self.s_unit, 4 * n + 3)
            dve.tensor_scalar(self.w[:, n % 2], self.w[:, n % 2], ROUND, None, ALU.add).then_inc(self.s_unit, 1)
            dve.wait_ge(self.s_unit, 4 * n + 4)
            dve.tensor_scalar(self.w[:, n % 2], self.w[:, n % 2], ROUND, 7.0, ALU.subtract, ALU.min).then_inc(self.s_round, 1)
            self.low(dve, n - 1)
        self.low(dve, 2)

    def low(self, dve, n):
        if n < 0:
            return
        for i, (_, dst) in enumerate(self.turns(n)):
            g = MF * n + i
            dve.wait_ge(self.s_hi, g + 1)
            dve.tensor_tensor(self.parts[:, n % 2, 1, dst], self.banks[g % 2][:], self.parts[:, n % 2, 0, dst],
                              ALU.subtract).then_inc(self.s_lo, 1)

    def on_gpsimd(self, pool):
        for n in range(3):
            w = self.w[:, n % 2].rearrange("p (b i) -> p b i", i=QB)
            pool.wait_ge(self.s_round, n + 1)
            pool.tensor_tensor(w, w, self.scale[:, 0].unsqueeze(2).broadcast_to([P, WCOLS // QB, QB]),
                               ALU.mult).then_inc(self.s_back, 1)

    def on_tensor(self, pe):
        for n in range(3):
            pe.wait_ge(self.s_back, n + 1)
            for i, (blocks, _) in enumerate(self.turns(n)):
                g = MF * n + i
                if g >= 2:
                    pe.wait_ge(self.s_lo, g - 1)
                for a, block in enumerate(blocks):
                    last = pe.transpose(self.banks[g % 2][:, P * a:P * a + P], block, self.ident[:])
                last.then_inc(self.s_turn, 1)

    def on_scalar(self, act):
        for n in range(3):
            if n == 2:
                act.wait_ge(self.s_out[0], 16)
            for i, (_, dst) in enumerate(self.turns(n)):
                g = MF * n + i
                act.wait_ge(self.s_turn, g + 1)
                self.nc.scalar.copy(self.parts[:, n % 2, 0, dst], self.banks[g % 2][:]).then_inc(self.s_hi, 1)


def dequant_phase(k, ident):
    nc = k.nc
    with ExitStack() as ctx:
        banks = [k.ps(ctx, f"w_bank{n}", [P, 512]) for n in range(2)]
        dq = Dequant(k, ctx, "w", banks, ident)
        block = ctx.enter_context(nc.Block())
        block.sync(dq.on_sync)
        block.vector(dq.on_vector)
        block.gpsimd(dq.on_gpsimd)
        block.tensor(dq.on_tensor)
        block.scalar(dq.on_scalar)


def quant_ffn(k, ident, x):
    nc, d = k.nc, k.d
    with ExitStack() as ctx:
        up = k.sb(ctx, "g_up", [P, MF, TOK])
        gate = k.sb(ctx, "g_gate", [P, MF, TOK])
        early = gate[:].rearrange("p m n -> p (m n)")
        xhat = early[:, 0:NT * D].rearrange("p (t n) -> p t n", t=NT)
        uT = early[:, NT * D:2 * NT * D].rearrange("p (j n) -> p j n", j=KD)
        xs = k.sb(ctx, "g_x_split", [P, 2, KD, TOK], BF16)
        tmp = xs[:, 0].rearrange("p j n -> p (j n)").bitcast(F32).rearrange("p (a n) -> p a n", a=2)
        wug = k.sb(ctx, "g_w", [P, 2, 2, WCOLS], BF16)
        osplit = wug[:].rearrange("p a b n -> p (a b n)").rearrange("p (h m n) -> p h m n", h=2, m=MF)
        wd = k.sb(ctx, "g_wd", [P, 2, MF, D], BF16)
        amax = k.sb(ctx, "g_amax", [P, 5, 2 * MF])
        peak = k.sb(ctx, "g_peak", [P, 5, 2])
        unit = k.sb(ctx, "g_unit", [P, 5, 3])
        big = k.sb(ctx, "g_round", [P, 1])
        banks = [k.ps(ctx, f"g_bank{n}", [P, 512]) for n in range(8)]
        s_w = [k.sem(ctx, f"g_w_in{n}") for n in range(3)]
        s_big = k.sem(ctx, "g_round_set")
        s_peak = k.sem(ctx, "g_peak")
        s_all = k.sem(ctx, "g_peak_all")
        s_unit = k.sem(ctx, "g_unit")
        s_xh = k.sem(ctx, "g_x_high")
        s_xl = k.sem(ctx, "g_x_low")
        s_ug = k.sem(ctx, "g_hidden_full")
        s_ugc = k.sem(ctx, "g_hidden_done")
        s_am = k.sem(ctx, "g_hidden_absmax")
        s_u1 = k.sem(ctx, "g_up_rounded")
        s_u2 = k.sem(ctx, "g_up_done")
        s_g1 = k.sem(ctx, "g_gate_rounded")
        s_g2 = k.sem(ctx, "g_gate_done")
        s_sg = k.sem(ctx, "g_sigmoid")
        s_sr = k.sem(ctx, "g_sigmoid_rounded")
        s_s2 = k.sem(ctx, "g_sigmoid_done")
        s_gs = k.sem(ctx, "g_product")
        s_am2 = k.sem(ctx, "g_product_absmax")
        s_h1 = k.sem(ctx, "g_silu_rounded")
        s_h2 = k.sem(ctx, "g_hidden_out")
        s_am3 = k.sem(ctx, "g_out_absmax")
        s_o1 = k.sem(ctx, "g_out_rounded")
        s_oh = k.sem(ctx, "g_out_high")
        s_ol = k.sem(ctx, "g_out_low")
        s_y = k.sem(ctx, "g_y_full")
        s_x = k.sem(ctx, "g_x_done")
        s_st = k.sem(ctx, "g_stored")
        norm = Norm(k, ctx, "g", x, ident, banks[0:2], None, xhat=xhat)
        block = ctx.enter_context(nc.Block())
        groups = [(w, m, c) for w in range(2) for m in range(MF) for c in range(2)]
        half = len(groups) // 2
        NB_G = 6

        @block.sync
        def _(sp):
            for n in range(2):
                sp.dma_start(wug[:, n], k.scratch[Dequant.MATRICES[n]]).then_inc(s_w[n], 16)
            sp.dma_start(wd[:].rearrange("p h m n -> p h (m n)"), k.scratch[Dequant.MATRICES[2]]).then_inc(s_w[2], 16)
            out = k.out.rearrange("(t p) n -> p t n", p=P)
            for t in range(NT):
                sp.wait_ge(s_x, t + 1)
                sp.dma_start(out[:, t, :], x[:, t, :]).then_inc(s_st, 16)
            sp.wait_ge(s_st, 16 * NT)

        @block.gpsimd
        def _(pool):
            pool.memset(big[:], ROUND).then_inc(s_big, 1)

            def spread(n):
                pool.wait_ge(s_peak, n + 1)
                pool.partition_all_reduce(peak[:, n, 1:2], peak[:, n, 0:1], P,
                                          bass.bass_isa.ReduceOp.max).then_inc(s_all, 1)

            for n in range(3):
                spread(n)
            for m in range(MF):
                pool.wait_ge(s_s2, m + 1)
                pool.tensor_tensor(gate[:, m, :], tmp[:, m % 2, :], gate[:, m, :], ALU.mult).then_inc(s_gs, 1)
            spread(3)
            spread(4)

        @block.tensor
        def _(pe):
            norm.on_tensor(pe)
            pe.wait_ge(s_xl, NT)
            for n, (w, m, c) in enumerate(groups):
                if m == 0 and c == 0:
                    pe.wait_ge(s_w[w], 16)
                if n >= NB_G:
                    pe.wait_ge(s_am, n - NB_G + 1)
                wt = wug[:, w].rearrange("p h (j n) -> p h j n", j=KD)
                for i, (hw, hx) in enumerate(TERMS):
                    for j in range(KD):
                        last = pe.matmul(banks[2 + n % NB_G][:], wt[:, hw, j, m * P:(m + 1) * P],
                                         xs[:, hx, j, 512 * c:512 * c + 512],
                                         start=(i == 0 and j == 0), stop=(i == 2 and j == KD - 1))
                last.then_inc(s_ug, 1)
            pe.wait_ge(s_w[2], 16)
            pe.wait_ge(s_am, len(groups))
            for m in range(MF):
                pe.wait_ge(s_ol, m + 1)
                for t in range(NT):
                    for i, (hh, hw) in enumerate(TERMS):
                        last = pe.matmul(banks[t][:], osplit[:, hh, m, t * P:(t + 1) * P], wd[:, hw, m, :],
                                         start=(m == 0 and i == 0), stop=(m == MF - 1 and i == 2))
                    if m == MF - 1:
                        last.then_inc(s_y, 1)

        @block.scalar
        def _(act):
            act.wait_ge(norm.s_var, 1)
            nc.scalar.activation(norm.small[:, 1, :], norm.small[:, 0, :], ACT.Sqrt).then_inc(norm.s_root, 1)
            act.wait_ge(s_big, 1)
            act.wait_ge(s_unit, 2)
            for t in range(NT):
                act.wait_ge(norm.s_turned, t + 1)
                nc.scalar.activation(uT[:, :, t * P:(t + 1) * P], banks[t % 2][:].rearrange("p (j n) -> p j n", j=KD),
                                     ACT.Identity, bias=big[:], scale=unit[:, 0, 1:2]).then_inc(norm.s_xT, 1)

            def hidden(n):
                w, m, c = groups[n]
                act.wait_ge(s_ug, n + 1)
                nc.scalar.mul((up, gate)[w][:, m, 512 * c:512 * c + 512], banks[2 + n % NB_G][:],
                              unit[:, 0, 0:1]).then_inc(s_ugc, 1)

            def rounded(dst, src, n, done):
                nc.scalar.activation(dst, src, ACT.Identity, bias=big[:], scale=unit[:, n, 1:2]).then_inc(done, 1)

            for n in range(half):
                hidden(n)
            for n in range(half, len(groups)):
                hidden(n)
                m = (n - half) // 2
                if n % 2:
                    if m == 0:
                        act.wait_ge(s_unit, 4)
                    rounded(up[:, m, :], up[:, m, :], 1, s_u1)
            act.wait_ge(s_unit, 6)
            for m in range(MF + 2):
                if m < MF:
                    rounded(gate[:, m, :], gate[:, m, :], 2, s_g1)
                if m >= 1 and m - 1 < MF:
                    act.wait_ge(s_g2, m)
                    if m >= 3:
                        act.wait_ge(s_gs, m - 2)
                    nc.scalar.activation(tmp[:, (m - 1) % 2, :], gate[:, m - 1, :], ACT.Sigmoid).then_inc(s_sg, 1)
            act.wait_ge(s_unit, 8)
            for m in range(MF):
                rounded(gate[:, m, :], gate[:, m, :], 3, s_h1)
            act.wait_ge(s_unit, 11)
            for m in range(MF):
                rounded(gate[:, m, :], gate[:, m, :], 4, s_o1)

        @block.vector
        def _(dve):
            def scale_of(n, a, count, factor):
                dve.tensor_reduce(peak[:, n, 0:1], a, AX, ALU.max).then_inc(s_peak, 1)
                dve.wait_ge(s_all, n + 1)
                dve.tensor_scalar(unit[:, n, 0:1], peak[:, n, 1:2], factor / QMAX, 1e-12, ALU.mult, ALU.max).then_inc(s_unit, 1)
                dve.wait_ge(s_unit, count)
                dve.reciprocal(unit[:, n, 1:2], unit[:, n, 0:1]).then_inc(s_unit, 1)

            norm.on_vector(dve)
            dve.wait_ge(norm.s_hat, NT)
            dve.tensor_reduce(amax[:, 0, 0:NT], xhat, AX, ALU.max, apply_absolute_value=True).then_inc(s_am2, 1)
            dve.wait_ge(s_am2, 1)
            scale_of(0, amax[:, 0, 0:NT], 1, 1.0)
            for t in range(NT):
                c = slice(t * P, (t + 1) * P)
                dve.wait_ge(norm.s_xT, t + 1)
                dve.tensor_scalar(xs[:, 0, :, c], uT[:, :, c], ROUND, None, ALU.subtract).then_inc(s_xh, 1)
                dve.wait_ge(s_xh, t + 1)
                dve.scalar_tensor_tensor(xs[:, 1, :, c], uT[:, :, c], ROUND, xs[:, 0, :, c], ALU.subtract,
                                         ALU.subtract).then_inc(s_xl, 1)

            def absmax(n):
                w, m, c = groups[n]
                dve.wait_ge(s_ugc, n + 1)
                dve.tensor_reduce(amax[:, 1 + w, 2 * m + c:2 * m + c + 1], (up, gate)[w][:, m, 512 * c:512 * c + 512],
                                  AX, ALU.max, apply_absolute_value=True).then_inc(s_am, 1)

            for n in range(half):
                absmax(n)
            dve.wait_ge(s_am, half)
            scale_of(1, amax[:, 1, :], 3, 1.0)
            for n in range(half, len(groups)):
                absmax(n)
                m = (n - half) // 2
                if n % 2:
                    dve.wait_ge(s_u1, m + 1)
                    dve.tensor_scalar(up[:, m, :], up[:, m, :], ROUND, unit[:, 1, 0:1], ALU.subtract,
                                      ALU.mult).then_inc(s_u2, 1)
            dve.wait_ge(s_am, len(groups))
            scale_of(2, amax[:, 2, :], 5, 1.0)
            for m in range(MF + 3):
                if m < MF:
                    dve.wait_ge(s_g1, m + 1)
                    dve.tensor_scalar(gate[:, m, :], gate[:, m, :], ROUND, unit[:, 2, 0:1], ALU.subtract,
                                      ALU.mult).then_inc(s_g2, 1)
                if 1 <= m <= MF:
                    i = m - 1
                    dve.wait_ge(s_sg, i + 1)
                    dve.tensor_scalar(tmp[:, i % 2, :], tmp[:, i % 2, :], 65536.0, ROUND, ALU.mult,
                                      ALU.add).then_inc(s_sr, 1)
                    dve.wait_ge(s_sr, i + 1)
                    dve.tensor_scalar(tmp[:, i % 2, :], tmp[:, i % 2, :], ROUND, 65535.0, ALU.subtract,
                                      ALU.min).then_inc(s_s2, 1)
                if m >= 3:
                    i = m - 3
                    dve.wait_ge(s_gs, i + 1)
                    dve.tensor_reduce(amax[:, 3, i:i + 1], gate[:, i, :], AX, ALU.max,
                                      apply_absolute_value=True).then_inc(s_am2, 1)
            dve.wait_ge(s_am2, 1 + MF)
            dve.tensor_reduce(peak[:, 3, 0:1], amax[:, 3, 0:MF], AX, ALU.max).then_inc(s_peak, 1)
            dve.wait_ge(s_all, 4)
            dve.tensor_scalar(unit[:, 3, 0:1], peak[:, 3, 1:2], 2.0 ** -16 / QMAX, 1e-12, ALU.mult,
                              ALU.max).then_inc(s_big, 1)
            dve.wait_ge(s_big, 2)
            dve.reciprocal(unit[:, 3, 2:3], unit[:, 3, 0:1]).then_inc(s_unit, 1)
            dve.wait_ge(s_unit, 7)
            dve.tensor_scalar(unit[:, 3, 1:2], unit[:, 3, 2:3], 2.0 ** -16, None, ALU.mult).then_inc(s_unit, 1)
            for m in range(MF):
                dve.wait_ge(s_h1, m + 1)
                dve.scalar_tensor_tensor(gate[:, m, :], gate[:, m, :], ROUND, up[:, m, :], ALU.subtract,
                                         ALU.mult).then_inc(s_h2, 1)
                dve.wait_ge(s_h2, m + 1)
                dve.tensor_reduce(amax[:, 4, m:m + 1], gate[:, m, :], AX, ALU.max,
                                  apply_absolute_value=True).then_inc(s_am3, 1)
            dve.wait_ge(s_am3, MF)
            dve.tensor_reduce(peak[:, 4, 0:1], amax[:, 4, 0:MF], AX, ALU.max).then_inc(s_peak, 1)
            dve.wait_ge(s_all, 5)
            dve.tensor_scalar(unit[:, 4, 2:3], peak[:, 4, 1:2], unit[:, 3, 0:1], 1.0 / QMAX, ALU.mult,
                              ALU.mult).then_inc(s_unit, 1)
            dve.wait_ge(s_unit, 9)
            dve.tensor_scalar(unit[:, 4, 0:1], unit[:, 4, 2:3], 1e-12, None, ALU.max).then_inc(s_unit, 1)
            dve.wait_ge(s_unit, 10)
            dve.reciprocal(unit[:, 4, 2:3], unit[:, 4, 0:1]).then_inc(s_big, 1)
            dve.wait_ge(s_big, 3)
            dve.tensor_tensor(unit[:, 4, 1:2], unit[:, 4, 2:3], unit[:, 3, 0:1], ALU.mult).then_inc(s_unit, 1)
            for m in range(MF):
                dve.wait_ge(s_o1, m + 1)
                dve.tensor_scalar(osplit[:, 0, m, :], gate[:, m, :], ROUND, None, ALU.subtract).then_inc(s_oh, 1)
                dve.wait_ge(s_oh, m + 1)
                dve.scalar_tensor_tensor(osplit[:, 1, m, :], gate[:, m, :], ROUND, osplit[:, 0, m, :],
                                         ALU.subtract, ALU.subtract).then_inc(s_ol, 1)
            for t in range(NT):
                dve.wait_ge(s_y, t + 1)
                dve.scalar_tensor_tensor(x[:, t, :], banks[t][:], unit[:, 4, 0:1], x[:, t, :], ALU.mult,
                                         ALU.add).then_inc(s_x, 1)


def cross0(k, ident, x):
    d = k.d
    with ExitStack() as c0:
        catT = k.sb(c0, "catT", [P, 2, 2, TOK])
        bvT = k.sb(c0, "bvT", [P, 4])
        qT = k.sb(c0, "qT", [P, B, 2, KD, L], BF16)
        wk = k.sb(c0, "wk_split", [P, 2, KC, D], BF16)
        wv = k.sb(c0, "wv_split", [P, 2, KC, D], BF16)
        bk = k.sb(c0, "bk", [P, KD])
        load_small(k, [(bvT, d["L0_xattn_bv"])])
        cross0_queries(k, ident, qT, wk, wv, bk)
        cross0_batches(k, ident, qT, wk, wv, bk, catT, bvT)
        cross0_output(k, x, catT)


def build(nc, d, out):
    k = Kit(nc, d, out)
    with ExitStack() as ctx:
        ident = k.sb(ctx, "ident", [P, P])
        tri = k.sb(ctx, "tri", [P, P])
        low = k.sb(ctx, "low", [P, P])
        constants(k, ident, tri, low)
        x = k.sb(ctx, "x", [P, NT, D])
        cross0(k, ident, x)
        state_space(k, ident, tri, x)
        block_ffn(k, ident, x)
        k.clear_semaphores()
        cross1(k, ident, x)
        self1(k, ident, low, x)
        dequant_phase(k, ident)
        quant_ffn(k, ident, x)


def load_small(k, pairs):
    nc = k.nc
    with ExitStack() as ctx:
        s = k.sem(ctx, "small_in")
        block = ctx.enter_context(nc.Block())

        @block.sync
        def _(sp):
            for dst, src in pairs:
                sp.dma_start(dst[:], src).then_inc(s, 16)
            sp.wait_ge(s, 16 * len(pairs))


def columns(a):
    return np.ascontiguousarray(a.reshape(-1, P).T)


def lay_out(i):
    f = np.ascontiguousarray
    pairs = lambda a: a.reshape((2, 4, 2, DH) + a.shape[1:])
    ctx = i["ctx_512"]
    return {
        "x": f(i["x"].reshape(TOK, D)),
        "ctxT": f(ctx.transpose(0, 2, 1)),
        "L0_xattn_Wq": f(i["L0_xattn_Wq"]), "L0_xattn_Wk": f(i["L0_xattn_Wk"]), "L0_xattn_Wv": f(i["L0_xattn_Wv"]),
        "L0_xattn_bq": columns(i["L0_xattn_bq"]), "L0_xattn_bk": columns(i["L0_xattn_bk"]),
        "L0_xattn_bv": f(pairs(i["L0_xattn_bv"]).transpose(1, 3, 0, 2).reshape(P, 4)),
        "L0_xattn_Wo": f(pairs(i["L0_xattn_Wo"]).transpose(0, 2, 1, 3, 4).reshape(4, P, D)),
        "L0_xattn_bo": f(i["L0_xattn_bo"].reshape(1, D)),
        "L0_attn_WX": f(i["L0_attn_W_XBC"][:, 0:DH].transpose(2, 0, 1)),
        "L0_attn_WB": f(i["L0_attn_W_XBC"][:, DH:DH + NS].transpose(2, 0, 1)),
        "L0_attn_WC": f(i["L0_attn_W_XBC"][:, DH + NS:].transpose(2, 0, 1)),
        "L0_attn_WG": f(i["L0_attn_W_gate"].transpose(2, 0, 1)),
        "L0_attn_WA": f(i["L0_attn_W_logA"][:, 0].T),
        "L0_attn_bX": f(i["L0_attn_b_XBC"][:, 0:DH].reshape(1, D)),
        "L0_attn_bB": columns(i["L0_attn_b_XBC"][:, DH:DH + NS]),
        "L0_attn_bC": columns(i["L0_attn_b_XBC"][:, DH + NS:]),
        "L0_attn_bG": columns(i["L0_attn_b_gate"]),
        "L0_attn_bA": f(i["L0_attn_b_logA"].reshape(1, H)),
        "L0_attn_W_out": f(i["L0_attn_W_out"].T),
        "L0_attn_bO": f(i["L0_attn_b_out"].reshape(1, D)),
        "ctx": f(ctx),
        "L1_ffn_w_up": f(i["L1_ffn_w_up"]), "L1_ffn_w_gate": f(i["L1_ffn_w_gate"]), "L1_ffn_w_down": f(i["L1_ffn_w_down"]),
        "L1_xattn_Wq": f(i["L1_xattn_Wq"]), "L1_xattn_WkT": f(i["L1_xattn_Wk"].T), "L1_xattn_Wv": f(i["L1_xattn_Wv"]),
        "L1_xattn_bq": columns(i["L1_xattn_bq"]), "L1_xattn_bk": columns(i["L1_xattn_bk"]),
        "L1_xattn_bv": f(i["L1_xattn_bv"].reshape(1, D)),
        "L1_attn_Wq": f(i["L1_attn_Wq"]), "L1_attn_Wk": f(i["L1_attn_Wk"]), "L1_attn_Wv": f(i["L1_attn_Wv"]),
        "L0_ffn_router_w": f(i["L0_ffn_router_w"].T), "L0_ffn_router_b": f(i["L0_ffn_router_b"].reshape(1, NB)),
        "L0_ffn_w1": f(i["L0_ffn_w1"].T), "L0_ffn_b1": columns(i["L0_ffn_b1"]),
        "L0_ffn_w2": f(i["L0_ffn_w2"].T), "L0_ffn_b2": f(i["L0_ffn_b2"].reshape(1, D)),
    }


def kernel(**inputs):
    import concourse.bacc as _bacc
    from concourse.bass_utils import run_bass_kernel_spmd as _run

    nc = _bacc.Bacc("TRN2", target_bir_lowering=False, num_devices=1)
    arrays = lay_out({n: np.asarray(a) for n, a in inputs.items()})
    d = {n: nc.dram_tensor(f"in_{n}", a.shape, mybir.dt.from_np(a.dtype), kind="ExternalInput").ap()
         for n, a in arrays.items()}
    out = nc.dram_tensor("out", (TOK, D), F32, kind="ExternalOutput").ap()
    build(nc, d, out)
    r = _run(nc, [{f"in_{n}": a for n, a in arrays.items()}], core_ids=[0])
    return r.results[0]["out"].reshape(B, L, D)
```

```python
from contextlib import ExitStack

import numpy as np
import concourse.bass as bass
from concourse import mybir

F32 = mybir.dt.float32
BF16 = mybir.dt.bfloat16
ALU = mybir.AluOpType
ACT = mybir.ActivationFunctionType
AX = mybir.AxisListType.X

P = 128
B, L, D = 16, 64, 512
TOK = B * L
NT = TOK // P
KD = D // P
NK, CD = 1601, 256
KC = CD // P
H, DH = 16, D // 16
NPAIR = H // 2
KTILES = [(n, min(P, NK - n)) for n in range(0, NK, P)]
CHUNKS = [(n, min(512, NK - n)) for n in range(0, NK, 512)]
NTG = 4
TGROUPS = [KTILES[4 * j:4 * j + 4] for j in range(NTG)]
EPS = 1e-5
ROUND = 12582912.0
FAR = -3.0e38
QMAX = 32767.0


class Kit:

    def __init__(self, nc, d, out):
        self.nc, self.d, self.out = nc, d, out
        self.used = []
        self.stats = None
        self.scratch = {n: nc.dram_tensor(f"parts_{n}", (P, 2, WCOLS), BF16, kind="Internal").ap()
                        for n in Dequant.MATRICES}

    def sb(self, ctx, name, shape, dt=F32):
        return ctx.enter_context(self.nc.sbuf_tensor(name, shape, dt))

    def ps(self, ctx, name, shape, dt=F32):
        return ctx.enter_context(self.nc.psum_tensor(name, shape, dt))

    def sem(self, ctx, name):
        self.used.append(self.nc.alloc_semaphore(name=name))
        return self.used[-1]

    def tile_stats(self, dve, x, t, done):
        dve.wait_ge(*done)
        if isinstance(t, int):
            dve.bn_stats(self.stats[:, t, :], x[:, t, :])
        else:
            dve.bn_stats(self.stats[:, bass.ds(t, 1), :].rearrange("p a n -> p (a n)"),
                         x[:, bass.ds(t, 1), :].rearrange("p a n -> p (a n)"))

    def clear_semaphores(self):
        self.nc.clear_and_free_semaphores(self.used)
        self.used = []
        self.nc.all_engine_barrier()



class Norm:

    def __init__(self, k, ctx, name, x, ident, banks, xT, loaded=None, xhat=None, split=None):
        self.split = split
        self.x, self.ident, self.banks, self.xT = x, ident, banks, xT
        self.loaded = loaded
        self.stats = k.sb(ctx, name + "_stats", [P, NT, 6]) if loaded else k.stats
        self.meanvar = k.sb(ctx, name + "_meanvar", [P, NT, 2])
        self.rstd = k.sb(ctx, name + "_rstd", [P, NT, 1])
        self.xhat = k.sb(ctx, name + "_xhat", [P, NT, D]) if xhat is None else xhat
        self.s_stats = k.sem(ctx, name + "_stats_done")
        self.small = k.sb(ctx, name + "_small", [P, 4, NT])
        self.s_var = k.sem(ctx, name + "_var_done")
        self.s_root = k.sem(ctx, name + "_root_done")
        self.s_hat = k.sem(ctx, name + "_xhat_done")
        self.s_low = k.sem(ctx, name + "_low_done")
        self.s_turned = k.sem(ctx, name + "_turned")
        self.s_xT = k.sem(ctx, name + "_xT_done")

    def on_vector(self, dve):
        before = NT if self.loaded else 0
        if self.loaded:
            for t in range(NT):
                dve.wait_ge(*self.loaded(t))
                dve.bn_stats(self.stats[:, t, :], self.x[:, t, :]).then_inc(self.s_stats, 1)
            dve.wait_ge(self.s_stats, before)
        for t in range(NT):
            dve.bn_aggr(self.meanvar[:, t, :], self.stats[:, t, :]).then_inc(self.s_stats, 1)
        dve.wait_ge(self.s_stats, before + NT)
        ve, root, r, u = (self.small[:, n, :] for n in range(4))
        dve.tensor_scalar(ve, self.meanvar[:, :, 1], EPS, None, ALU.add).then_inc(self.s_var, 1)
        dve.wait_ge(self.s_root, 1)
        dve.reciprocal(r, root).then_inc(self.s_var, 1)
        dve.wait_ge(self.s_var, 2)
        dve.tensor_tensor(u, r, r, ALU.mult).then_inc(self.s_var, 1)
        dve.wait_ge(self.s_var, 3)
        dve.tensor_tensor(u, u, ve, ALU.mult).then_inc(self.s_var, 1)
        dve.wait_ge(self.s_var, 4)
        dve.tensor_scalar(u, u, -0.5, 1.5, ALU.mult, ALU.add).then_inc(self.s_var, 1)
        dve.wait_ge(self.s_var, 5)
        dve.tensor_tensor(self.rstd[:, :, 0], r, u, ALU.mult).then_inc(self.s_var, 1)
        dve.wait_ge(self.s_var, 6)
        for t in range(NT):
            dve.tensor_scalar(self.xhat[:, t, :], self.x[:, t, :], self.meanvar[:, t, 0:1],
                              self.rstd[:, t, :], ALU.subtract, ALU.mult).then_inc(self.s_hat, 1)

    def on_tensor(self, pe):
        for t in range(NT):
            pe.wait_ge(self.s_hat, t + 1)
            if t >= 2:
                pe.wait_ge(self.s_xT, t - 1)
            for j in range(KD):
                last = pe.transpose(self.banks[t % 2][:, j * P:(j + 1) * P],
                                    self.xhat[:, t, j * P:(j + 1) * P], self.ident[:])
            last.then_inc(self.s_turned, 1)

    def on_scalar(self, nc, act):
        act.wait_ge(self.s_var, 1)
        nc.scalar.activation(self.small[:, 1, :], self.small[:, 0, :], ACT.Sqrt).then_inc(self.s_root, 1)
        for t in range(NT):
            act.wait_ge(self.s_turned, t + 1)
            for dst in (self.xT,) if self.split is None else (self.xT, self.split[0]):
                last = nc.scalar.copy(dst[:, :, t * P:(t + 1) * P],
                                      self.banks[t % 2][:].rearrange("p (j n) -> p j n", j=KD))
            last.then_inc(self.s_xT, 1)

    def low_on_vector(self, dve):
        for t in range(NT):
            c = slice(t * P, (t + 1) * P)
            dve.wait_ge(self.s_xT, t + 1)
            dve.tensor_tensor(self.split[1][:, :, c], self.xT[:, :, c], self.split[0][:, :, c],
                              ALU.subtract).then_inc(self.s_low, 1)



def constants(k, ident, tri, low):
    nc = k.nc
    with ExitStack() as ctx:
        s_set = k.sem(ctx, "c_set")
        s_done = k.sem(ctx, "c_done")
        block = ctx.enter_context(nc.Block())

        @block.gpsimd
        def _(pool):
            pool.memset(ident[:], 0.0).then_inc(s_set, 1)
            pool.memset(tri[:], 1.0).then_inc(s_set, 1)
            pool.memset(low[:], 0.0).then_inc(s_set, 1)
            pool.wait_ge(s_set, 3)
            pool.affine_select(out=ident[:], in_=ident[:], compare_op=ALU.not_equal, fill=1.0, base=0,
                               pattern=[[-1, P]], channel_multiplier=1).then_inc(s_done, 1)
            pool.affine_select(out=tri[:], in_=tri[:], compare_op=ALU.is_ge, fill=0.0, base=0,
                               pattern=[[1, P]], channel_multiplier=-1).then_inc(s_done, 1)
            pool.wait_ge(s_done, 2)
            pool.affine_select(out=tri[:, L:P], in_=tri[:, L:P], compare_op=ALU.is_ge, fill=0.0, base=-L,
                               pattern=[[0, P - L]], channel_multiplier=1).then_inc(s_done, 1)
            pool.affine_select(out=low[:], in_=low[:], compare_op=ALU.is_ge, fill=FAR, base=0,
                               pattern=[[-1, P]], channel_multiplier=1).then_inc(s_done, 1)
            pool.wait_ge(s_done, 4)
            pool.affine_select(out=low[:, 0:L], in_=low[:, 0:L], compare_op=ALU.is_ge, fill=FAR, base=L - 1,
                               pattern=[[0, L]], channel_multiplier=-1).then_inc(s_done, 1)
            pool.wait_ge(s_done, 5)



def cross0_queries(k, ident, qT, wk, wv, bk):
    nc, d = k.nc, k.d
    with ExitStack() as ctx:
        x = k.sb(ctx, "q0_x", [P, NT, D])
        xT = k.sb(ctx, "q0_xT", [P, KD, TOK])
        wq = k.sb(ctx, "q0_wq", [P, KD, D])
        bq = k.sb(ctx, "q0_bq", [P, KD])
        qf = k.sb(ctx, "q0_qf", [P, 2, 512])
        wkf = k.sb(ctx, "q0_wkf", [P, 2, KC, D])
        banks = [k.ps(ctx, f"q0_bank{n}", [P, 512]) for n in range(4)]
        s_x = k.sem(ctx, "q0_x_in")
        s_x2 = k.sem(ctx, "q0_x_in2")
        s_w = k.sem(ctx, "q0_w_in")
        s_wkv = k.sem(ctx, "q0_wkv_in")
        s_split = k.sem(ctx, "q0_split")
        s_q = k.sem(ctx, "q0_q_done")
        s_qf = k.sem(ctx, "q0_qf_done")
        s_hi = k.sem(ctx, "q0_hi_done")
        s_lo = k.sem(ctx, "q0_lo_done")
        norm = Norm(k, ctx, "q0", x, ident, banks[0:2], xT,
                    lambda t: (s_x, 16) if t < NT // 2 else (s_x2, 16))
        block = ctx.enter_context(nc.Block())
        xv = d["x"].rearrange("(t p) n -> p t n", p=P)
        groups = [(m, c) for m in range(KD) for c in range(TOK // 512)]

        @block.sync
        def _(sp):
            sp.dma_start(x[:, 0:NT // 2, :], xv[:, 0:NT // 2, :]).then_inc(s_x, 16)
            sp.dma_start(x[:, NT // 2:NT, :], xv[:, NT // 2:NT, :]).then_inc(s_x2, 16)
            sp.dma_start(wq[:], d["L0_xattn_Wq"].rearrange("(j p) n -> p j n", p=P)).then_inc(s_w, 16)
            sp.dma_start(bq[:], d["L0_xattn_bq"]).then_inc(s_w, 16)
            sp.dma_start(wkf[:, 0], d["L0_xattn_Wk"].rearrange("(j p) n -> p j n", p=P)).then_inc(s_wkv, 16)
            sp.dma_start(wkf[:, 1], d["L0_xattn_Wv"].rearrange("(j p) n -> p j n", p=P)).then_inc(s_wkv, 16)
            sp.dma_start(bk[:], d["L0_xattn_bk"]).then_inc(s_wkv, 16)
            sp.wait_ge(s_wkv, 48)

        @block.vector
        def _(dve):
            norm.on_vector(dve)
            dve.wait_ge(s_wkv, 48)
            for n, w in enumerate((wk, wv)):
                dve.tensor_copy(w[:, 0], wkf[:, n]).then_inc(s_split, 1)
            dve.wait_ge(s_split, 2)
            for n, w in enumerate((wk, wv)):
                dve.tensor_tensor(w[:, 1], wkf[:, n], w[:, 0], ALU.subtract).then_inc(s_split, 1)
            for n, (m, c) in enumerate(groups):
                dve.wait_ge(s_q, n + 1)
                dve.tensor_scalar(qf[:, n % 2, :], banks[2 + n % 2][:], bq[:, m:m + 1], float(DH) ** -0.5,
                                  ALU.add, ALU.mult).then_inc(s_qf, 1)
                half = qT[:, 8 * c:8 * c + 8, :, m, :]
                src = qf[:, n % 2, :].rearrange("p (b q) -> p b q", q=L)
                dve.wait_ge(s_qf, n + 1)
                dve.tensor_copy(half[:, :, 0, :], src).then_inc(s_hi, 1)
                dve.wait_ge(s_hi, n + 1)
                dve.tensor_tensor(half[:, :, 1, :], src, half[:, :, 0, :], ALU.subtract).then_inc(s_lo, 1)

        @block.scalar
        def _(act):
            norm.on_scalar(nc, act)

        @block.tensor
        def _(pe):
            norm.on_tensor(pe)
            pe.wait_ge(s_w, 32)
            pe.wait_ge(norm.s_xT, NT)
            for n, (m, c) in enumerate(groups):
                if n >= 2:
                    pe.wait_ge(s_qf, n - 1)
                for j in range(KD):
                    last = pe.matmul(banks[2 + n % 2][:], wq[:, j, m * P:(m + 1) * P],
                                     xT[:, j, 512 * c:512 * c + 512], start=(j == 0), stop=(j == KD - 1))
                last.then_inc(s_q, 1)



PROJ = []
for _c in range(len(CHUNKS)):
    PROJ += [("K", _c, (m,)) for m in range(KD)] if CHUNKS[_c][1] == 512 else [("K", _c, tuple(range(KD)))]
    PROJ += [("V", _c, t) for t in range(4 * _c, min(4 * _c + 4, len(KTILES)))]
NPROJ = len(PROJ)
CUTS = [0, 4, 7, 10, 13, 16, 19, 22, NPROJ]
SLICES = list(zip(CUTS[:-1], CUTS[1:]))
CHUNK_AT = {0: 0, 1: 1, 3: 2, 5: 3}
RING = 3
EXP_AFTER = 2


def batch_plan(project, first):
    slots = []
    for p in range(NPAIR):
        proj = list(range(*SLICES[p])) if project else []
        turn = not (p == 0 and first)
        steps = [("late", 2), ("late", 3)] if not first or p > 1 else []
        for j in range(3):
            steps += [("proj", proj[j])] if j < len(proj) else []
            steps += [("turn", j)] if turn else []
        steps += [("pv", 0)] if turn else []
        steps += [("proj", n) for n in proj[3:]]
        steps += [("turn", 3), ("pv", 1)] if turn else []
        if p == 1 and not first:
            steps += [("out", 0)]
        slots.append(steps)
    return slots


def last_plan():
    return [[("late", 2), ("late", 3), ("turn", 0), ("turn", 1), ("turn", 2), ("pv", 0), ("turn", 3), ("pv", 1)],
            [("late", 2), ("late", 3), ("out", 0)]]


def ring_uses(plan):
    return sum(1 for s in plan for e in s if e[0] not in ("pv", "late"))


PLAN_FIRST = batch_plan(True, True)
PLAN_MID = batch_plan(True, False)
PLAN_END = batch_plan(False, False)
PLAN_LAST = last_plan()
N_FIRST, N_MID, N_END = ring_uses(PLAN_FIRST), ring_uses(PLAN_MID), ring_uses(PLAN_END)


def ring_base(b):
    return NPROJ + N_FIRST - N_MID + b * N_MID


def cross0_batches(k, ident, qT, wk, wv, bk, catT, bvT):
    nc, d = k.nc, k.d
    with ExitStack() as ctx:
        stage = k.sb(ctx, "x0_stage", [P, 2, KC, 512])
        chi = k.sb(ctx, "x0_ctx_hi", [P, 2, KC, 512], BF16)
        clo = k.sb(ctx, "x0_ctx_lo", [P, 2, KC, 512], BF16)
        qp = k.sb(ctx, "x0_q_padded", [P, 2, 2, KD, 2, 2, L], BF16)
        kT = k.sb(ctx, "x0_kT", [P, 2, 2, KD, NK], BF16)
        v = k.sb(ctx, "x0_v", [P, 2, 2, len(KTILES), D], BF16)
        prob = k.sb(ctx, "x0_prob", [P, 2, NK])
        pT = k.sb(ctx, "x0_pT", [P, 2, NTG, 512], BF16)
        nmax = k.sb(ctx, "x0_negmax", [P, 2])
        rsum = k.sb(ctx, "x0_rowsum", [P, 2])
        rinv = k.sb(ctx, "x0_rowinv", [P, 2])
        o = k.sb(ctx, "x0_o", [P, 2, NPAIR, DH])
        ot = k.sb(ctx, "x0_ot", [P, 2 * P])
        score = k.ps(ctx, "x0_score", [P, 2048])
        ring = [k.ps(ctx, f"x0_ring{n}", [P, 512]) for n in range(RING)]
        pv = k.ps(ctx, "x0_pv", [P, 512])
        ctx_in = [k.sem(ctx, f"x0_ctx_in{n}") for n in range(2)]
        qp_in = [k.sem(ctx, f"x0_qp_in{n}") for n in range(2)]
        qp_zero = k.sem(ctx, "x0_qp_zero")
        chi_done = k.sem(ctx, "x0_chi_done")
        clo_done = k.sem(ctx, "x0_clo_done")
        ring_full = k.sem(ctx, "x0_ring_full")
        hi_done = k.sem(ctx, "x0_hi_done")
        ring_free = k.sem(ctx, "x0_ring_free")
        s_done = k.sem(ctx, "x0_scores_done")
        max_done = k.sem(ctx, "x0_max_done")
        exp_done = k.sem(ctx, "x0_exp_done")
        pv_done = k.sem(ctx, "x0_pv_done")
        inv_done = k.sem(ctx, "x0_inv_done")
        o_done = k.sem(ctx, "x0_o_done")
        block = ctx.enter_context(nc.Block())
        ctxT = d["ctxT"].rearrange("b (j p) n -> p b j n", p=P)

        def each_batch(eng, do, last=None):
            do(0, 0, PLAN_FIRST, NPROJ)
            with eng.Fori(0, (B - 2) // 2) as i:
                for u in range(2):
                    do(2 * i + 1 + u, (1 + u) % 2, PLAN_MID, ring_base(2 * i + 1 + u))
            do(B - 1, (B - 1) % 2, PLAN_END, ring_base(B - 1))
            do(B, B % 2, PLAN_LAST, ring_base(B - 1) + N_END)

        @block.sync
        def _(sp):
            def load_chunk(b, c, ready):
                if ready is not None:
                    sp.wait_ge(clo_done, ready)
                n0, n = CHUNKS[c]
                src = ctxT[:, b, :, n0:n0 + n] if isinstance(b, int) else \
                    ctxT[:, bass.ds(b, 1), :, n0:n0 + n].rearrange("p a j n -> p (a j) n")
                sp.dma_start(stage[:, c % 2, :, 0:n], src).then_inc(ctx_in[c % 2], 16)

            def load_queries(b, par, free):
                if free is not None:
                    sp.wait_ge(s_done, free)
                for a in range(4):
                    src = qT[32 * a:32 * a + 32, b] if isinstance(b, int) else \
                        qT[32 * a:32 * a + 32, bass.ds(b, 1)].rearrange("p a h m q -> p (a h) m q")
                    for hl in range(2):
                        sp.dma_start(qp[32 * a:32 * a + 32, par, hl, :, a // 2, a % 2, :],
                                     src[:, hl]).then_inc(qp_in[par], 16)

            load_chunk(0, 0, None)
            load_chunk(0, 1, None)
            sp.wait_ge(qp_zero, 1)
            load_queries(0, 0, None)
            load_chunk(0, 2, 1)
            load_chunk(0, 3, 2)
            load_chunk(1, 0, 3)
            load_chunk(1, 1, 4)
            load_queries(1, 1, None)
            load_chunk(1, 2, 5)
            load_chunk(1, 3, 6)
            load_chunk(2, 0, 7)
            load_chunk(2, 1, 8)
            with sp.Fori(0, (B - 4) // 2) as i:
                for u in range(2):
                    b = 2 * i + 1 + u
                    load_queries(b + 1, u % 2, 8 * b)
                    load_chunk(b + 1, 2, 4 * b + 5)
                    load_chunk(b + 1, 3, 4 * b + 6)
                    load_chunk(b + 2, 0, 4 * b + 7)
                    load_chunk(b + 2, 1, 4 * b + 8)
            for b in (B - 3, B - 2):
                load_queries(b + 1, (b + 1) % 2, 8 * b)
                load_chunk(b + 1, 2, 4 * b + 5)
                load_chunk(b + 1, 3, 4 * b + 6)
                if b + 2 < B:
                    load_chunk(b + 2, 0, 4 * b + 7)
                    load_chunk(b + 2, 1, 4 * b + 8)

        @block.gpsimd
        def _(pool):
            pool.memset(qp[:], 0.0).then_inc(qp_zero, 1)
            with pool.Fori(0, B) as b:
                for c, (n0, n) in enumerate(CHUNKS):
                    pool.wait_ge(chi_done, 4 * b + c + 1)
                    pool.tensor_tensor(clo[:, c % 2, :, 0:n], stage[:, c % 2, :, 0:n],
                                       chi[:, c % 2, :, 0:n], ALU.subtract).then_inc(clo_done, 1)

        def ring_events(plan):
            r = 0
            for p, steps in enumerate(plan):
                for e in steps:
                    yield p, e, (None if e[0] in ("pv", "late") else r)
                    r += e[0] not in ("pv", "late")

        def by_vector(plan, r):
            slot = next(p for p, e, r_ in ring_events(plan) if r_ == r)
            groups = [r_ for p, e, r_ in ring_events(plan) if p == slot and r_ is not None]
            return plan is not PLAN_LAST and groups.index(r) == EXP_AFTER

        def after(plan, steps):
            return ring_uses(plan) - 1 - max(r for p, e, r in ring_events(plan) if (p, e) in steps)

        LAST_KEYS = max(n for n in range(NPROJ) if PROJ[n][0] == "K")
        AFTER_KEYS = after(PLAN_MID, [(p, ("proj", LAST_KEYS)) for p in range(NPAIR)])
        AFTER_TURN = [after(PLAN_MID, [(NPAIR - 1, ("turn", j))]) for j in range(NTG)]
        AFTER_TURN_END = [after(PLAN_END, [(NPAIR - 1, ("turn", j))]) for j in range(NTG)]

        def turn_place(plan, at, j):
            return next(r for p, e, r in ring_events(plan) if p == at and e == ("turn", j))

        def proj_end(plan, c):
            return 1 + max(r for p, e, r in ring_events(plan)
                           if e[0] == "proj" and PROJ[e[1]][1] == c)

        @block.tensor
        def _(pe):
            def wait_bank(r, base):
                if r >= RING:
                    pe.wait_ge(ring_free, base + (r - RING + 1))
                elif not (isinstance(base, int) and base == 0):
                    pe.wait_ge(ring_free, base - 1 if r == 0 else base)

            def project(n, b_next, par, r, base):
                kind, c, m = PROJ[n]
                n0, w = CHUNKS[c]
                if n == 0 or PROJ[n - 1][1] != c:
                    pe.wait_ge(clo_done, 4 * b_next + c + 1)
                wait_bank(r, base)
                bank = ring[r % RING]
                steps = [(hl_w, src, j) for hl_w, src in ((0, chi), (1, chi), (0, clo)) for j in range(KC)]
                for a, tile in enumerate(m if kind == "K" else (m,)):
                    for i, (hl_w, src, j) in enumerate(steps):
                        if kind == "K":
                            out_, lhs, rhs = (bank[:, a * w:a * w + w], wk[:, hl_w, j, tile * P:(tile + 1) * P],
                                              src[:, c % 2, j, 0:w])
                        else:
                            k0, kw = KTILES[tile]
                            out_, lhs, rhs = bank[0:kw, :], src[:, c % 2, j, k0 - n0:k0 - n0 + kw], wv[:, hl_w, j, :]
                        last = pe.matmul(out_, lhs, rhs, start=(i == 0), stop=(i == len(steps) - 1))
                last.then_inc(ring_full, 1)

            def batch(b, par, plan, base):
                if plan is not PLAN_LAST:
                    pe.wait_ge(qp_in[par], 128 * (b // 2 + 1) if isinstance(b, int) else
                               64 * (b + (1 if par else 2)))
                for p, steps in enumerate(plan):
                    if plan is not PLAN_LAST:
                        if p or plan is not PLAN_FIRST:
                            pe.wait_ge(exp_done, 8 * b + p)
                        for c, (n0, w) in enumerate(CHUNKS):
                            if p == 0 and c == len(CHUNKS) - 1:
                                pe.wait_ge(ring_free, base if plan is PLAN_FIRST else base - AFTER_KEYS)
                            elif p == 0 and c == 0 and plan is PLAN_FIRST:
                                pe.wait_ge(ring_free, base)
                            for i, (hq, hk) in enumerate(((0, 0), (1, 0), (0, 1))):
                                last = pe.matmul(score[:, 512 * c:512 * c + w],
                                                 qp[:, par, hq, p // 2, p % 2, :, :].rearrange("p a q -> p (a q)"),
                                                 kT[:, par, hk, p // 2, n0:n0 + w], start=(i == 0), stop=(i == 2))
                        last.then_inc(s_done, 1)
                    for p_, e, r in ring_events(plan):
                        if p_ != p:
                            continue
                        if e[0] == "proj":
                            project(e[1], b + 1, 1 - par, r, base)
                        elif e[0] == "turn":
                            if e[1] == 0:
                                pe.wait_ge(exp_done, 8 * b + p)
                            wait_bank(r, base)
                            for i, (k0, kw) in enumerate(TGROUPS[e[1]]):
                                last = pe.transpose(ring[r % RING][0:kw, P * i:P * i + P],
                                                    prob[:, (p - 1) % 2, k0:k0 + kw], ident[:])
                            last.then_inc(ring_full, 1)
                        elif e[0] in ("pv", "late"):
                            j = e[1]
                            back = 1 if e[0] == "pv" else 2
                            pp, vpar = (p - back) % NPAIR, (par if p >= back else 1 - par)
                            if j == 0 and not (plan is PLAN_FIRST and p == 1):
                                pe.wait_ge(o_done, 8 * b + p - 1)
                            if e[0] == "pv":
                                pe.wait_ge(ring_free, base + (turn_place(plan, p, j) + 1))
                            elif p:
                                pe.wait_ge(ring_free, base + (turn_place(plan, p - 1, j) + 1))
                            else:
                                pe.wait_ge(ring_free, base - (AFTER_TURN[j] if plan is not PLAN_LAST else AFTER_TURN_END[j]))
                            for i, (k0, kw) in enumerate(TGROUPS[j]):
                                for n, (hp, hv) in enumerate(((0, 0), (0, 1), (1, 0))):
                                    last = pe.matmul(pv[:, 0:2 * DH], pT[0:kw, hp, j, P * i:P * i + P],
                                                     v[0:kw, vpar, hv, 4 * j + i, 2 * DH * pp:2 * DH * (pp + 1)],
                                                     start=(j == 0 and i == 0 and n == 0),
                                                     stop=(j == NTG - 1 and n == 2))
                            if j == NTG - 1:
                                last.then_inc(pv_done, 1)
                        else:
                            pe.wait_ge(o_done, 8 * b)
                            wait_bank(r, base)
                            for h in range(2):
                                last = pe.transpose(ring[r % RING][:, P * h:P * h + P],
                                                    o[:, 1 - par, 4 * h:4 * h + 4, :].rearrange("p a d -> p (a d)"),
                                                    ident[:])
                            last.then_inc(ring_full, 1)

            for n in range(NPROJ):
                project(n, 0, 0, n, 0)
            each_batch(pe, batch)

        @block.scalar
        def _(act):
            def project_hi(n, par, r, number):
                kind, c, m = PROJ[n]
                n0, w = CHUNKS[c]
                act.wait_ge(ring_full, number)
                if kind == "K":
                    for a, tile in enumerate(m):
                        last = nc.scalar.activation(kT[:, par, 0, tile, n0:n0 + w], ring[r % RING][:, a * w:a * w + w],
                                                    ACT.Identity, bias=bk[:, tile:tile + 1])
                    last.then_inc(hi_done, 1)
                else:
                    kw = KTILES[m][1]
                    nc.scalar.copy(v[0:kw, par, 0, m, :], ring[r % RING][0:kw, :]).then_inc(hi_done, 1)

            def batch(b, par, plan, base):
                for p, steps in enumerate(plan):
                    def exps():
                        act.wait_ge(max_done, 8 * b + p + 1)
                        nc.scalar.activation(prob[:, p % 2, :], score[:, 0:NK], ACT.Exp, bias=nmax[:, p % 2:p % 2 + 1],
                                             accum_out=rsum[:, p % 2:p % 2 + 1]).then_inc(exp_done, 1)
                    done = plan is PLAN_LAST
                    if not done and len(steps) < EXP_AFTER:
                        exps()
                        done = True
                    seen = 0
                    for p_, e, r in ring_events(plan):
                        if p_ != p or r is None:
                            continue
                        seen += 1
                        if by_vector(plan, r):
                            continue
                        if r and by_vector(plan, r - 1):
                            act.wait_ge(hi_done, base + r)
                        if e[0] == "proj":
                            project_hi(e[1], 1 - par, r, base + (r + 1))
                        else:
                            act.wait_ge(ring_full, base + (r + 1))
                            if e[0] == "turn":
                                n = P * len(TGROUPS[e[1]])
                                kw = TGROUPS[e[1]][0][1]
                                nc.scalar.copy(pT[0:kw, 0, e[1], 0:n], ring[r % RING][0:kw, 0:n]).then_inc(hi_done, 1)
                            else:
                                nc.scalar.copy(ot[:], ring[r % RING][:, 0:2 * P]).then_inc(hi_done, 1)
                        if not done and seen == EXP_AFTER:
                            exps()
                            done = True

            for n in range(NPROJ):
                project_hi(n, 0, n, n + 1)
            each_batch(act, batch)

        @block.vector
        def _(dve):
            def split_chunk(b, c, ready):
                n0, n = CHUNKS[c]
                dve.wait_ge(ctx_in[c % 2], 16 * (2 * b + (c // 2 + 1)))
                if ready is not None:
                    dve.wait_ge(ring_full, ready)
                dve.tensor_copy(chi[:, c % 2, :, 0:n], stage[:, c % 2, :, 0:n]).then_inc(chi_done, 1)

            def project_hi(n, par, r, number):
                kind, c, m = PROJ[n]
                n0, w = CHUNKS[c]
                dve.wait_ge(ring_full, number)
                if kind == "K":
                    for a, tile in enumerate(m):
                        last = dve.tensor_scalar(kT[:, par, 0, tile, n0:n0 + w], ring[r % RING][:, a * w:a * w + w],
                                                 bk[:, tile:tile + 1], None, ALU.add)
                    last.then_inc(hi_done, 1)
                else:
                    kw = KTILES[m][1]
                    dve.tensor_copy(v[0:kw, par, 0, m, :], ring[r % RING][0:kw, :]).then_inc(hi_done, 1)

            def project_lo(n, par, r, number):
                kind, c, m = PROJ[n]
                n0, w = CHUNKS[c]
                dve.wait_ge(hi_done, number)
                if kind == "K":
                    for a, tile in enumerate(m):
                        last = dve.scalar_tensor_tensor(
                            kT[:, par, 1, tile, n0:n0 + w], ring[r % RING][:, a * w:a * w + w], bk[:, tile:tile + 1],
                            kT[:, par, 0, tile, n0:n0 + w], ALU.add, ALU.subtract)
                    last.then_inc(ring_free, 1)
                else:
                    kw = KTILES[m][1]
                    dve.tensor_tensor(v[0:kw, par, 1, m, :], ring[r % RING][0:kw, :], v[0:kw, par, 0, m, :],
                                      ALU.subtract).then_inc(ring_free, 1)

            def batch(b, par, plan, base):
                for p, steps in enumerate(plan):
                    if plan in (PLAN_FIRST, PLAN_MID) and p in CHUNK_AT:
                        c = CHUNK_AT[p]
                        split_chunk(b + 1, c, base if c < 2 else base + proj_end(plan, c - 2))
                    if plan is not PLAN_LAST:
                        dve.wait_ge(s_done, 8 * b + p + 1)
                        dve.tensor_reduce(nmax[:, p % 2:p % 2 + 1], score[:, 0:NK], AX, ALU.max,
                                          negate=True).then_inc(max_done, 1)
                    for p_, e, r in ring_events(plan):
                        if p_ != p:
                            continue
                        if e[0] == "proj":
                            if by_vector(plan, r):
                                project_hi(e[1], 1 - par, r, base + (r + 1))
                            project_lo(e[1], 1 - par, r, base + (r + 1))
                        elif e[0] == "turn":
                            n = P * len(TGROUPS[e[1]])
                            kw = TGROUPS[e[1]][0][1]
                            if by_vector(plan, r):
                                dve.wait_ge(ring_full, base + (r + 1))
                                dve.tensor_copy(pT[0:kw, 0, e[1], 0:n], ring[r % RING][0:kw, 0:n]).then_inc(hi_done, 1)
                            dve.wait_ge(hi_done, base + (r + 1))
                            dve.tensor_tensor(pT[0:kw, 1, e[1], 0:n], ring[r % RING][0:kw, 0:n], pT[0:kw, 0, e[1], 0:n],
                                              ALU.subtract).then_inc(ring_free, 1)
                        elif e[0] == "out":
                            dve.wait_ge(hi_done, base + (r + 1))
                            tok = bass.ds(L * (b - 1), L) if not isinstance(b, int) else slice(L * (b - 1), L * b)
                            dve.tensor_tensor(catT[:, :, :, tok], ot[:].rearrange("p (a h q) -> p a h q", a=2, h=2),
                                              bvT[:].rearrange("p (a h) -> p a h", a=2).unsqueeze(3).broadcast_to([P, 2, 2, L]),
                                              ALU.add).then_inc(ring_free, 1)
                        elif e == ("pv", 0):
                            pp = (p - 1) % NPAIR
                            dve.reciprocal(rinv[:, pp % 2:pp % 2 + 1], rsum[:, pp % 2:pp % 2 + 1]).then_inc(inv_done, 1)
                        elif e == ("late", 3):
                            pp, opar = (p - 2) % NPAIR, (par if p >= 2 else 1 - par)
                            dve.wait_ge(inv_done, 8 * b + p - 1)
                            dve.wait_ge(pv_done, 8 * b + p - 1)
                            dve.tensor_scalar(o[0:L, opar, pp, :], pv[0:L, 0:DH], rinv[0:L, pp % 2:pp % 2 + 1], None,
                                              ALU.mult)
                            dve.tensor_scalar(o[L:P, opar, pp, :], pv[L:P, DH:2 * DH], rinv[L:P, pp % 2:pp % 2 + 1], None,
                                              ALU.mult).then_inc(o_done, 1)

            for c in range(4):
                split_chunk(0, c, None if c < 2 else proj_end([[("proj", n) for n in range(NPROJ)]], c - 2))
                for n in range(NPROJ):
                    if PROJ[n][1] == c - 1:
                        project_lo(n, 0, n, n + 1)
            for n in range(NPROJ):
                if PROJ[n][1] == 3:
                    project_lo(n, 0, n, n + 1)
            each_batch(dve, batch)



def load_x_again(k, sp, x, s_in):
    sp.dma_start(x[:], k.d["x"].rearrange("(t p) n -> p t n", p=P)).then_inc(s_in, 16)


def cross0_output(k, ident, x, catT):
    nc, d = k.nc, k.d
    NB_O = 6
    with ExitStack() as ctx:
        wo = k.sb(ctx, "o0_wo", [P, 4, D])
        bo = k.sb(ctx, "o0_bo", [P, D])
        banks = [k.ps(ctx, f"o0_bank{n}", [P, 512]) for n in range(8)]
        s_in = k.sem(ctx, "o0_in")
        s_wo = k.sem(ctx, "o0_wo_in")
        s_x = k.sem(ctx, "o0_x")
        s_sum = k.sem(ctx, "o0_sum")
        s_out = k.sem(ctx, "o0_out")
        dq = Dequant(k, ctx, 0, banks[NB_O:], ident)
        block = ctx.enter_context(nc.Block())

        @block.sync
        def _(sp):
            sp.dma_start(wo[:], d["L0_xattn_Wo"].rearrange("t p n -> p t n")).then_inc(s_wo, 16)
            dq.load(sp)
            load_x_again(k, sp, x, s_in)
            sp.dma_start(bo[:], d["L0_xattn_bo"].partition_broadcast(P)).then_inc(s_in, 16)
            sp.wait_ge(s_wo, 16)
            sp.wait_ge(s_in, 32)
            dq.store(sp)

        @block.tensor
        def _(pe):
            pe.wait_ge(s_wo, 16)
            for t in range(NT):
                if t >= NB_O:
                    pe.wait_ge(s_out, t - NB_O + 1)
                for i in range(4):
                    last = pe.matmul(banks[t % NB_O][:], catT[:, i // 2, i % 2, t * P:(t + 1) * P], wo[:, i, :],
                                     start=(i == 0), stop=(i == 3))
                last.then_inc(s_sum, 1)
            dq.turn(pe, range(MF))

        @block.gpsimd
        def _(pool):
            dq.multiply(pool)

        @block.scalar
        def _(act):
            dq.high(act, range(MF))

        @block.vector
        def _(dve):
            dq.scales(dve)
            dq.divide(dve)
            dq.round(dve)
            dq.unshift(dve)
            dve.wait_ge(s_in, 32)
            for t in range(NT):
                dve.tensor_tensor(x[:, t, :], x[:, t, :], bo[:], ALU.add).then_inc(s_x, 1)
            for t in range(NT):
                dve.wait_ge(s_x, t + 1)
                dve.wait_ge(s_sum, t + 1)
                dve.tensor_tensor(x[:, t, :], x[:, t, :], banks[t % NB_O][:], ALU.add).then_inc(s_out, 1)
                k.tile_stats(dve, x, t, (s_out, t + 1))
            dq.low(dve, range(MF))



NS = 64


def state_space(k, ident, tri, x):
    nc, d = k.nc, k.d
    with ExitStack() as ctx:
        xT = k.sb(ctx, "m_xT", [P, KD, TOK])
        wB = k.sb(ctx, "m_wB", [P, NPAIR, 2 * NS])
        wC = k.sb(ctx, "m_wC", [P, NPAIR, 2 * NS])
        wX = k.sb(ctx, "m_wX", [P, KD, P])
        wG = k.sb(ctx, "m_wG", [P, KD, P])
        wA = k.sb(ctx, "m_wA", [P, KD * H])
        wO = k.sb(ctx, "m_wO", [P, KD, D])
        bB = k.sb(ctx, "m_bB", [P, NPAIR])
        bC = k.sb(ctx, "m_bC", [P, NPAIR])
        bG = k.sb(ctx, "m_bG", [P, KD])
        bX = k.sb(ctx, "m_bX", [P, D])
        bA = k.sb(ctx, "m_bA", [P, H])
        bO = k.sb(ctx, "m_bO", [P, D])
        part_rows = slice(0, 64 + H)
        sel3 = k.sb(ctx, "m_sel3", [P, H, P], BF16)
        bT = k.sb(ctx, "m_bT", [P, NPAIR, TOK])
        cT = k.sb(ctx, "m_cT", [P, NPAIR, TOK])
        xn = k.sb(ctx, "m_xn", [P, NT, D])
        xb = k.sb(ctx, "m_xb", [P, 2, D])
        gT = k.sb(ctx, "m_gT", [P, KD, TOK])
        la3 = k.sb(ctx, "m_la", [P, NT, 64 + H])
        la = la3[:, :, 0:H]
        cum = k.sb(ctx, "m_cum", [P, NT, H])
        cum3 = k.sb(ctx, "m_cum3", [P, TOK], BF16)
        rest = k.sb(ctx, "m_cum_rest", [P, TOK])
        middle = k.sb(ctx, "m_cum_middle", [P, TOK], BF16)
        decay = k.sb(ctx, "m_decay", [P, 2, 2, 4, P])
        diff, dec = decay[:, 0], decay[:, 1]
        sel = decay[:].rearrange("p n u a i -> p (n u a) i")
        mix = k.sb(ctx, "m_mix", [P, 2, 4, P])
        banks = [k.ps(ctx, f"m_bank{n}", [P, 512]) for n in range(8)]
        s_zero = k.sem(ctx, "m_zero")
        s_sel = k.sem(ctx, "m_sel_done")
        s_sel3 = k.sem(ctx, "m_sel3_done")
        s_w = k.sem(ctx, "m_w_in")
        s_b = k.sem(ctx, "m_b_in")
        s_p = k.sem(ctx, "m_p_full")
        s_pf = k.sem(ctx, "m_p_free")
        s_x = k.sem(ctx, "m_x_full")
        s_xb = k.sem(ctx, "m_xb_done")
        s_xn = k.sem(ctx, "m_xn_done")
        s_g = k.sem(ctx, "m_g_full")
        s_gT = k.sem(ctx, "m_gT_done")
        s_a = k.sem(ctx, "m_a_full")
        s_la = k.sem(ctx, "m_la_done")
        s_c = k.sem(ctx, "m_cum_full")
        s_cum = k.sem(ctx, "m_cum_done")
        s_cumT = k.sem(ctx, "m_cumT_done")
        s_r = k.sem(ctx, "m_r_full")
        s_diff = k.sem(ctx, "m_diff_done")
        s_dec = k.sem(ctx, "m_dec_done")
        s_mask = k.sem(ctx, "m_mask_done")
        s_mix = k.sem(ctx, "m_mix_done")
        s_y = k.sem(ctx, "m_y_full")
        s_yg = k.sem(ctx, "m_yg_done")
        s_o = k.sem(ctx, "m_o_full")
        s_xo = k.sem(ctx, "m_xo")
        s_out = k.sem(ctx, "m_out")
        norm = Norm(k, ctx, "m", x, ident, banks[0:2], xT)
        yg = norm.xhat[:].rearrange("p t n -> p (t n)").rearrange("p (g n) -> p g n", g=KD)
        block = ctx.enter_context(nc.Block())
        projections = [(w, dst, pr, c) for w, dst in ((0, bT), (1, cT)) for pr in range(NPAIR) for c in range(2)]
        units = [(t, g) for t in range(NT) for g in range(KD)]

        @block.gpsimd
        def _(pool):
            for w in (wB, wC, wX, wG, wA):
                pool.memset(w[:], 0.0).then_inc(s_zero, 1)
            pool.memset(la3[:], 0.0).then_inc(s_zero, 1)
            pool.memset(sel, 0.0).then_inc(s_zero, 1)
            pool.wait_ge(s_zero, 7)
            for n in range(3):
                if n:
                    pool.wait_ge(s_sel, n)
                pool.affine_select(out=sel, in_=sel, compare_op=ALU.not_equal, fill=1.0, base=-32 * n,
                                   pattern=[[-1, H], [0, P]], channel_multiplier=1).then_inc(s_sel, 1)
            for n in range(len(units)):
                pool.wait_ge(s_dec, n + 1)
                pool.tensor_tensor(diff[:, n % 2], dec[:, n % 2],
                                   tri[:].unsqueeze(1).broadcast_to([P, 4, P]), ALU.mult).then_inc(s_mask, 1)

        @block.sync
        def _(sp):
            for dst, n in ((bB, "L0_attn_bB"), (bC, "L0_attn_bC"), (bG, "L0_attn_bG")):
                sp.dma_start(dst[:], d[n]).then_inc(s_b, 16)
            for dst, n in ((bX, "L0_attn_bX"), (bA, "L0_attn_bA"), (bO, "L0_attn_bO")):
                sp.dma_start(dst[:], d[n].partition_broadcast(P)).then_inc(s_b, 16)
            sp.dma_start(wO[:], d["L0_attn_W_out"].rearrange("(g p) n -> p g n", p=P)).then_inc(s_b, 16)
            sp.wait_ge(s_zero, 5)
            for a in range(4):
                r = slice(32 * a, 32 * a + 32)
                c = slice(NS * (a % 2), NS * (a % 2) + NS)
                sp.dma_start(wB[r, a // 2::2, c], d["L0_attn_WB"][:, a::4, :]).then_inc(s_w, 16)
                sp.dma_start(wC[r, a // 2::2, c], d["L0_attn_WC"][:, a::4, :]).then_inc(s_w, 16)
                sp.dma_start(wX[r, :, r], d["L0_attn_WX"][:, a::4, :]).then_inc(s_w, 16)
                sp.dma_start(wG[r, :, r], d["L0_attn_WG"][:, a::4, :]).then_inc(s_w, 16)
                sp.dma_start(wA[r, a::H + 4], d["L0_attn_WA"][:, a::4], allow_slow_non_contiguous=True).then_inc(s_w, 16)
            sp.wait_ge(s_w, 16 * 20)
            sp.wait_ge(s_b, 16 * 7)

        @block.tensor
        def _(pe):
            norm.on_tensor(pe)
            pe.wait_ge(norm.s_xT, NT)
            pe.wait_ge(s_w, 16 * 20)
            for t in range(NT):
                tile = slice(t * P, (t + 1) * P)
                for g in range(KD):
                    last = pe.matmul(banks[2][:, H * t:H * t + H], xT[:, g, tile], wA[:, H * g:H * g + H],
                                     start=(g == 0), stop=(g == KD - 1))
            last.then_inc(s_a, 1)
            for n, (w, dst, pr, c) in enumerate(projections):
                if n >= 2:
                    pe.wait_ge(s_pf, n - 1)
                pe.matmul(banks[n % 2][:], (wB, wC)[w][:, pr, :], xT[:, pr // 2, 512 * c:512 * c + 512],
                          start=True, stop=True).then_inc(s_p, 1)
                if n == 4:
                    pe.wait_ge(s_la, 3)
                    pe.matmul(banks[3][:, 0:NT * H], tri[:], la,
                              start=True, stop=True).then_inc(s_c, 1)
                    for t in range(NT):
                        last = pe.matmul(banks[4 + t // 4][part_rows, P * (t % 4):P * (t % 4) + P], la3[:, t, :], tri[:],
                                         start=True, stop=True)
                    last.then_inc(s_c, 1)
            for t in range(NT):
                if t >= 2:
                    pe.wait_ge(s_xb, t - 1)
                for g in range(KD):
                    last = pe.matmul(banks[6 + t % 2][:, P * g:P * g + P], xT[:, g, t * P:(t + 1) * P], wX[:, g, :],
                                     start=True, stop=True)
                last.then_inc(s_x, 1)
            pe.wait_ge(s_pf, len(projections))
            for n in range(2 * KD):
                if n >= 2:
                    pe.wait_ge(s_gT, n - 1)
                pe.matmul(banks[n % 2][:], wG[:, n // 2, :], xT[:, n // 2, 512 * (n % 2):512 * (n % 2) + 512],
                          start=True, stop=True).then_inc(s_g, 1)
            pe.wait_ge(s_gT, 2 * KD)
            pe.wait_ge(s_xb, NT)
            pe.wait_ge(s_sel3, 1)
            pe.wait_ge(s_cumT, 10)
            pe.wait_ge(s_cum, 1)

            def products(n):
                t, g = units[n]
                pe.wait_ge(s_mix, n + 1)
                if n == 0:
                    pe.wait_ge(s_xn, NT)
                if n >= 2:
                    pe.wait_ge(s_yg, n - 1)
                for a in range(4):
                    last = pe.matmul(banks[6 + n % 2][32 * a:32 * a + 32, 0:P],
                                     xn[:, t, P * g + 32 * a:P * g + 32 * a + 32], mix[:, n % 2, a, :],
                                     start=True, stop=True)
                last.then_inc(s_y, 1)

            for n, (t, g) in enumerate(units):
                tile = slice(t * P, (t + 1) * P)
                if n >= 2:
                    pe.wait_ge(s_diff, 4 * (n - 1))
                for a in range(4):
                    last = pe.matmul(banks[n % 2][:, P * a:P * a + P], sel3[part_rows, 4 * g + a, :], cum3[part_rows, tile],
                                     start=True, stop=True)
                last.then_inc(s_r, 1)
                if n >= 2:
                    products(n - 2)
                for a in range(4):
                    r = slice(NS * (a % 2), NS * (a % 2) + NS)
                    last = pe.matmul(banks[2 + 2 * (n % 2) + a % 2][:, P * (a // 2):P * (a // 2) + P],
                                     bT[r, 2 * g + a // 2, tile],
                                     cT[r, 2 * g + a // 2, tile], start=True, stop=True)
                last.then_inc(s_r, 1)
            products(len(units) - 2)
            products(len(units) - 1)
            pe.wait_ge(s_yg, len(units))
            for t in range(NT):
                if t >= 2:
                    pe.wait_ge(s_out, t - 1)
                for g in range(KD):
                    last = pe.matmul(banks[6 + t % 2][:], yg[:, g, t * P:(t + 1) * P], wO[:, g, :],
                                     start=(g == 0), stop=(g == KD - 1))
                last.then_inc(s_o, 1)

        @block.scalar
        def _(act):
            norm.on_scalar(nc, act)
            act.wait_ge(s_sel, 3)
            nc.scalar.copy(sel3[:], sel).then_inc(s_sel3, 1)
            act.wait_ge(s_b, 16 * 7)
            for n, (w, dst, pr, c) in enumerate(projections):
                act.wait_ge(s_p, n + 1)
                nc.scalar.activation(dst[:, pr, 512 * c:512 * c + 512], banks[n % 2][:], ACT.Silu,
                                     bias=(bB, bC)[w][:, pr:pr + 1]).then_inc(s_pf, 1)
            for t in range(NT):
                act.wait_ge(s_xb, t + 1)
                nc.scalar.activation(xn[:, t, :], xb[:, t % 2, :], ACT.Silu).then_inc(s_xn, 1)
            for n in range(len(units)):
                act.wait_ge(s_diff, 4 * (n + 1))
                if n >= 2:
                    act.wait_ge(s_mask, n - 1)
                nc.scalar.activation(dec[:, n % 2], diff[:, n % 2], ACT.Exp).then_inc(s_dec, 1)

        @block.vector
        def _(dve):
            norm.on_vector(dve)
            dve.wait_ge(s_b, 16 * 7)
            dve.wait_ge(s_a, 1)
            dve.wait_ge(s_zero, 6)
            for n in range(3):
                dve.tensor_tensor(la3[:, :, 32 * n:32 * n + H], banks[2][:, 0:NT * H].rearrange("p (t h) -> p t h", t=NT),
                                  bA[:].unsqueeze(1).broadcast_to([P, NT, H]), ALU.add).then_inc(s_la, 1)
            dve.wait_ge(s_c, 2)
            dve.tensor_copy(cum[:], banks[3][:, 0:NT * H].rearrange("p (t h) -> p t h", t=NT)).then_inc(s_cum, 1)
            for n in range(2):
                c, sums = slice(512 * n, 512 * n + 512), banks[4 + n][part_rows, :]
                mid, low_ = slice(32, 32 + H), slice(64, 64 + H)
                dve.tensor_copy(cum3[part_rows, c], sums).then_inc(s_cumT, 1)
                dve.wait_ge(s_cumT, 5 * n + 1)
                dve.tensor_tensor(rest[part_rows, c], sums, cum3[part_rows, c], ALU.subtract).then_inc(s_cumT, 1)
                dve.wait_ge(s_cumT, 5 * n + 2)
                dve.tensor_copy(middle[part_rows, c], rest[part_rows, c]).then_inc(s_cumT, 1)
                dve.tensor_copy(cum3[mid, c], rest[mid, c]).then_inc(s_cumT, 1)
                dve.wait_ge(s_cumT, 5 * n + 3)
                dve.tensor_tensor(cum3[low_, c], rest[low_, c], middle[low_, c], ALU.subtract).then_inc(s_cumT, 1)
            for t in range(NT):
                dve.wait_ge(s_x, t + 1)
                if t >= 2:
                    dve.wait_ge(s_xn, t - 1)
                dve.tensor_tensor(xb[:, t % 2, :], banks[6 + t % 2][:], bX[:], ALU.add).then_inc(s_xb, 1)
            for n in range(2 * KD):
                dve.wait_ge(s_g, n + 1)
                dve.tensor_scalar(gT[:, n // 2, 512 * (n % 2):512 * (n % 2) + 512], banks[n % 2][:],
                                  bG[:, n // 2:n // 2 + 1], None, ALU.add).then_inc(s_gT, 1)
            for t in range(NT):
                dve.tensor_tensor(x[:, t, :], x[:, t, :], bO[:], ALU.add).then_inc(s_xo, 1)

            def gated(n):
                t, g = units[n]
                dve.wait_ge(s_y, n + 1)
                dve.tensor_tensor(yg[:, g, t * P:(t + 1) * P], banks[6 + n % 2][:, 0:P],
                                  gT[:, g, t * P:(t + 1) * P], ALU.mult).then_inc(s_yg, 1)

            def mixed(n):
                dve.wait_ge(s_mask, n + 1)
                dve.wait_ge(s_r, 2 * (n + 1))
                if n >= 2:
                    dve.wait_ge(s_y, n - 1)
                for r in range(2):
                    last = dve.tensor_tensor(mix[:, n % 2, r::2, :], diff[:, n % 2, r::2, :],
                                             banks[2 + 2 * (n % 2) + r][:, 0:2 * P].rearrange("p (a i) -> p a i", a=2),
                                             ALU.mult)
                last.then_inc(s_mix, 1)

            for n, (t, g) in enumerate(units):
                dve.wait_ge(s_r, 2 * n + 1)
                if n >= 2:
                    dve.wait_ge(s_mix, n - 1)
                for a in range(4):
                    h = 4 * g + a
                    dve.scalar_tensor_tensor(diff[:, n % 2, a, :], banks[n % 2][:, P * a:P * a + P],
                                             cum[:, t, h:h + 1], tri[:], ALU.subtract, ALU.mult).then_inc(s_diff, 1)
                if n >= 1:
                    mixed(n - 1)
                if n >= 3:
                    gated(n - 3)
            mixed(len(units) - 1)
            for n in range(len(units) - 3, len(units)):
                gated(n)
            for t in range(NT):
                dve.wait_ge(s_xo, NT)
                dve.wait_ge(s_o, t + 1)
                dve.tensor_tensor(x[:, t, :], x[:, t, :], banks[6 + t % 2][:], ALU.add).then_inc(s_out, 1)
                k.tile_stats(dve, x, t, (s_out, t + 1))



class Split:

    WIDTH = 2048

    def __init__(self, k, ctx, name, pieces):
        self.nc, self.pieces = k.nc, pieces
        self.stage = k.sb(ctx, name + "_stage", [P, 2, self.WIDTH])
        self.s_in = [k.sem(ctx, f"{name}_in{n}") for n in range(2)]
        self.s_hi = k.sem(ctx, name + "_hi_done")
        self.s_lo = k.sem(ctx, name + "_lo_done")

    def view(self, n):
        a, b = self.pieces[n][0].shape[1:]
        return self.stage[:, n % 2, 0:a * b].rearrange("p (a b) -> p a b", a=a)

    def on_sync(self, sp):
        for n, (src, _, _) in enumerate(self.pieces):
            if n >= 2:
                sp.wait_ge(self.s_lo, n - 1)
            sp.dma_start(self.view(n), src).then_inc(self.s_in[n % 2], 16)

    def high_on_scalar(self, act, which):
        for n in which:
            act.wait_ge(self.s_in[n % 2], 16 * (n // 2 + 1))
            self.nc.scalar.copy(self.pieces[n][1], self.view(n)).then_inc(self.s_hi, 1)

    def low_on_gpsimd(self, pool):
        for n, (_, hi, lo) in enumerate(self.pieces):
            pool.wait_ge(self.s_hi, n + 1)
            pool.tensor_tensor(lo, self.view(n), hi, ALU.subtract).then_inc(self.s_lo, 1)


TERMS = ((0, 0), (1, 0), (0, 1))



NB, BW = 16, 128
TOPK = NB // 4


def block_ffn(k, ident, x):
    nc, d = k.nc, k.d
    F = NB * BW
    with ExitStack() as ctx:
        h = k.sb(ctx, "f_h", [P, 2, NB, TOK], BF16)
        early = h[:, 0].rearrange("p a n -> p (a n)").bitcast(F32)
        xhat = early[:, 0:NT * D].rearrange("p (t n) -> p t n", t=NT)
        xT = early[:, NT * D:2 * NT * D].rearrange("p (j n) -> p j n", j=KD)
        xs = k.sb(ctx, "f_x_split", [P, 2, KD, TOK], BF16)
        w1 = k.sb(ctx, "f_w1", [P, 2, KD, F], BF16)
        w2 = k.sb(ctx, "f_w2", [P, 2, NB, D], BF16)
        rw = k.sb(ctx, "f_router", [P, KD, NB])
        rb = k.sb(ctx, "f_router_b", [P, NB])
        b1 = k.sb(ctx, "f_b1", [P, NB])
        b2 = k.sb(ctx, "f_b2", [P, D])
        logit = k.sb(ctx, "f_logit", [P, NT, NB])
        stat = k.sb(ctx, "f_stat", [P, 3, NT])
        prob = k.sb(ctx, "f_prob", [P, NT, NB])
        beats = k.sb(ctx, "f_beats", [P, 2, NB, NB])
        lower = k.sb(ctx, "f_lower", [P, NB, NB])
        rank = k.sb(ctx, "f_rank", [P, NT, NB])
        mask = k.sb(ctx, "f_mask", [P, NT, NB])
        maskT = k.sb(ctx, "f_maskT", [NB, TOK], BF16)
        sel = k.sb(ctx, "f_sel", [NB, NB, P], BF16)
        act_out = k.sb(ctx, "f_relu", [P, 2, 512])
        masked = k.sb(ctx, "f_masked", [P, 2, 512])
        banks = [k.ps(ctx, f"f_bank{n}", [P, 512]) for n in range(8)]
        pieces = [(d["L0_ffn_w1"].rearrange("(j p) n -> p j n", p=P)[:, j:j + 1, :], w1[:, 0, j:j + 1, :],
                   w1[:, 1, j:j + 1, :]) for j in range(KD)]
        pieces += [(d["L0_ffn_w2"].rearrange("(j p) n -> p j n", p=P)[:, j:j + 4, :], w2[:, 0, j:j + 4, :],
                    w2[:, 1, j:j + 4, :]) for j in range(0, NB, 4)]
        split = Split(k, ctx, "f_split", pieces)
        s_in = k.sem(ctx, "f_in")
        s_set = k.sem(ctx, "f_set")
        s_sel = k.sem(ctx, "f_sel_done")
        s_r = k.sem(ctx, "f_router_full")
        s_v = k.sem(ctx, "f_route_step")
        s_e = k.sem(ctx, "f_exp_done")
        s_mt = k.sem(ctx, "f_maskT_full")
        s_mtc = k.sem(ctx, "f_maskT_done")
        s_h = k.sem(ctx, "f_h_full")
        s_relu = k.sem(ctx, "f_relu_done")
        s_masked = k.sem(ctx, "f_masked_done")
        s_hhi = k.sem(ctx, "f_h_hi_done")
        s_hlo = k.sem(ctx, "f_h_lo_done")
        s_y = k.sem(ctx, "f_y_full")
        s_xo = k.sem(ctx, "f_x_bias")
        s_out = k.sem(ctx, "f_out")
        norm = Norm(k, ctx, "f", x, ident, banks[0:2], xT, xhat=xhat, split=(xs[:, 0], xs[:, 1]))
        block = ctx.enter_context(nc.Block())
        groups = [(blk, c) for blk in range(NB) for c in range(2)]

        @block.sync
        def _(sp):
            sp.dma_start(rw[:], d["L0_ffn_router_w"].rearrange("(j p) n -> p j n", p=P)).then_inc(s_in, 16)
            sp.dma_start(rb[:], d["L0_ffn_router_b"].partition_broadcast(P)).then_inc(s_in, 16)
            sp.dma_start(b1[:], d["L0_ffn_b1"]).then_inc(s_in, 16)
            sp.dma_start(b2[:], d["L0_ffn_b2"].partition_broadcast(P)).then_inc(s_in, 16)
            split.on_sync(sp)
            sp.wait_ge(s_in, 64)

        @block.gpsimd
        def _(pool):
            pool.memset(sel[:], 0.0).then_inc(s_set, 1)
            pool.memset(lower[:], 1.0).then_inc(s_set, 1)
            pool.wait_ge(s_set, 2)
            pool.affine_select(out=sel[:], in_=sel[:], compare_op=ALU.not_equal, fill=1.0, base=0,
                               pattern=[[-1, NB], [0, P]], channel_multiplier=1).then_inc(s_sel, 1)
            pool.affine_select(out=lower[:], in_=lower[:], compare_op=ALU.is_ge, fill=0.0, base=-1,
                               pattern=[[1, NB], [-1, NB]], channel_multiplier=0).then_inc(s_sel, 1)
            split.low_on_gpsimd(pool)
            for n, (blk, c) in enumerate(groups):
                pool.wait_ge(s_hhi, n + 1)
                pool.tensor_tensor(h[:, 1, blk, 512 * c:512 * c + 512], masked[:, n % 2, :],
                                   h[:, 0, blk, 512 * c:512 * c + 512], ALU.subtract).then_inc(s_hlo, 1)

        @block.tensor
        def _(pe):
            norm.on_tensor(pe)
            pe.wait_ge(s_in, 64)
            for t in range(NT):
                pe.wait_ge(norm.s_xT, t + 1)
                for j in range(KD):
                    last = pe.matmul(banks[2][:, NB * t:NB * t + NB], xT[:, j, t * P:(t + 1) * P], rw[:, j, :],
                                     start=(j == 0), stop=(j == KD - 1))
            last.then_inc(s_r, 1)

            def hidden(n):
                blk, c = groups[n]
                if n >= 3:
                    pe.wait_ge(s_relu, n - 2)
                for i, (hw, hx) in enumerate(TERMS):
                    for j in range(KD):
                        last = pe.matmul(banks[3 + n % 3][:], w1[:, hw, j, blk * BW:(blk + 1) * BW],
                                         xs[:, hx, j, 512 * c:512 * c + 512],
                                         start=(i == 0 and j == 0), stop=(i == 2 and j == KD - 1))
                last.then_inc(s_h, 1)

            def masks(n):
                blk, c = groups[n]
                if n >= 2:
                    pe.wait_ge(s_masked, n - 1)
                pe.matmul(banks[6 + n % 2][:], sel[:, blk, :], maskT[:, 512 * c:512 * c + 512],
                          start=True, stop=True).then_inc(s_mt, 1)

            pe.wait_ge(split.s_lo, KD)
            pe.wait_ge(norm.s_low, NT)
            for n in range(3):
                hidden(n)
            pe.wait_ge(s_v, 6 + 6 * NT)
            for t in range(NT):
                last = pe.transpose(banks[t // 4][0:NB, P * (t % 4):P * (t % 4) + P], mask[:, t, :], ident[:])
            last.then_inc(s_mt, 1)
            pe.wait_ge(s_sel, 2)
            pe.wait_ge(s_mtc, 2)
            for n in range(3):
                if n < 2:
                    masks(n)
            for n in range(3, len(groups)):
                masks(n - 1)
                hidden(n)
            masks(len(groups) - 1)
            pe.wait_ge(split.s_lo, KD + 4)
            pe.wait_ge(s_hlo, len(groups))
            for t in range(NT):
                if t >= 2:
                    pe.wait_ge(s_out, t - 1)
                for i, (hh, hw) in enumerate(TERMS):
                    for j in range(NB):
                        last = pe.matmul(banks[t % 2][:], h[:, hh, j, t * P:(t + 1) * P], w2[:, hw, j, :],
                                         start=(i == 0 and j == 0), stop=(i == 2 and j == NB - 1))
                last.then_inc(s_y, 1)

        @block.scalar
        def _(act):
            def high(n):
                blk, c = groups[n]
                act.wait_ge(s_masked, n + 1)
                nc.scalar.copy(h[:, 0, blk, 512 * c:512 * c + 512], masked[:, n % 2, :]).then_inc(s_hhi, 1)

            norm.on_scalar(nc, act)
            split.high_on_scalar(act, range(0, 2))
            act.wait_ge(s_v, 3)
            nc.scalar.activation(prob[:], logit[:], ACT.Exp).then_inc(s_e, 1)
            split.high_on_scalar(act, range(2, KD + 4))
            act.wait_ge(s_in, 64)
            for n, (blk, c) in enumerate(groups):
                act.wait_ge(s_h, n + 1)
                if n >= 2:
                    act.wait_ge(s_masked, n - 1)
                nc.scalar.activation(act_out[:, n % 2, :], banks[3 + n % 3][:], ACT.Relu,
                                     bias=b1[:, blk:blk + 1]).then_inc(s_relu, 1)
                if n >= 1:
                    high(n - 1)
            high(len(groups) - 1)

        @block.vector
        def _(dve):
            norm.on_vector(dve)
            norm.low_on_vector(dve)
            dve.wait_ge(s_in, 64)
            dve.wait_ge(s_r, 1)
            dve.tensor_tensor(logit[:], banks[2][:, 0:NT * NB].rearrange("p (t n) -> p t n", t=NT),
                              rb[:].unsqueeze(1).broadcast_to([P, NT, NB]), ALU.add).then_inc(s_v, 1)
            dve.wait_ge(s_v, 1)
            dve.tensor_reduce(stat[:, 0, :], logit[:], AX, ALU.max).then_inc(s_v, 1)
            dve.wait_ge(s_v, 2)
            dve.tensor_tensor(logit[:], logit[:], stat[:, 0, :].unsqueeze(2).broadcast_to([P, NT, NB]),
                              ALU.subtract).then_inc(s_v, 1)
            dve.wait_ge(s_e, 1)
            dve.tensor_reduce(stat[:, 1, :], prob[:], AX, ALU.add).then_inc(s_v, 1)
            dve.wait_ge(s_v, 4)
            dve.reciprocal(stat[:, 2, :], stat[:, 1, :]).then_inc(s_v, 1)
            dve.wait_ge(s_v, 5)
            dve.tensor_tensor(prob[:], prob[:], stat[:, 2, :].unsqueeze(2).broadcast_to([P, NT, NB]),
                              ALU.mult).then_inc(s_v, 1)
            dve.wait_ge(s_v, 6)
            dve.wait_ge(s_sel, 2)
            for t in range(NT):
                pj = prob[:, t, :].unsqueeze(1).broadcast_to([P, NB, NB])
                pi = prob[:, t, :].unsqueeze(2).broadcast_to([P, NB, NB])
                if t:
                    dve.wait_ge(s_v, 6 + 6 * t)
                dve.tensor_tensor(beats[:, 0], pj, pi, ALU.is_gt).then_inc(s_v, 1)
                dve.tensor_tensor(beats[:, 1], pj, pi, ALU.is_equal).then_inc(s_v, 1)
                dve.wait_ge(s_v, 6 + 6 * t + 2)
                dve.tensor_tensor(beats[:, 1], beats[:, 1], lower[:], ALU.mult).then_inc(s_v, 1)
                dve.wait_ge(s_v, 6 + 6 * t + 3)
                dve.tensor_tensor(beats[:, 0], beats[:, 0], beats[:, 1], ALU.add).then_inc(s_v, 1)
                dve.wait_ge(s_v, 6 + 6 * t + 4)
                dve.tensor_reduce(rank[:, t, :], beats[:, 0], AX, ALU.add).then_inc(s_v, 1)
                dve.wait_ge(s_v, 6 + 6 * t + 5)
                dve.tensor_scalar(mask[:, t, :], rank[:, t, :], float(TOPK), None, ALU.is_lt).then_inc(s_v, 1)
            dve.wait_ge(s_mt, 1)
            for n in range(2):
                dve.tensor_copy(maskT[:, 512 * n:512 * n + 512], banks[n][0:NB, :]).then_inc(s_mtc, 1)
            for t in range(NT):
                dve.tensor_tensor(x[:, t, :], x[:, t, :], b2[:], ALU.add).then_inc(s_xo, 1)
            for n, (blk, c) in enumerate(groups):
                dve.wait_ge(s_relu, n + 1)
                dve.wait_ge(s_mt, n + 2)
                if n >= 2:
                    dve.wait_ge(s_hlo, n - 1)
                dve.tensor_tensor(masked[:, n % 2, :], act_out[:, n % 2, :], banks[6 + n % 2][:],
                                  ALU.mult).then_inc(s_masked, 1)
            dve.wait_ge(s_xo, NT)
            for t in range(NT):
                dve.wait_ge(s_y, t + 1)
                dve.tensor_tensor(x[:, t, :], x[:, t, :], banks[t % 2][:], ALU.add).then_inc(s_out, 1)
                k.tile_stats(dve, x, t, (s_out, t + 1))



def cross1(k, ident, x):
    nc, d = k.nc, k.d
    with ExitStack() as ctx:
        qk = k.sb(ctx, "y_qk", [P, NT, KC, P])
        cq = k.sb(ctx, "y_cq", [P, NT])
        cT = k.sb(ctx, "y_ctxT", [P, 2, 2, KC, NK])
        cT_in = [k.sem(ctx, f"y_ctxT_in{n}") for n in range(2)]
        cross1_queries(k, ident, x, qk, cq, cT, cT_in)
        cross1_batches(k, ident, x, qk, cq, cT, cT_in)


def cross1_queries(k, ident, x, qk, cq, cT, cT_in):
    nc, d = k.nc, k.d
    with ExitStack() as ctx:
        xT = k.sb(ctx, "yq_xT", [P, KD, TOK])
        qT = k.sb(ctx, "yq_qT", [P, KD, TOK])
        wq = k.sb(ctx, "yq_wq", [P, KD, D])
        wkT = k.sb(ctx, "yq_wkT", [P, KD, CD])
        bq = k.sb(ctx, "yq_bq", [P, KD])
        bk = k.sb(ctx, "yq_bk", [P, KD])
        bv = k.sb(ctx, "yq_bv", [P, D])
        banks = [k.ps(ctx, f"yq_bank{n}", [P, 512]) for n in range(8)]
        wide = [banks[n] for n in (2, 3, 5)]
        s_in = k.sem(ctx, "yq_in")
        s_q = k.sem(ctx, "yq_q_full")
        s_qT = k.sem(ctx, "yq_qT_done")
        s_k = k.sem(ctx, "yq_qk_full")
        s_qk = k.sem(ctx, "yq_qk_done")
        s_c = k.sem(ctx, "yq_cq_full")
        s_x = k.sem(ctx, "yq_x_done")
        norm = Norm(k, ctx, "yq", x, ident, banks[0:2], xT)
        dq = Dequant(k, ctx, 1, banks[6:8], ident)
        block = ctx.enter_context(nc.Block())
        groups = [(m, c) for c in range(2) for m in range(KD)]
        kgroups = [(m, c) for c in range(2) for m in range(KC)]

        @block.sync
        def _(sp):
            sp.dma_start(wq[:], d["L1_xattn_Wq"].rearrange("(j p) n -> p j n", p=P)).then_inc(s_in, 16)
            sp.dma_start(wkT[:], d["L1_xattn_WkT"].rearrange("(j p) n -> p j n", p=P)).then_inc(s_in, 16)
            sp.dma_start(bq[:], d["L1_xattn_bq"]).then_inc(s_in, 16)
            sp.dma_start(bk[:], d["L1_xattn_bk"]).then_inc(s_in, 16)
            sp.dma_start(bv[:], d["L1_xattn_bv"].partition_broadcast(P)).then_inc(s_in, 16)
            dq.load(sp)
            ctxT = d["ctxT"].rearrange("b (j p) n -> p b j n", p=P)
            for u in range(2):
                for s in range(2):
                    sp.dma_start(cT[:, u, s], ctxT[:, 2 * u + s]).then_inc(cT_in[u], 16)
            sp.wait_ge(s_in, 80)
            dq.store(sp)

        @block.gpsimd
        def _(pool):
            dq.multiply(pool)

        @block.tensor
        def _(pe):
            norm.on_tensor(pe)
            pe.wait_ge(s_in, 80)
            pe.wait_ge(norm.s_xT, NT)
            for n, (m, c) in enumerate(groups):
                if n >= 3:
                    pe.wait_ge(s_qT, n - 2)
                for j in range(KD):
                    last = pe.matmul(wide[n % 3][:], wq[:, j, m * P:(m + 1) * P],
                                     xT[:, j, 512 * c:512 * c + 512], start=(j == 0), stop=(j == KD - 1))
                last.then_inc(s_q, 1)
            pe.wait_ge(s_qT, 2 * KD)
            for n, (m, c) in enumerate(kgroups):
                if n >= 2:
                    pe.wait_ge(s_qk, n - 1)
                for j in range(KD):
                    last = pe.matmul(banks[n % 2][:], wkT[:, j, m * P:(m + 1) * P],
                                     qT[:, j, 512 * c:512 * c + 512], start=(j == 0), stop=(j == KD - 1))
                last.then_inc(s_k, 1)
                if n >= 2:
                    dq.turn(pe, range(MF // 2 * (n - 2), MF // 2 * (n - 1)))
            for t in range(NT):
                for j in range(KD):
                    last = pe.matmul(banks[4][:, t:t + 1], qT[:, j, t * P:(t + 1) * P], bk[:, j:j + 1],
                                     start=(j == 0), stop=(j == KD - 1))
            last.then_inc(s_c, 1)

        @block.scalar
        def _(act):
            norm.on_scalar(nc, act)
            dq.high(act, range(MF))

        @block.vector
        def _(dve):
            norm.on_vector(dve)
            dve.wait_ge(s_in, 80)
            for t in range(NT):
                dve.tensor_tensor(x[:, t, :], x[:, t, :], bv[:], ALU.add).then_inc(s_x, 1)
            dq.scales(dve)
            for n, (m, c) in enumerate(groups):
                dve.wait_ge(s_q, n + 1)
                dve.tensor_scalar(qT[:, m, 512 * c:512 * c + 512], wide[n % 3][:], bq[:, m:m + 1], None,
                                  ALU.add).then_inc(s_qT, 1)
                if n == 1:
                    dq.divide(dve)
                elif n == 3:
                    dq.round(dve)
                elif n == 4:
                    dq.unshift(dve)
            for n, (m, c) in enumerate(kgroups):
                dve.wait_ge(s_k, n + 1)
                dve.tensor_copy(qk[:, 4 * c:4 * c + 4, m, :],
                                banks[n % 2][:].rearrange("p (t q) -> p t q", q=P)).then_inc(s_qk, 1)
                if n >= 2:
                    dq.low(dve, range(MF // 2 * (n - 2), MF // 2 * (n - 1)))
            dve.wait_ge(s_c, 1)
            dve.tensor_copy(cq[:], banks[4][:, 0:NT]).then_inc(s_x, 1)


def cross1_batches(k, ident, x, qk, cq, cT, cT_in):
    nc, d = k.nc, k.d
    NKT = len(KTILES)
    FULL = NK // P
    with ExitStack() as ctx:
        cn = k.sb(ctx, "y_ctx", [P, 2, 2, NKT, CD])
        qs = k.sb(ctx, "y_qs", [P, 2, KC, P])
        cqs = k.sb(ctx, "y_cqs", [P, 2])
        prob = k.sb(ctx, "y_prob", [P, 2, NK])
        pT = k.sb(ctx, "y_pT", [P, NTG, 512])
        o = k.sb(ctx, "y_o", [P, CD])
        oT = k.sb(ctx, "y_oT", [P, KC * P])
        wv = k.sb(ctx, "y_wv", [P, KC, D])
        stat = k.sb(ctx, "y_stat", [P, 2, 4])
        rinv = k.sb(ctx, "y_rinv", [P, 1])
        score = k.ps(ctx, "y_score", [P, 2048])
        tb = [k.ps(ctx, f"y_turn{n}", [P, 512]) for n in range(2)]
        pv = k.ps(ctx, "y_pv", [P, 512])
        wb = k.ps(ctx, "y_wout", [P, 512])
        s_w = k.sem(ctx, "y_w_in")
        cn_in = [k.sem(ctx, f"y_ctx_in{n}") for n in range(2)]
        qs_in = [k.sem(ctx, f"y_qs_in{n}") for n in range(2)]
        cqs_in = [k.sem(ctx, f"y_cqs_in{n}") for n in range(2)]
        s_s = k.sem(ctx, "y_scores_done")
        s_m = k.sem(ctx, "y_stat_step")
        s_e = k.sem(ctx, "y_exp_done")
        s_t = k.sem(ctx, "y_turn_full")
        s_tf = k.sem(ctx, "y_turn_free")
        s_pv = k.sem(ctx, "y_pv_full")
        s_inv = k.sem(ctx, "y_inv_done")
        s_o = k.sem(ctx, "y_o_done")
        s_wo = k.sem(ctx, "y_wout_full")
        s_x = k.sem(ctx, "y_x_done")
        block = ctx.enter_context(nc.Block())
        ctxT = d["ctxT"].rearrange("b (j p) n -> p b j n", p=P)
        ctxN = d["ctx"].rearrange("b n c -> n b c")

        @block.sync
        def _(sp):
            def load(u, par, ready):
                one = isinstance(u, int)
                if ready is not None:
                    sp.wait_ge(s_s, ready)
                if one:
                    sp.dma_start(qs[:, par], qk[:, u]).then_inc(qs_in[par], 16)
                else:
                    sp.dma_start(qs[:, par], qk[:, bass.ds(u, 1)].rearrange("p a j q -> p (a j) q")).then_inc(qs_in[par], 16)
                for s in () if one else range(2):
                    src = ctxT[:, bass.ds(2 * u + s, 1)].rearrange("p a j n -> p (a j) n")
                    sp.dma_start(cT[:, par, s], src).then_inc(cT_in[par], 16)
                if ready is not None:
                    sp.wait_ge(s_pv, ready)
                sp.dma_start(cqs[:, par:par + 1], cq[:, u:u + 1] if one else cq[:, bass.ds(u, 1)]).then_inc(cqs_in[par], 16)
                for s in range(2):
                    src = ctxN[:, 2 * u + s] if one else \
                        ctxN[:, bass.ds(2 * u + s, 1)].rearrange("n a c -> n (a c)")
                    sp.dma_start(cn[:, par, s, 0:FULL, :],
                                 src[0:FULL * P, :].rearrange("(t p) c -> p t c", p=P)).then_inc(cn_in[par], 16)
                    sp.dma_start(cn[0:NK - FULL * P, par, s, FULL, :], src[FULL * P:NK, :]).then_inc(cn_in[par], 16)

            sp.dma_start(wv[:], d["L1_xattn_Wv"].rearrange("(j p) n -> p j n", p=P)).then_inc(s_w, 16)
            load(0, 0, None)
            load(1, 1, None)
            with sp.Fori(0, (NT - 2) // 2) as i:
                for a in range(2):
                    load(2 * i + 2 + a, a, 2 * i + 1 + a)
            sp.wait_ge(s_w, 16)

        def each_tile(eng, do):
            do(0, 0, True, False)
            do(1, 1, True, True)
            with eng.Fori(0, (NT - 2) // 2) as i:
                for a in range(2):
                    do(2 * i + 2 + a, a, True, True)
            do(NT, NT % 2, False, True)

        @block.tensor
        def _(pe):
            def tile(u, par, scores, products):
                if scores:
                    n_in = 32 * (u // 2 + 1) if isinstance(u, int) else 16 * (u + (1 if par else 2))
                    n_q = 16 * (u // 2 + 1) if isinstance(u, int) else 8 * (u + (1 if par else 2))
                    pe.wait_ge(qs_in[par], n_q)
                    pe.wait_ge(cT_in[par], n_in)
                    if products:
                        pe.wait_ge(s_e, u)
                    for c, (n0, w) in enumerate(CHUNKS):
                        for s in range(2):
                            for j in range(KC):
                                last = pe.matmul(score[L * s:L * s + L, 512 * c:512 * c + w],
                                                 qs[:, par, j, L * s:L * s + L], cT[:, par, s, j, n0:n0 + w],
                                                 start=(j == 0), stop=(j == KC - 1))
                    last.then_inc(s_s, 1)
                if products:
                    other = 1 - par
                    n_in = 64 * ((u - 1) // 2 + 1) if isinstance(u, int) else 32 * (u + (1 if par else 0))
                    pe.wait_ge(s_e, u)
                    pe.wait_ge(cn_in[other], n_in)
                    pe.wait_ge(s_w, 16)

                    def turn(j):
                        t = (other + j) % 2
                        if j >= 2 or not (isinstance(u, int) and u == 1):
                            pe.wait_ge(s_tf, 5 * (u - 1) + j - 1)
                        for i, (k0, kw) in enumerate(TGROUPS[j]):
                            last = pe.transpose(tb[t][0:kw, P * i:P * i + P], prob[:, other, k0:k0 + kw], ident[:])
                        last.then_inc(s_t, 1)

                    def product(j):
                        pe.wait_ge(s_tf, 5 * (u - 1) + j + 1)
                        for i, (k0, kw) in enumerate(TGROUPS[j]):
                            for s in range(2):
                                last = pe.matmul(pv[L * s:L * s + L, 0:CD], pT[0:kw, j, P * i + L * s:P * i + L * s + L],
                                                 cn[0:kw, other, s, 4 * j + i, :],
                                                 start=(j == 0 and i == 0), stop=(j == NTG - 1))
                        return last

                    turn(0)
                    turn(1)
                    if not (isinstance(u, int) and u == 1):
                        pe.wait_ge(s_o, u - 1)
                    product(0)
                    turn(2)
                    product(1)
                    turn(3)
                    product(2)
                    product(3).then_inc(s_pv, 1)
                    pe.wait_ge(s_o, u)
                    pe.wait_ge(s_tf, 5 * (u - 1) + 3)
                    for j in range(KC):
                        last = pe.transpose(tb[other][:, P * j:P * j + P], o[:, P * j:P * j + P], ident[:])
                    last.then_inc(s_t, 1)
                    pe.wait_ge(s_tf, 5 * u)
                    if not (isinstance(u, int) and u == 1):
                        pe.wait_ge(s_x, u - 1)
                    for j in range(KC):
                        last = pe.matmul(wb[:], oT[:, P * j:P * j + P], wv[:, j, :], start=(j == 0), stop=(j == KC - 1))
                    last.then_inc(s_wo, 1)

            each_tile(pe, tile)

        @block.scalar
        def _(act):
            def tile(u, par, scores, products):
                if scores:
                    act.wait_ge(s_m, 3 * u + 3)
                    nc.scalar.activation(prob[:, par, :], score[:, 0:NK], ACT.Exp, bias=stat[:, par, 2:3],
                                         accum_out=stat[:, par, 3:4]).then_inc(s_e, 1)
                if products:
                    other = 1 - par
                    for j in range(NTG):
                        t = (other + j) % 2
                        n, kw = P * len(TGROUPS[j]), TGROUPS[j][0][1]
                        act.wait_ge(s_t, 5 * (u - 1) + j + 1)
                        nc.scalar.copy(pT[0:kw, j, 0:n], tb[t][0:kw, 0:n]).then_inc(s_tf, 1)
                    act.wait_ge(s_t, 5 * u)
                    nc.scalar.copy(oT[:], tb[other][:, 0:KC * P]).then_inc(s_tf, 1)

            each_tile(act, tile)

        @block.vector
        def _(dve):
            def tile(u, par, scores, products):
                if scores:
                    dve.wait_ge(s_s, u + 1)
                    dve.tensor_reduce(stat[:, par, 0:1], score[:, 0:NK], AX, ALU.max).then_inc(s_m, 1)
                    dve.wait_ge(s_m, 3 * u + 1)
                    n_q = 16 * (u // 2 + 1) if isinstance(u, int) else 8 * (u + (1 if par else 2))
                    dve.wait_ge(cqs_in[par], n_q)
                    dve.tensor_tensor(stat[:, par, 1:2], stat[:, par, 0:1], cqs[:, par:par + 1],
                                      ALU.add).then_inc(s_m, 1)
                    dve.wait_ge(s_m, 3 * u + 2)
                    dve.tensor_tensor(stat[:, par, 2:3], cqs[:, par:par + 1], stat[:, par, 1:2],
                                      ALU.subtract).then_inc(s_m, 1)
                if products:
                    other = 1 - par
                    dve.wait_ge(s_e, u)
                    dve.reciprocal(rinv[:], stat[:, other, 3:4]).then_inc(s_inv, 1)
                    dve.wait_ge(s_inv, u)
                    dve.wait_ge(s_pv, u)
                    dve.tensor_scalar(o[:], pv[:, 0:CD], rinv[:], None, ALU.mult).then_inc(s_o, 1)
                    dve.wait_ge(s_wo, u)
                    if isinstance(u, int):
                        xt = x[:, u - 1, :]
                    else:
                        xt = x[:, bass.ds(u - 1, 1), :].rearrange("p a n -> p (a n)")
                    dve.tensor_tensor(xt, xt, wb[:], ALU.add).then_inc(s_x, 1)
                    k.tile_stats(dve, x, u - 1, (s_x, u))

            each_tile(dve, tile)



DQ = 64


def self1(k, ident, low, x):
    nc, d = k.nc, k.d
    with ExitStack() as ctx:
        xT = k.sb(ctx, "s_xT", [P, KD, TOK])
        wq = k.sb(ctx, "s_wq", [P, 2, KD, DQ])
        wv = k.sb(ctx, "s_wv", [P, KD, D])
        qkT = k.sb(ctx, "s_qkT", [DQ, 2, TOK])
        v = k.sb(ctx, "s_v", [P, NT, D])
        sc = k.sb(ctx, "s_sc", [P, NT, P])
        prob = k.sb(ctx, "s_prob", [P, NT, P])
        pT = k.sb(ctx, "s_pT", [P, NT, P])
        stat = k.sb(ctx, "s_stat", [P, 4, NT])
        banks = [k.ps(ctx, f"s_bank{n}", [P, 512]) for n in range(8)]
        s_in = k.sem(ctx, "s_in")
        s_q = k.sem(ctx, "s_q_full")
        s_qc = k.sem(ctx, "s_q_done")
        s_v = k.sem(ctx, "s_v_full")
        s_vc = k.sem(ctx, "s_v_done")
        s_s = k.sem(ctx, "s_scores_full")
        s_sc = k.sem(ctx, "s_scores_done")
        s_m = k.sem(ctx, "s_max_done")
        s_b = k.sem(ctx, "s_shift_done")
        s_e = k.sem(ctx, "s_exp_done")
        s_t = k.sem(ctx, "s_turned")
        s_tc = k.sem(ctx, "s_turned_done")
        s_r = k.sem(ctx, "s_inv_done")
        s_o = k.sem(ctx, "s_o_full")
        s_x = k.sem(ctx, "s_x_done")
        norm = Norm(k, ctx, "sn", x, ident, banks[0:2], xT)
        dq = Dequant(k, ctx, 2, banks[0:2], ident)
        block = ctx.enter_context(nc.Block())

        @block.sync
        def _(sp):
            for n, w in enumerate(("L1_attn_Wq", "L1_attn_Wk")):
                sp.dma_start(wq[:, n], d[w].rearrange("(j p) n -> p j n", p=P)).then_inc(s_in, 16)
            sp.dma_start(wv[:], d["L1_attn_Wv"].rearrange("(j p) n -> p j n", p=P)).then_inc(s_in, 16)
            dq.load(sp)
            sp.wait_ge(s_in, 48)
            dq.store(sp)

        @block.gpsimd
        def _(pool):
            dq.multiply(pool)

        @block.tensor
        def _(pe):
            norm.on_tensor(pe)
            pe.wait_ge(s_in, 48)
            pe.wait_ge(norm.s_xT, NT)
            for n in range(4):
                for j in range(KD):
                    last = pe.matmul(banks[2 + n][0:DQ, :], wq[:, n // 2, j, :],
                                     xT[:, j, 512 * (n % 2):512 * (n % 2) + 512], start=(j == 0), stop=(j == KD - 1))
                last.then_inc(s_q, 1)

            def values(t):
                if t >= 2:
                    pe.wait_ge(s_vc, t - 1)
                for j in range(KD):
                    last = pe.matmul(banks[t % 2][:], xT[:, j, t * P:(t + 1) * P], wv[:, j, :],
                                     start=(j == 0), stop=(j == KD - 1))
                last.then_inc(s_v, 1)

            for t in range(2):
                values(t)
            pe.wait_ge(s_qc, 4)
            for t in range(NT):
                tile = slice(t * P, (t + 1) * P)
                last = pe.matmul(banks[6 + t // 4][:, P * (t % 4):P * (t % 4) + P], qkT[:, 0, tile], qkT[:, 1, tile],
                                 start=True, stop=True)
            last.then_inc(s_s, 1)
            for t in range(2, NT):
                values(t)
            pe.wait_ge(s_vc, NT)
            dq.turn(pe, range(MF))
            pe.wait_ge(s_sc, NT)
            for t in range(NT):
                pe.wait_ge(s_e, t + 1)
                last = pe.transpose(banks[6 + t // 4][:, P * (t % 4):P * (t % 4) + P], prob[:, t, :], ident[:])
                if t % 4 == 3:
                    last.then_inc(s_t, 1)
            for t in range(NT):
                pe.wait_ge(s_tc, t // 4 + 1)
                if t >= 4:
                    pe.wait_ge(s_x, t - 3)
                pe.matmul(banks[2 + t % 4][:], pT[:, t, :], v[:, t, :], start=True, stop=True).then_inc(s_o, 1)

        @block.scalar
        def _(act):
            norm.on_scalar(nc, act)
            for t in range(NT):
                act.wait_ge(s_v, t + 1)
                nc.scalar.copy(v[:, t, :], banks[t % 2][:]).then_inc(s_vc, 1)
            act.wait_ge(s_b, 1)
            for t in range(NT):
                nc.scalar.activation(prob[:, t, :], sc[:, t, :], ACT.Exp, bias=stat[:, 1, t:t + 1],
                                     scale=float(DQ) ** -0.5, accum_out=stat[:, 2, t:t + 1]).then_inc(s_e, 1)
            dq.high(act, range(MF))

        @block.vector
        def _(dve):
            norm.on_vector(dve)
            dq.scales(dve)
            dq.divide(dve)
            for n in range(4):
                dve.wait_ge(s_q, n + 1)
                dve.tensor_copy(qkT[:, n // 2, 512 * (n % 2):512 * (n % 2) + 512], banks[2 + n][0:DQ, :]).then_inc(s_qc, 1)
            dq.round(dve)
            dq.unshift(dve)
            dve.wait_ge(s_s, 1)
            for t in range(NT):
                dve.tensor_tensor(sc[:, t, :], banks[6 + t // 4][:, P * (t % 4):P * (t % 4) + P], low[:],
                                  ALU.add).then_inc(s_sc, 1)
            dve.wait_ge(s_sc, NT)
            dve.tensor_reduce(stat[:, 0, :], sc[:], AX, ALU.max).then_inc(s_m, 1)
            dve.wait_ge(s_m, 1)
            dve.tensor_scalar(stat[:, 1, :], stat[:, 0, :], -float(DQ) ** -0.5, None, ALU.mult).then_inc(s_b, 1)
            dq.low(dve, range(MF))
            for n in range(2):
                dve.wait_ge(s_t, n + 1)
                dve.tensor_copy(pT[:, 4 * n:4 * n + 4, :],
                                banks[6 + n][:].rearrange("p (t q) -> p t q", q=P)).then_inc(s_tc, 1)
            dve.wait_ge(s_e, NT)
            dve.reciprocal(stat[:, 3, :], stat[:, 2, :]).then_inc(s_r, 1)
            dve.wait_ge(s_r, 1)
            for t in range(NT):
                dve.wait_ge(s_o, t + 1)
                dve.scalar_tensor_tensor(x[:, t, :], banks[2 + t % 4][:], stat[:, 3, t:t + 1], x[:, t, :],
                                         ALU.mult, ALU.add).then_inc(s_x, 1)
                k.tile_stats(dve, x, t, (s_x, t + 1))



NF = 1536
MF = NF // P
QB = 32
WCOLS = NF * D // P


class Dequant:

    MATRICES = ("L1_ffn_w_up", "L1_ffn_w_gate", "L1_ffn_w_down")

    def __init__(self, k, ctx, n, banks, ident):
        self.k, self.nc, self.banks, self.ident = k, k.nc, banks, ident
        self.name = self.MATRICES[n]
        self.w = k.sb(ctx, f"w{n}_w", [P, WCOLS])
        self.scale = k.sb(ctx, f"w{n}_scale", [P, 2, WCOLS // QB])
        self.parts = k.sb(ctx, f"w{n}_parts", [P, 2, WCOLS], BF16)
        self.s_in = k.sem(ctx, f"w{n}_in")
        self.s_unit = k.sem(ctx, f"w{n}_units")
        self.s_back = k.sem(ctx, f"w{n}_scaled")
        self.s_turn = k.sem(ctx, f"w{n}_turned")
        self.s_hi = k.sem(ctx, f"w{n}_high")
        self.s_lo = k.sem(ctx, f"w{n}_low")
        self.s_out = k.sem(ctx, f"w{n}_out")
        if n < 2:
            w = self.w[:].rearrange("p (o j c) -> p o j c", o=MF, j=KD)
            self.groups = [([w[:, 4 * og + i, j, :] for i in range(4)],
                            slice(j * NF + 512 * og, j * NF + 512 * og + 512))
                           for j in range(KD) for og in range(MF // 4)]
        else:
            w = self.w[:].rearrange("p (o j c) -> p o j c", o=KD, j=MF)
            self.groups = [([w[:, i, j, :] for i in range(4)], slice(512 * j, 512 * j + 512)) for j in range(MF)]

    def load(self, sp):
        src = self.k.d[self.name].rearrange("(o p) c -> p o c", p=P)
        sp.dma_start(self.w[:].rearrange("p (o c) -> p o c", o=src.shape[1]), src).then_inc(self.s_in, 16)

    def store(self, sp):
        step = 3
        for g in range(0, len(self.groups), step):
            sp.wait_ge(self.s_lo, g + step)
            c = slice(512 * g, 512 * (g + step))
            sp.dma_start(self.k.scratch[self.name][:, :, c], self.parts[:, :, c]).then_inc(self.s_out, 16)
        sp.wait_ge(self.s_out, 16 * (len(self.groups) // step))

    def scales(self, dve):
        s, inv = self.scale[:, 0], self.scale[:, 1]
        dve.wait_ge(self.s_in, 16)
        dve.tensor_reduce(s, self.w[:].rearrange("p (b i) -> p b i", i=QB), AX, ALU.max,
                          apply_absolute_value=True).then_inc(self.s_unit, 1)
        dve.wait_ge(self.s_unit, 1)
        dve.tensor_scalar(s, s, 1.0 / 7.0, 1e-12, ALU.mult, ALU.max).then_inc(self.s_unit, 1)
        dve.wait_ge(self.s_unit, 2)
        dve.reciprocal(inv, s).then_inc(self.s_unit, 1)

    def divide(self, dve):
        w = self.w[:].rearrange("p (b i) -> p b i", i=QB)
        dve.wait_ge(self.s_unit, 3)
        dve.tensor_tensor(w, w, self.scale[:, 1].unsqueeze(2).broadcast_to([P, WCOLS // QB, QB]),
                          ALU.mult).then_inc(self.s_unit, 1)

    def round(self, dve):
        dve.wait_ge(self.s_unit, 4)
        dve.tensor_scalar(self.w[:], self.w[:], ROUND, None, ALU.add).then_inc(self.s_unit, 1)

    def unshift(self, dve):
        dve.wait_ge(self.s_unit, 5)
        dve.tensor_scalar(self.w[:], self.w[:], ROUND, 7.0, ALU.subtract, ALU.min).then_inc(self.s_unit, 1)

    def multiply(self, pool):
        w = self.w[:].rearrange("p (b i) -> p b i", i=QB)
        pool.wait_ge(self.s_unit, 6)
        pool.tensor_tensor(w, w, self.scale[:, 0].unsqueeze(2).broadcast_to([P, WCOLS // QB, QB]),
                           ALU.mult).then_inc(self.s_back, 1)

    def turn(self, pe, which):
        for g in which:
            if g == 0:
                pe.wait_ge(self.s_back, 1)
            if g >= 2:
                pe.wait_ge(self.s_lo, g - 1)
            for a, block in enumerate(self.groups[g][0]):
                last = pe.transpose(self.banks[g % 2][:, P * a:P * a + P], block, self.ident[:])
            last.then_inc(self.s_turn, 1)

    def high(self, act, which):
        for g in which:
            act.wait_ge(self.s_turn, g + 1)
            self.nc.scalar.copy(self.parts[:, 0, self.groups[g][1]], self.banks[g % 2][:]).then_inc(self.s_hi, 1)

    def low(self, dve, which):
        for g in which:
            dst = self.groups[g][1]
            dve.wait_ge(self.s_hi, g + 1)
            dve.tensor_tensor(self.parts[:, 1, dst], self.banks[g % 2][:], self.parts[:, 0, dst],
                              ALU.subtract).then_inc(self.s_lo, 1)


def quant_ffn(k, ident, x):
    nc, d = k.nc, k.d
    with ExitStack() as ctx:
        up = k.sb(ctx, "g_up", [P, MF, TOK])
        gate = k.sb(ctx, "g_gate", [P, MF, TOK])
        early = gate[:].rearrange("p m n -> p (m n)")
        xhat = early[:, 0:NT * D].rearrange("p (t n) -> p t n", t=NT)
        uT = early[:, NT * D:2 * NT * D].rearrange("p (j n) -> p j n", j=KD)
        xs = k.sb(ctx, "g_x_split", [P, 2, KD, TOK], BF16)
        tmp = xs[:, 0].rearrange("p j n -> p (j n)").bitcast(F32).rearrange("p (a n) -> p a n", a=2)
        wug = k.sb(ctx, "g_w", [P, 2, 2, WCOLS], BF16)
        osplit = wug[:].rearrange("p a b n -> p (a b n)").rearrange("p (h m n) -> p h m n", h=2, m=MF)
        wd = k.sb(ctx, "g_wd", [P, 2, MF, D], BF16)
        amax = k.sb(ctx, "g_amax", [P, 5, 2 * MF])
        peak = k.sb(ctx, "g_peak", [P, 5, 2])
        unit = k.sb(ctx, "g_unit", [P, 5, 3])
        big = k.sb(ctx, "g_round", [P, 1])
        unbig = k.sb(ctx, "g_unround", [P, 1])
        banks = [k.ps(ctx, f"g_bank{n}", [P, 512]) for n in range(8)]
        s_w = [k.sem(ctx, f"g_w_in{n}") for n in range(3)]
        s_big = k.sem(ctx, "g_round_set")
        s_unbig = k.sem(ctx, "g_unround_set")
        s_whole = k.sem(ctx, "g_silu_whole")
        s_hp = k.sem(ctx, "g_hidden_out_gpsimd")
        s_peak = k.sem(ctx, "g_peak")
        s_all = k.sem(ctx, "g_peak_all")
        s_unit = k.sem(ctx, "g_unit")
        s_xh = k.sem(ctx, "g_x_high")
        s_xl = k.sem(ctx, "g_x_low")
        s_ug = k.sem(ctx, "g_hidden_full")
        s_ugc = k.sem(ctx, "g_hidden_done")
        s_am = k.sem(ctx, "g_hidden_absmax")
        s_u1 = k.sem(ctx, "g_up_rounded")
        s_u2 = k.sem(ctx, "g_up_done")
        s_g1 = k.sem(ctx, "g_gate_rounded")
        s_g2 = k.sem(ctx, "g_gate_done")
        s_sg = k.sem(ctx, "g_sigmoid")
        s_sr = k.sem(ctx, "g_sigmoid_rounded")
        s_s2 = k.sem(ctx, "g_sigmoid_done")
        s_gs = k.sem(ctx, "g_product")
        s_am2 = k.sem(ctx, "g_product_absmax")
        s_h1 = k.sem(ctx, "g_silu_rounded")
        s_h2 = k.sem(ctx, "g_hidden_out")
        s_am3 = k.sem(ctx, "g_out_absmax")
        s_o1 = k.sem(ctx, "g_out_rounded")
        s_oh = k.sem(ctx, "g_out_high")
        s_ol = k.sem(ctx, "g_out_low")
        s_y = k.sem(ctx, "g_y_full")
        s_x = k.sem(ctx, "g_x_done")
        s_st = k.sem(ctx, "g_stored")
        norm = Norm(k, ctx, "g", x, ident, banks[0:2], None, xhat=xhat)
        block = ctx.enter_context(nc.Block())
        groups = [(w, m, c) for w in range(2) for m in range(MF) for c in range(2)]
        half = len(groups) // 2
        by_vector = [m for m in range(MF) if m % 3 == 0]
        by_gpsimd = [m for m in range(MF) if m % 3]
        NB_G = 6

        @block.sync
        def _(sp):
            for n in range(2):
                sp.dma_start(wug[:, n], k.scratch[Dequant.MATRICES[n]]).then_inc(s_w[n], 16)
            sp.dma_start(wd[:].rearrange("p h m n -> p h (m n)"), k.scratch[Dequant.MATRICES[2]]).then_inc(s_w[2], 16)
            out = k.out.rearrange("(t p) n -> p t n", p=P)
            for t in range(NT):
                sp.wait_ge(s_x, t + 1)
                sp.dma_start(out[:, t, :], x[:, t, :]).then_inc(s_st, 16)
            sp.wait_ge(s_st, 16 * NT)

        @block.gpsimd
        def _(pool):
            pool.memset(big[:], ROUND).then_inc(s_big, 1)
            pool.memset(unbig[:], -ROUND).then_inc(s_unbig, 1)

            def spread(n):
                pool.wait_ge(s_peak, n + 1)
                pool.partition_all_reduce(peak[:, n, 1:2], peak[:, n, 0:1], P,
                                          bass.bass_isa.ReduceOp.max).then_inc(s_all, 1)

            for n in range(3):
                spread(n)
            for m in range(MF):
                pool.wait_ge(s_s2, m + 1)
                pool.tensor_tensor(gate[:, m, :], tmp[:, m % 2, :], gate[:, m, :], ALU.mult).then_inc(s_gs, 1)
            spread(3)
            for n, m in enumerate(by_gpsimd):
                pool.wait_ge(s_whole, n + 1)
                pool.tensor_tensor(gate[:, m, :], gate[:, m, :], up[:, m, :], ALU.mult).then_inc(s_hp, 1)
            spread(4)

        @block.tensor
        def _(pe):
            norm.on_tensor(pe)
            pe.wait_ge(s_xl, NT)
            for n, (w, m, c) in enumerate(groups):
                if m == 0 and c == 0:
                    pe.wait_ge(s_w[w], 16)
                if n >= NB_G:
                    pe.wait_ge(s_am, n - NB_G + 1)
                wt = wug[:, w].rearrange("p h (j n) -> p h j n", j=KD)
                for i, (hw, hx) in enumerate(TERMS):
                    for j in range(KD):
                        last = pe.matmul(banks[2 + n % NB_G][:], wt[:, hw, j, m * P:(m + 1) * P],
                                         xs[:, hx, j, 512 * c:512 * c + 512],
                                         start=(i == 0 and j == 0), stop=(i == 2 and j == KD - 1))
                last.then_inc(s_ug, 1)
            pe.wait_ge(s_w[2], 16)
            pe.wait_ge(s_am, len(groups))
            for m in range(MF):
                pe.wait_ge(s_ol, m + 1)
                for t in range(NT):
                    for i, (hh, hw) in enumerate(TERMS):
                        last = pe.matmul(banks[t][:], osplit[:, hh, m, t * P:(t + 1) * P], wd[:, hw, m, :],
                                         start=(m == 0 and i == 0), stop=(m == MF - 1 and i == 2))
                    if m == MF - 1:
                        last.then_inc(s_y, 1)

        @block.scalar
        def _(act):
            act.wait_ge(norm.s_var, 1)
            nc.scalar.activation(norm.small[:, 1, :], norm.small[:, 0, :], ACT.Sqrt).then_inc(norm.s_root, 1)
            act.wait_ge(s_big, 1)
            act.wait_ge(s_unit, 2)
            for t in range(NT):
                act.wait_ge(norm.s_turned, t + 1)
                nc.scalar.activation(uT[:, :, t * P:(t + 1) * P], banks[t % 2][:].rearrange("p (j n) -> p j n", j=KD),
                                     ACT.Identity, bias=big[:], scale=unit[:, 0, 1:2]).then_inc(norm.s_xT, 1)

            def hidden(n):
                w, m, c = groups[n]
                act.wait_ge(s_ug, n + 1)
                nc.scalar.mul((up, gate)[w][:, m, 512 * c:512 * c + 512], banks[2 + n % NB_G][:],
                              unit[:, 0, 0:1]).then_inc(s_ugc, 1)

            def rounded(dst, src, n, done):
                nc.scalar.activation(dst, src, ACT.Identity, bias=big[:], scale=unit[:, n, 1:2]).then_inc(done, 1)

            for n in range(half):
                hidden(n)
            for n in range(half, len(groups)):
                hidden(n)
                m = (n - half) // 2
                if n % 2:
                    if m == 0:
                        act.wait_ge(s_unit, 4)
                    rounded(up[:, m, :], up[:, m, :], 1, s_u1)
            act.wait_ge(s_unit, 6)
            for m in range(MF + 2):
                if m < MF:
                    rounded(gate[:, m, :], gate[:, m, :], 2, s_g1)
                if m >= 1 and m - 1 < MF:
                    act.wait_ge(s_g2, m)
                    if m >= 3:
                        act.wait_ge(s_gs, m - 2)
                    nc.scalar.activation(tmp[:, (m - 1) % 2, :], gate[:, m - 1, :], ACT.Sigmoid).then_inc(s_sg, 1)
            act.wait_ge(s_unit, 8)
            act.wait_ge(s_unbig, 1)
            for m in range(MF + 1):
                if m < MF:
                    rounded(gate[:, m, :], gate[:, m, :], 3, s_h1)
                if m - 1 in by_gpsimd:
                    act.wait_ge(s_h1, m)
                    nc.scalar.activation(gate[:, m - 1, :], gate[:, m - 1, :], ACT.Identity, bias=unbig[:],
                                         scale=1.0).then_inc(s_whole, 1)
            act.wait_ge(s_unit, 11)
            for m in range(MF):
                rounded(gate[:, m, :], gate[:, m, :], 4, s_o1)

        @block.vector
        def _(dve):
            def scale_of(n, a, count, factor):
                dve.tensor_reduce(peak[:, n, 0:1], a, AX, ALU.max).then_inc(s_peak, 1)
                dve.wait_ge(s_all, n + 1)
                dve.tensor_scalar(unit[:, n, 0:1], peak[:, n, 1:2], factor / QMAX, 1e-12, ALU.mult, ALU.max).then_inc(s_unit, 1)
                dve.wait_ge(s_unit, count)
                dve.reciprocal(unit[:, n, 1:2], unit[:, n, 0:1]).then_inc(s_unit, 1)

            norm.on_vector(dve)
            dve.wait_ge(norm.s_hat, NT)
            dve.tensor_reduce(amax[:, 0, 0:NT], xhat, AX, ALU.max, apply_absolute_value=True).then_inc(s_am2, 1)
            dve.wait_ge(s_am2, 1)
            scale_of(0, amax[:, 0, 0:NT], 1, 1.0)
            for t in range(NT):
                c = slice(t * P, (t + 1) * P)
                dve.wait_ge(norm.s_xT, t + 1)
                dve.tensor_scalar(xs[:, 0, :, c], uT[:, :, c], ROUND, None, ALU.subtract).then_inc(s_xh, 1)
                dve.wait_ge(s_xh, t + 1)
                dve.scalar_tensor_tensor(xs[:, 1, :, c], uT[:, :, c], ROUND, xs[:, 0, :, c], ALU.subtract,
                                         ALU.subtract).then_inc(s_xl, 1)

            def absmax(n):
                w, m, c = groups[n]
                dve.wait_ge(s_ugc, n + 1)
                dve.tensor_reduce(amax[:, 1 + w, 2 * m + c:2 * m + c + 1], (up, gate)[w][:, m, 512 * c:512 * c + 512],
                                  AX, ALU.max, apply_absolute_value=True).then_inc(s_am, 1)

            for n in range(half):
                absmax(n)
            dve.wait_ge(s_am, half)
            scale_of(1, amax[:, 1, :], 3, 1.0)
            for n in range(half, len(groups)):
                absmax(n)
                m = (n - half) // 2
                if n % 2:
                    dve.wait_ge(s_u1, m + 1)
                    dve.tensor_scalar(up[:, m, :], up[:, m, :], ROUND, unit[:, 1, 0:1], ALU.subtract,
                                      ALU.mult).then_inc(s_u2, 1)
            dve.wait_ge(s_am, len(groups))
            scale_of(2, amax[:, 2, :], 5, 1.0)
            for m in range(MF + 3):
                if m < MF:
                    dve.wait_ge(s_g1, m + 1)
                    dve.tensor_scalar(gate[:, m, :], gate[:, m, :], ROUND, unit[:, 2, 0:1], ALU.subtract,
                                      ALU.mult).then_inc(s_g2, 1)
                if 1 <= m <= MF:
                    i = m - 1
                    dve.wait_ge(s_sg, i + 1)
                    dve.tensor_scalar(tmp[:, i % 2, :], tmp[:, i % 2, :], 65536.0, ROUND, ALU.mult,
                                      ALU.add).then_inc(s_sr, 1)
                    dve.wait_ge(s_sr, i + 1)
                    dve.tensor_scalar(tmp[:, i % 2, :], tmp[:, i % 2, :], ROUND, 65535.0, ALU.subtract,
                                      ALU.min).then_inc(s_s2, 1)
                if m >= 3:
                    i = m - 3
                    dve.wait_ge(s_gs, i + 1)
                    dve.tensor_reduce(amax[:, 3, i:i + 1], gate[:, i, :], AX, ALU.max,
                                      apply_absolute_value=True).then_inc(s_am2, 1)
            dve.wait_ge(s_am2, 1 + MF)
            dve.tensor_reduce(peak[:, 3, 0:1], amax[:, 3, 0:MF], AX, ALU.max).then_inc(s_peak, 1)
            dve.wait_ge(s_all, 4)
            dve.tensor_scalar(unit[:, 3, 0:1], peak[:, 3, 1:2], 2.0 ** -16 / QMAX, 1e-12, ALU.mult,
                              ALU.max).then_inc(s_big, 1)
            dve.wait_ge(s_big, 2)
            dve.reciprocal(unit[:, 3, 2:3], unit[:, 3, 0:1]).then_inc(s_unit, 1)
            dve.wait_ge(s_unit, 7)
            dve.tensor_scalar(unit[:, 3, 1:2], unit[:, 3, 2:3], 2.0 ** -16, None, ALU.mult).then_inc(s_unit, 1)
            for m in range(MF + 3):
                if m in by_vector:
                    dve.wait_ge(s_h1, m + 1)
                    dve.scalar_tensor_tensor(gate[:, m, :], gate[:, m, :], ROUND, up[:, m, :], ALU.subtract,
                                             ALU.mult).then_inc(s_h2, 1)
                    dve.wait_ge(s_h2, by_vector.index(m) + 1)
                    dve.tensor_reduce(amax[:, 4, m:m + 1], gate[:, m, :], AX, ALU.max,
                                      apply_absolute_value=True).then_inc(s_am3, 1)
                if m - 3 in by_gpsimd:
                    dve.wait_ge(s_hp, by_gpsimd.index(m - 3) + 1)
                    dve.tensor_reduce(amax[:, 4, m - 3:m - 2], gate[:, m - 3, :], AX, ALU.max,
                                      apply_absolute_value=True).then_inc(s_am3, 1)
            dve.wait_ge(s_am3, MF)
            dve.tensor_reduce(peak[:, 4, 0:1], amax[:, 4, 0:MF], AX, ALU.max).then_inc(s_peak, 1)
            dve.wait_ge(s_all, 5)
            dve.tensor_scalar(unit[:, 4, 2:3], peak[:, 4, 1:2], unit[:, 3, 0:1], 1.0 / QMAX, ALU.mult,
                              ALU.mult).then_inc(s_unit, 1)
            dve.wait_ge(s_unit, 9)
            dve.tensor_scalar(unit[:, 4, 0:1], unit[:, 4, 2:3], 1e-12, None, ALU.max).then_inc(s_unit, 1)
            dve.wait_ge(s_unit, 10)
            dve.reciprocal(unit[:, 4, 2:3], unit[:, 4, 0:1]).then_inc(s_big, 1)
            dve.wait_ge(s_big, 3)
            dve.tensor_tensor(unit[:, 4, 1:2], unit[:, 4, 2:3], unit[:, 3, 0:1], ALU.mult).then_inc(s_unit, 1)
            for m in range(MF):
                dve.wait_ge(s_o1, m + 1)
                dve.tensor_scalar(osplit[:, 0, m, :], gate[:, m, :], ROUND, None, ALU.subtract).then_inc(s_oh, 1)
                dve.wait_ge(s_oh, m + 1)
                dve.scalar_tensor_tensor(osplit[:, 1, m, :], gate[:, m, :], ROUND, osplit[:, 0, m, :],
                                         ALU.subtract, ALU.subtract).then_inc(s_ol, 1)
            for t in range(NT):
                dve.wait_ge(s_y, t + 1)
                dve.scalar_tensor_tensor(x[:, t, :], banks[t][:], unit[:, 4, 0:1], x[:, t, :], ALU.mult,
                                         ALU.add).then_inc(s_x, 1)


def cross0(k, ident, x):
    d = k.d
    with ExitStack() as c0:
        catT = k.sb(c0, "catT", [P, 2, 2, TOK])
        bvT = k.sb(c0, "bvT", [P, 4])
        qT = k.sb(c0, "qT", [P, B, 2, KD, L], BF16)
        wk = k.sb(c0, "wk_split", [P, 2, KC, D], BF16)
        wv = k.sb(c0, "wv_split", [P, 2, KC, D], BF16)
        bk = k.sb(c0, "bk", [P, KD])
        load_small(k, [(bvT, d["L0_xattn_bv"])])
        cross0_queries(k, ident, qT, wk, wv, bk)
        cross0_batches(k, ident, qT, wk, wv, bk, catT, bvT)
        cross0_output(k, ident, x, catT)


def build(nc, d, out):
    k = Kit(nc, d, out)
    with ExitStack() as ctx:
        ident = k.sb(ctx, "ident", [P, P])
        tri = k.sb(ctx, "tri", [P, P])
        low = k.sb(ctx, "low", [P, P])
        constants(k, ident, tri, low)
        x = k.sb(ctx, "x", [P, NT, D])
        k.stats = k.sb(ctx, "x_stats", [P, NT, 6])
        cross0(k, ident, x)
        state_space(k, ident, tri, x)
        block_ffn(k, ident, x)
        k.clear_semaphores()
        cross1(k, ident, x)
        self1(k, ident, low, x)
        quant_ffn(k, ident, x)


def load_small(k, pairs):
    nc = k.nc
    with ExitStack() as ctx:
        s = k.sem(ctx, "small_in")
        block = ctx.enter_context(nc.Block())

        @block.sync
        def _(sp):
            for dst, src in pairs:
                sp.dma_start(dst[:], src).then_inc(s, 16)
            sp.wait_ge(s, 16 * len(pairs))


def columns(a):
    return np.ascontiguousarray(a.reshape(-1, P).T)


def lay_out(i):
    f = np.ascontiguousarray
    pairs = lambda a: a.reshape((2, 4, 2, DH) + a.shape[1:])
    ctx = i["ctx_512"]
    return {
        "x": f(i["x"].reshape(TOK, D)),
        "ctxT": f(ctx.transpose(0, 2, 1)),
        "L0_xattn_Wq": f(i["L0_xattn_Wq"]), "L0_xattn_Wk": f(i["L0_xattn_Wk"]), "L0_xattn_Wv": f(i["L0_xattn_Wv"]),
        "L0_xattn_bq": columns(i["L0_xattn_bq"]), "L0_xattn_bk": columns(i["L0_xattn_bk"]),
        "L0_xattn_bv": f(pairs(i["L0_xattn_bv"]).transpose(1, 3, 0, 2).reshape(P, 4)),
        "L0_xattn_Wo": f(pairs(i["L0_xattn_Wo"]).transpose(0, 2, 1, 3, 4).reshape(4, P, D)),
        "L0_xattn_bo": f(i["L0_xattn_bo"].reshape(1, D)),
        "L0_attn_WX": f(i["L0_attn_W_XBC"][:, 0:DH].transpose(2, 0, 1)),
        "L0_attn_WB": f(i["L0_attn_W_XBC"][:, DH:DH + NS].transpose(2, 0, 1)),
        "L0_attn_WC": f(i["L0_attn_W_XBC"][:, DH + NS:].transpose(2, 0, 1)),
        "L0_attn_WG": f(i["L0_attn_W_gate"].transpose(2, 0, 1)),
        "L0_attn_WA": f(i["L0_attn_W_logA"][:, 0].T),
        "L0_attn_bX": f(i["L0_attn_b_XBC"][:, 0:DH].reshape(1, D)),
        "L0_attn_bB": columns(i["L0_attn_b_XBC"][:, DH:DH + NS]),
        "L0_attn_bC": columns(i["L0_attn_b_XBC"][:, DH + NS:]),
        "L0_attn_bG": columns(i["L0_attn_b_gate"]),
        "L0_attn_bA": f(i["L0_attn_b_logA"].reshape(1, H)),
        "L0_attn_W_out": f(i["L0_attn_W_out"].T),
        "L0_attn_bO": f(i["L0_attn_b_out"].reshape(1, D)),
        "ctx": f(ctx),
        "L1_ffn_w_up": f(i["L1_ffn_w_up"]), "L1_ffn_w_gate": f(i["L1_ffn_w_gate"]), "L1_ffn_w_down": f(i["L1_ffn_w_down"]),
        "L1_xattn_Wq": f(i["L1_xattn_Wq"]), "L1_xattn_WkT": f(i["L1_xattn_Wk"].T), "L1_xattn_Wv": f(i["L1_xattn_Wv"]),
        "L1_xattn_bq": columns(i["L1_xattn_bq"]), "L1_xattn_bk": columns(i["L1_xattn_bk"]),
        "L1_xattn_bv": f(i["L1_xattn_bv"].reshape(1, D)),
        "L1_attn_Wq": f(i["L1_attn_Wq"]), "L1_attn_Wk": f(i["L1_attn_Wk"]), "L1_attn_Wv": f(i["L1_attn_Wv"]),
        "L0_ffn_router_w": f(i["L0_ffn_router_w"].T), "L0_ffn_router_b": f(i["L0_ffn_router_b"].reshape(1, NB)),
        "L0_ffn_w1": f(i["L0_ffn_w1"].T), "L0_ffn_b1": columns(i["L0_ffn_b1"]),
        "L0_ffn_w2": f(i["L0_ffn_w2"].T), "L0_ffn_b2": f(i["L0_ffn_b2"].reshape(1, D)),
    }


def kernel(**inputs):
    import concourse.bacc as _bacc
    from concourse.bass_utils import run_bass_kernel_spmd as _run

    nc = _bacc.Bacc("TRN2", target_bir_lowering=False, num_devices=1)
    arrays = lay_out({n: np.asarray(a) for n, a in inputs.items()})
    d = {n: nc.dram_tensor(f"in_{n}", a.shape, mybir.dt.from_np(a.dtype), kind="ExternalInput").ap()
         for n, a in arrays.items()}
    out = nc.dram_tensor("out", (TOK, D), F32, kind="ExternalOutput").ap()
    build(nc, d, out)
    r = _run(nc, [{f"in_{n}": a for n, a in arrays.items()}], core_ids=[0])
    return r.results[0]["out"].reshape(B, L, D)
```
